# Optimizing a Trainium2 kernel written in Bass

```python
import numpy as np
import jax
import jax.numpy as jnp

def _softmax(x, axis=-1):
    return jax.nn.softmax(x, axis=axis)

def _gelu(x):
    return jax.nn.gelu(x, approximate=True)

def _silu(x):
    return jax.nn.silu(x)

def _sigmoid(x):
    return jax.nn.sigmoid(x)

def _layernorm(x, axis=-1, eps=1e-05):
    m = jnp.mean(x, axis=axis, keepdims=True)
    v = jnp.var(x, axis=axis, keepdims=True)
    return (x - m) / jnp.sqrt(v + eps)

def _scatter_add(tgt, idx, src, axis=0):
    return tgt.at[idx].add(src)

def _segment_sum(src, seg, n):
    return jax.ops.segment_sum(src, seg, n)
kernel_name = 'mk_seq_postln_d1_jaxref_r8_356ec3'

def setup_inputs(seed: int=0):
    np.random.seed(seed)
    _w = jnp.asarray

    def _L0_attn_setup():
        import jax, jax.numpy as jnp
        import numpy as np
        B, T, D_IN, D = (16, 256, 128, 128)
        LN_EPS = 1e-05

        def _lru_forward(x, W_in, b_in, params_log, W_mid, b_mid, w1_w, w1_b, w2_w, w2_b, ln_g, ln_b):
            u = jnp.einsum('btd,edh->ebth', x, W_in) + b_in[:, None, None, :]
            in_r, in_i, o = (u[0], u[1], u[2])
            p = jnp.exp(params_log)
            nu, theta, gamma = (p[0], p[1], p[2])
            lam = jnp.exp(jax.lax.complex(-nu, theta))
            uc = jax.lax.complex(gamma * in_r, gamma * in_i)
            f = jnp.broadcast_to(lam, uc.shape)

            def combine(a, b):
                fa, ua = a
                fb, ub = b
                return (fa * fb, fb * ua + ub)
            _, h = jax.lax.associative_scan(combine, (f, uc), axis=1)
            hidden = jnp.concatenate([h[:, -1, :].real, h[:, -1, :].imag], axis=-1)[None]
            hri = jnp.stack([h.real, h.imag])
            out2 = jnp.einsum('ebtd,edh->ebth', hri, W_mid) + b_mid[:, None, None, :]
            out = out2[0] - out2[1] + o
            y = jax.nn.gelu(out @ w1_w + w1_b, approximate=False)
            y = y @ w2_w + w2_b + out
            mean = jnp.mean(y, axis=-1, keepdims=True)
            var = jnp.var(y, axis=-1, keepdims=True)
            y = (y - mean) * jax.lax.rsqrt(var + LN_EPS) * ln_g + ln_b
            return (y, hidden)

        def _reference_tuple_inner(x, W_in, b_in, params_log, W_mid, b_mid, w1_w, w1_b, w2_w, w2_b, ln_g, ln_b):
            return _lru_forward(x, W_in, b_in, params_log, W_mid, b_mid, w1_w, w1_b, w2_w, w2_b, ln_g, ln_b)
        key = jax.random.key(seed)
        ks = jax.random.split(key, 13)
        s_in = 1.0 / np.sqrt(D_IN)
        s_d = 1.0 / np.sqrt(D)
        x = jax.random.normal(ks[0], (B, T, D_IN), jnp.float32)
        W_in = jax.random.uniform(ks[1], (3, D_IN, D), jnp.float32, -s_in, s_in)
        b_in = jax.random.uniform(ks[2], (3, D), jnp.float32, -s_in, s_in)
        r_min, r_max = (0.9, 0.999)
        u1 = jax.random.uniform(ks[3], (D,), jnp.float32)
        u2 = jax.random.uniform(ks[4], (D,), jnp.float32)
        nu_log = jnp.log(-0.5 * jnp.log(u1 * (r_max ** 2 - r_min ** 2) + r_min ** 2))
        theta_log = jnp.log(u2 * 2.0 * np.pi)
        lam_abs = jnp.exp(-jnp.exp(nu_log))
        gamma_log = jnp.log(jnp.sqrt(1.0 - lam_abs ** 2))
        params_log = jnp.stack([nu_log, theta_log, gamma_log])
        W_mid = jax.random.uniform(ks[5], (2, D, D), jnp.float32, -s_d, s_d)
        b_mid = jax.random.uniform(ks[6], (2, D), jnp.float32, -s_d, s_d)
        w1_w = jax.random.uniform(ks[7], (D, D), jnp.float32, -s_d, s_d)
        w1_b = jax.random.uniform(ks[8], (D,), jnp.float32, -s_d, s_d)
        w2_w = jax.random.uniform(ks[9], (D, D), jnp.float32, -s_d, s_d)
        w2_b = jax.random.uniform(ks[10], (D,), jnp.float32, -s_d, s_d)
        ln_g = jnp.ones((D,), jnp.float32)
        ln_b = jnp.zeros((D,), jnp.float32)
        return {'x': x, 'W_in': W_in, 'b_in': b_in, 'params_log': params_log, 'W_mid': W_mid, 'b_mid': b_mid, 'w1_w': w1_w, 'w1_b': w1_b, 'w2_w': w2_w, 'w2_b': w2_b, 'ln_g': ln_g, 'ln_b': ln_b}
    _L0_attn_in = _L0_attn_setup()

    def _L0_ffn_setup():
        import jax, jax.numpy as jnp
        import numpy as np
        EPS = 1e-05
        NUM_HEADS = 16
        NUM_KV_HEADS = 4
        NUM_EXPERTS = 8
        TOP_K = 2

        def _layernorm(x, w, b):
            mu = jnp.mean(x, axis=-1, keepdims=True)
            var = jnp.mean((x - mu) ** 2, axis=-1, keepdims=True)
            return (x - mu) * jax.lax.rsqrt(var + EPS) * w + b
        key = jax.random.key(seed)
        ks = jax.random.split(key, 8)
        S, B, H = (128, 4, 128)
        F = 256
        hd = H // NUM_HEADS
        qkv_out = (NUM_HEADS + 2 * NUM_KV_HEADS) * hd
        w_scale = 0.02
        return {'hidden_states': jax.random.normal(ks[0], (S, B, H), jnp.float32), 'ln1_weight': jnp.ones((H,), jnp.float32), 'ln1_bias': jnp.zeros((H,), jnp.float32), 'ln2_weight': jnp.ones((H,), jnp.float32), 'ln2_bias': jnp.zeros((H,), jnp.float32), 'qkv_weight': jax.random.normal(ks[1], (qkv_out, H), jnp.float32) * w_scale, 'proj_weight': jax.random.normal(ks[2], (H, H), jnp.float32) * w_scale, 'router_weight': jax.random.normal(ks[3], (NUM_EXPERTS, H), jnp.float32) * w_scale, 'moe_w1': jax.random.normal(ks[4], (NUM_EXPERTS, H, F), jnp.float32) * w_scale, 'moe_w2': jax.random.normal(ks[5], (NUM_EXPERTS, F, H), jnp.float32) * w_scale}
    _L0_ffn_in = _L0_ffn_setup()
    _d = {'L0_attn_x': _L0_attn_in['x'], 'L0_attn_W_in': _L0_attn_in['W_in'], 'L0_attn_b_in': _L0_attn_in['b_in'], 'L0_attn_params_log': _L0_attn_in['params_log'], 'L0_attn_W_mid': _L0_attn_in['W_mid'], 'L0_attn_b_mid': _L0_attn_in['b_mid'], 'L0_attn_w1_w': _L0_attn_in['w1_w'], 'L0_attn_w1_b': _L0_attn_in['w1_b'], 'L0_attn_w2_w': _L0_attn_in['w2_w'], 'L0_attn_w2_b': _L0_attn_in['w2_b'], 'L0_attn_ln_g': _L0_attn_in['ln_g'], 'L0_attn_ln_b': _L0_attn_in['ln_b'], 'L0_ffn_ln1_weight': _L0_ffn_in['ln1_weight'], 'L0_ffn_ln1_bias': _L0_ffn_in['ln1_bias'], 'L0_ffn_ln2_weight': _L0_ffn_in['ln2_weight'], 'L0_ffn_ln2_bias': _L0_ffn_in['ln2_bias'], 'L0_ffn_qkv_weight': _L0_ffn_in['qkv_weight'], 'L0_ffn_proj_weight': _L0_ffn_in['proj_weight'], 'L0_ffn_router_weight': _L0_ffn_in['router_weight'], 'L0_ffn_moe_w1': _L0_ffn_in['moe_w1'], 'L0_ffn_moe_w2': _L0_ffn_in['moe_w2']}
    _x0 = _d['L0_attn_x']
    _d['L0_attn_x'] = jax.random.normal(jax.random.fold_in(jax.random.key(seed), 1), (8, 1024, 128), dtype=_x0.dtype)
    del _x0
    return _d

def reference(L0_attn_x, L0_attn_W_in, L0_attn_b_in, L0_attn_params_log, L0_attn_W_mid, L0_attn_b_mid, L0_attn_w1_w, L0_attn_w1_b, L0_attn_w2_w, L0_attn_w2_b, L0_attn_ln_g, L0_attn_ln_b, L0_ffn_ln1_weight, L0_ffn_ln1_bias, L0_ffn_ln2_weight, L0_ffn_ln2_bias, L0_ffn_qkv_weight, L0_ffn_proj_weight, L0_ffn_router_weight, L0_ffn_moe_w1, L0_ffn_moe_w2):

    def _L0_attn_ref(x, W_in, b_in, params_log, W_mid, b_mid, w1_w, w1_b, w2_w, w2_b, ln_g, ln_b):
        import jax, jax.numpy as jnp
        import numpy as np
        B, T, D_IN, D = (16, 256, 128, 128)
        LN_EPS = 1e-05

        def _lru_forward(x, W_in, b_in, params_log, W_mid, b_mid, w1_w, w1_b, w2_w, w2_b, ln_g, ln_b):
            u = jnp.einsum('btd,edh->ebth', x, W_in) + b_in[:, None, None, :]
            in_r, in_i, o = (u[0], u[1], u[2])
            p = jnp.exp(params_log)
            nu, theta, gamma = (p[0], p[1], p[2])
            lam = jnp.exp(jax.lax.complex(-nu, theta))
            uc = jax.lax.complex(gamma * in_r, gamma * in_i)
            f = jnp.broadcast_to(lam, uc.shape)

            def combine(a, b):
                fa, ua = a
                fb, ub = b
                return (fa * fb, fb * ua + ub)
            _, h = jax.lax.associative_scan(combine, (f, uc), axis=1)
            hidden = jnp.concatenate([h[:, -1, :].real, h[:, -1, :].imag], axis=-1)[None]
            hri = jnp.stack([h.real, h.imag])
            out2 = jnp.einsum('ebtd,edh->ebth', hri, W_mid) + b_mid[:, None, None, :]
            out = out2[0] - out2[1] + o
            y = jax.nn.gelu(out @ w1_w + w1_b, approximate=False)
            y = y @ w2_w + w2_b + out
            mean = jnp.mean(y, axis=-1, keepdims=True)
            var = jnp.var(y, axis=-1, keepdims=True)
            y = (y - mean) * jax.lax.rsqrt(var + LN_EPS) * ln_g + ln_b
            return (y, hidden)

        def _reference_tuple_inner(x, W_in, b_in, params_log, W_mid, b_mid, w1_w, w1_b, w2_w, w2_b, ln_g, ln_b):
            return _lru_forward(x, W_in, b_in, params_log, W_mid, b_mid, w1_w, w1_b, w2_w, w2_b, ln_g, ln_b)
        return _reference_tuple_inner(x, W_in, b_in, params_log, W_mid, b_mid, w1_w, w1_b, w2_w, w2_b, ln_g, ln_b)[0]

    def _L0_ffn_ref(hidden_states, ln1_weight, ln1_bias, ln2_weight, ln2_bias, qkv_weight, proj_weight, router_weight, moe_w1, moe_w2):
        import jax, jax.numpy as jnp
        import numpy as np
        EPS = 1e-05
        NUM_HEADS = 16
        NUM_KV_HEADS = 4
        NUM_EXPERTS = 8
        TOP_K = 2

        def _layernorm(x, w, b):
            mu = jnp.mean(x, axis=-1, keepdims=True)
            var = jnp.mean((x - mu) ** 2, axis=-1, keepdims=True)
            return (x - mu) * jax.lax.rsqrt(var + EPS) * w + b
        S, B, H = hidden_states.shape
        hd = H // NUM_HEADS
        rep = NUM_HEADS // NUM_KV_HEADS
        scale = 1.0 / hd ** 0.5
        ln1_out = _layernorm(hidden_states, ln1_weight, ln1_bias)
        qkv = jnp.einsum('sbh,oh->sbo', ln1_out, qkv_weight)
        q = qkv[..., :NUM_HEADS * hd].reshape(S, B, NUM_HEADS, hd)
        k = qkv[..., NUM_HEADS * hd:(NUM_HEADS + NUM_KV_HEADS) * hd].reshape(S, B, NUM_KV_HEADS, hd)
        v = qkv[..., (NUM_HEADS + NUM_KV_HEADS) * hd:].reshape(S, B, NUM_KV_HEADS, hd)
        k = jnp.repeat(k, rep, axis=2)
        v = jnp.repeat(v, rep, axis=2)
        scores = jnp.einsum('sbhd,tbhd->bhst', q, k) * scale
        causal = jnp.tril(jnp.ones((S, S), bool))
        scores = jnp.where(causal, scores, jnp.finfo(scores.dtype).min)
        probs = jax.nn.softmax(scores, axis=-1)
        attn = jnp.einsum('bhst,tbhd->sbhd', probs, v).reshape(S, B, H)
        proj_out = jnp.einsum('sbh,oh->sbo', attn, proj_weight)
        hidden_after_attn = hidden_states + proj_out
        ln2_out = _layernorm(hidden_after_attn, ln2_weight, ln2_bias)
        x = ln2_out.reshape(-1, H)
        logits = jnp.einsum('th,eh->te', x, router_weight)
        gate = jax.nn.softmax(logits, axis=-1)
        top_probs, top_idx = jax.lax.top_k(gate, TOP_K)
        h_mid = jax.nn.gelu(jnp.einsum('th,ehf->etf', x, moe_w1))
        expert_out = jnp.einsum('etf,efh->eth', h_mid, moe_w2)
        e_ids = jnp.arange(NUM_EXPERTS)[:, None, None]
        weights = jnp.sum(jnp.where(top_idx[None] == e_ids, top_probs[None], 0.0), axis=-1)
        moe_out = jnp.einsum('eth,et->th', expert_out, weights).reshape(S, B, H)
        return hidden_after_attn + moe_out
    x = L0_attn_x
    x = _layernorm(x + _L0_attn_ref(x, L0_attn_W_in, L0_attn_b_in, L0_attn_params_log, L0_attn_W_mid, L0_attn_b_mid, L0_attn_w1_w, L0_attn_w1_b, L0_attn_w2_w, L0_attn_w2_b, L0_attn_ln_g, L0_attn_ln_b), axis=-1)
    x = _layernorm(x + _L0_ffn_ref(x, L0_ffn_ln1_weight, L0_ffn_ln1_bias, L0_ffn_ln2_weight, L0_ffn_ln2_bias, L0_ffn_qkv_weight, L0_ffn_proj_weight, L0_ffn_router_weight, L0_ffn_moe_w1, L0_ffn_moe_w2), axis=-1)
    return x

_drawn_inputs = setup_inputs


def setup_inputs(seed=0):
    import zlib

    import numpy as np

    out = dict(_drawn_inputs(seed))
    spreads = {'L0_attn_ln_g': (1.0, 0.2),
     'L0_attn_ln_b': (0.0, 0.1),
     'L0_ffn_ln1_weight': (1.0, 0.6),
     'L0_ffn_ln1_bias': (0.0, 0.8),
     'L0_ffn_ln2_weight': (1.0, 0.6),
     'L0_ffn_ln2_bias': (0.0, 0.8)}
    factors = {'L0_attn_w1_b': 3.05,
     'L0_ffn_qkv_weight': 3.421,
     'L0_ffn_proj_weight': 3.461,
     'L0_ffn_router_weight': 8.0,
     'L0_ffn_moe_w1': 8.0,
     'L0_ffn_moe_w2': 8.0}
    for name, (base, spread) in spreads.items():
        noise = np.random.default_rng([zlib.crc32(name.encode()), seed]).standard_normal(out[name].shape)
        drawn = base * np.exp(spread * noise) if base else spread * noise
        out[name] = jnp.asarray(drawn.astype(out[name].dtype))
    for name, factor in factors.items():
        out[name] = (out[name] * factor).astype(out[name].dtype)
    return out
```

```python
from contextlib import ExitStack

import concourse.bass as bass
from concourse import mybir

F32 = mybir.dt.float32
ALU = mybir.AluOpType
ACT = mybir.ActivationFunctionType
AX = mybir.AxisListType

P = 128
D = 128
HALF = 4
EPS = 1e-5
TWO_PI_HI = 6.28125
TWO_PI_LO = 0.0019353071795864769
ROUND = 12582912.0
MASKED = -3.4028234663852886e38
NKV, REP, HD = 4, 4, 8
NH = NKV * REP


class Signal:

    def __init__(self, sem, per_block):
        self.sem, self.per_block = sem, per_block

    def at(self, block, k):
        return self.per_block * block + k

    def before(self, block, k):
        return self.per_block * block - self.per_block + k


def has_earlier(block):
    return not (isinstance(block, int) and block == 0)


def build(nc, x, W_in, b_in, plog, W_mid, b_mid, w1_w, w1_b, w2_w, w2_b, ln_g, ln_b,
          ln1_w, ln1_b, ln2_w, ln2_b, qkv_w, proj_w, router_w, moe_w1, moe_w2, out):
    NS, T, _ = x.shape
    NB = T // P
    NE, _, FF = moe_w1.shape
    NF = FF // 128
    QKV = qkv_w.shape[0]
    GROUPS = 2 * NE
    row_of = [s * (s + 1) // 2 for s in range(NS + 1)]
    assert NS == 2 * HALF and NF == 2 and QKV == (NH + 2 * NKV) * HD
    POOL_S = range(0, 4)
    DVE_S = range(4, NS)

    with ExitStack() as ctx:
        def sb(name, *shape):
            return ctx.enter_context(nc.sbuf_tensor(name, list(shape), F32))

        def sem(name):
            return ctx.enter_context(nc.semaphore(name))

        def signal(name, per_block):
            return Signal(sem(name), per_block)

        win = sb("win", P, 3, D)
        wmid = sb("wmid", P, 2, D)
        w1 = sb("w1", P, D)
        w2 = sb("w2", P, D)
        qkv_rows = sb("qkv_rows", P, 2, D)
        qkvT = sb("qkvT", P, QKV)
        proj_rows = sb("proj_rows", P, D)
        projT = sb("projT", P, D)
        proj_perm = sb("proj_perm", P, D)
        router_rows = sb("router_rows", NE, D)
        routerT = sb("routerT", P, NE)
        ew1 = sb("ew1", P, NE, FF)
        ew2 = sb("ew2", P, NE, NF, D)
        ident = sb("ident", P, P)
        vecs = sb("vecs", P, 16)
        vec_rows = sb("vec_rows", 14, D)
        rowv = sb("rowv", 1, 2, D)
        ones_row = sb("ones_row", 1, P)
        gb = sb("gb", P, 2, D)
        lam = sb("lam", P, 16)
        basis = sb("basis", P, 8, 2)
        phase = sb("phase", P, 2, P)
        gphase = sb("gphase", P, 2, P)
        ptmp = sb("ptmp", P, 2, 64)
        decay = sb("decay", P, NS, P)
        minus_half = sb("minus_half", P, NS)
        eps_tile = sb("eps_tile", P, NS)
        rank8 = sb("rank8", P, NS, NE)

        VEC = dict(b0=0, b1=1, b2=2, m0=3, m1=4, w1b=5, w2b=6, l1w=7, l1b=8, l2w=9, l2b=10,
                   nu=11, theta=12, gamma=13, bo=14, bo2=15)

        def vec(name):
            return vecs[:, VEC[name]:VEC[name] + 1]

        x_in = sb("x_in", P, NS, D)
        xb = sb("xb", P, NS, D)
        xT = sb("xT", P, 2, HALF * P)
        rot = sb("rot", P, 4, HALF * P)
        drive = sb("drive", P, 2, NS, P)
        state = sb("state", P, 2, NS, P)
        init = sb("init", P, 2, NS)
        ctmp = sb("ctmp", P, 2, NS)
        post = sb("post", P, 4, NS, P)
        hid = sb("hid", P, 2, NS, P)
        outT = sb("outT", P, 2, HALF * P)
        outT2 = sb("outT2", P, 2, HALF * P)
        gT = sb("gT", P, 2, HALF * P)
        z = sb("z", P, NS, D)
        stA = sb("stA", P, NS, 6)
        mvA = sb("mvA", P, 3, NS)
        rsA = sb("rsA", P, 1, NS)
        stB = sb("stB", P, NS, 6)
        mvB = sb("mvB", P, 3, NS)
        rsB = sb("rsB", P, 4, NS)
        x1 = sb("x1", P, NS, D)
        xh = sb("xh", P, NS, D)
        lnT = sb("lnT", P, 2, HALF * P)
        qk = sb("qk", P, NS, 160)
        vx = sb("vx", P, NS, NH * HD)
        prod = sb("prod", P, row_of[NS], NH * HD)
        scores = sb("scores", P, NS, NS, NH)
        probs = sb("probs", P, NS, NS, NH)
        smax = sb("smax", P, NS, NH)
        ssum = sb("ssum", P, NS, NH)
        srec = sb("srec", P, NS, NH)
        att = sb("att", P, NS, NH * HD)
        attT = sb("attT", P, 2, HALF * P)
        tmpS = sb("tmpS", P, 5, NS)
        h2 = sb("h2", P, NS, D)
        stC = sb("stC", P, NS, 6)
        mvC = sb("mvC", P, 3, NS)
        rsC = sb("rsC", P, 1, NS)
        xh2 = sb("xh2", P, NS, D)
        l2T = sb("l2T", P, 2, HALF * P)
        rt = sb("rt", P, 6, NS, NE)
        rt1 = sb("rt1", P, 6, NS)
        gates = sb("gates", P, NS, NE)
        res = sb("res", P, NS, D)
        hT = sb("hT", P, 2, NF, HALF * P)
        stD = sb("stD", P, NS, 6)
        mvD = sb("mvD", P, 3, NS)
        rsD = sb("rsD", P, 1, NS)
        y = sb("y", P, NS, D)

        bank = [ctx.enter_context(nc.psum_tensor(f"bank{i}", [P, 512], F32)) for i in range(8)]
        bA, bB, bC, bD, bE, bF, bG, bH = bank

        w_loaded = sem("w_loaded")
        setup_pool = sem("setup_pool")
        setup_dve = sem("setup_dve")
        setup_act = sem("setup_act")
        setup_act_own = sem("setup_act_own")
        chain = sem("chain")
        setup_pe = sem("setup_pe")
        x_loaded = signal("x_loaded", 16)
        xb_done = signal("xb_done", 1)
        xT_ps = signal("xT_ps", 2)
        xT_done = signal("xT_done", 2)
        u_ps = signal("u_ps", 2)
        rot_done = signal("rot_done", 2)
        drive_done = signal("drive_done", 4)
        inject_done = signal("inject_done", 1)
        scan_done = signal("scan_done", 2)
        carry_mul = signal("carry_mul", 2)
        carry_done = signal("carry_done", 2)
        post_done = signal("post_done", 2)
        hid_done = signal("hid_done", 4)
        out_ps = signal("out_ps", 2)
        outT_done = signal("outT_done", 4)
        z_ps = signal("z_ps", 2)
        gT_done = signal("gT_done", 2)
        y_ps = signal("y_ps", 2)
        statA = signal("statA", 2)
        partA = signal("partA", 8)
        spreadA = signal("spreadA", 4)
        meanA = signal("meanA", 2)
        rstdA = signal("rstdA", 2)
        centred = signal("centred", 2)
        z_done = signal("z_done", 2)
        statB = signal("statB", 1)
        partB = signal("partB", 4)
        spreadB = signal("spreadB", 2)
        meanB = signal("meanB", 1)
        stepB = signal("stepB", 5)
        rstdB = signal("rstdB", 1)
        x1_done = signal("x1_done", 1)
        xh_done = signal("xh_done", 1)
        xhT_ps = signal("xhT_ps", 2)
        lnT_done = signal("lnT_done", 2)
        qkv_ps = signal("qkv_ps", 4)
        qkv_done = signal("qkv_done", 8)
        qk_pool = signal("qk_pool", 1)
        qk_dve = signal("qk_dve", 1)
        scores_done = signal("scores_done", 1)
        smax_done = signal("smax_done", 1)
        shift_done = signal("shift_done", 1)
        exp_done = signal("exp_done", 1)
        ssum_done = signal("ssum_done", 1)
        srec_done = signal("srec_done", 1)
        probs_done = signal("probs_done", 1)
        pv_pool = signal("pv_pool", 1)
        pv_dve = signal("pv_dve", 1)
        att_done = signal("att_done", 1)
        attT_ps = signal("attT_ps", 2)
        attT_done = signal("attT_done", 2)
        proj_ps = signal("proj_ps", 2)
        h2_done = signal("h2_done", 2)
        statC = signal("statC", 1)
        partC = signal("partC", 4)
        spreadC = signal("spreadC", 2)
        meanC = signal("meanC", 1)
        rstdC = signal("rstdC", 1)
        xh2_done = signal("xh2_done", 1)
        l2_ps = signal("l2_ps", 2)
        l2T_done = signal("l2T_done", 2)
        logit_ps = signal("logit_ps", 1)
        gstep = signal("gstep", 14)
        lshift = signal("lshift", 1)
        gexp = signal("gexp", 1)
        two_done = signal("two_done", 1)
        both_done = signal("both_done", 1)
        gates_done = signal("gates_done", 1)
        res_init = signal("res_init", 1)
        h_ps = signal("h_ps", NF * GROUPS)
        hT_done = signal("hT_done", NF * GROUPS)
        moe_ps = signal("moe_ps", GROUPS)
        acc_done = signal("acc_done", GROUPS)
        statD = signal("statD", 2)
        partD = signal("partD", 8)
        spreadD = signal("spreadD", 4)
        meanD = signal("meanD", 2)
        rstdD = signal("rstdD", 2)
        y_done = signal("y_done", 2)
        stored = [signal(f"stored{q}", 16) for q in range(2)]

        block = ctx.enter_context(nc.Block())

        def pipeline(eng, iteration):
            iteration(-1, True, False, False)
            iteration(0, True, True, False)
            iteration(1, True, True, True)
            with eng.Fori(2, NB - 1) as i:
                iteration(i, True, True, True)
            iteration(NB - 1, False, True, True)
            iteration(NB, False, False, True)

        def tiles(q):
            return range(HALF * q, HALF * q + HALF)

        def cols(n):
            return slice(n % HALF * P, n % HALF * P + P)

        def over_tiles(table, n):
            return table.unsqueeze(1).to_broadcast([P, n, P])

        SETUP_GB = 2
        W_ALL = 16 * 22

        def qk_product(g, s):
            n = s + 1
            o = prod[:, row_of[s]:row_of[s + 1], :].rearrange("p t (r c) -> p t r c", r=REP)
            q = qk[:, s, 0:NH * HD].rearrange("p (r c) -> p r c", r=REP).unsqueeze(1).to_broadcast([P, n, REP, NKV * HD])
            kk = qk[:, 0:n, NH * HD:160].unsqueeze(2).to_broadcast([P, n, REP, NKV * HD])
            return g.tensor_tensor(o, q, kk, ALU.mult)

        def pv_product(g, s):
            n = s + 1
            o = prod[:, row_of[s]:row_of[s + 1], :].rearrange("p t (h d) -> p (t h) d", d=HD)
            pr = probs[:, s, 0:n, :].rearrange("p t h -> p (t h)").unsqueeze(2).to_broadcast([P, n * NH, HD])
            v = vx[:, 0:n, :].rearrange("p t (h d) -> p (t h) d", d=HD)
            return g.tensor_tensor(o, pr, v, ALU.mult)


        @block.sync
        def _(sp):
            def load_x(b):
                if has_earlier(b):
                    sp.wait_ge(xT_ps.sem, xT_ps.before(b, 2))
                if has_earlier(b):
                    sp.wait_ge(xb_done.sem, xb_done.before(b, 1))
                sp.dma_start(x_in[:], x[:, bass.ts(b, P), :].rearrange("s p d -> p s d")).then_inc(x_loaded.sem, 16)

            def store(k, q):
                sp.wait_ge(y_done.sem, y_done.at(k, q + 1))
                sp.dma_start(out[HALF * q:HALF * q + HALF, bass.ts(k, P), :].rearrange("s p d -> p s d"),
                             y[:, HALF * q:HALF * q + HALF, :]).then_inc(stored[q].sem, 16)

            load_x(0)
            for dst, src in (
                (win[:], W_in.rearrange("e d h -> d e h")),
                (wmid[:], W_mid.rearrange("e d h -> d e h")),
                (w1[:], w1_w), (w2[:], w2_w),
                (qkv_rows[:, 0, :], qkv_w[0:P, :]), (qkv_rows[0:QKV - P, 1, :], qkv_w[P:QKV, :]),
                (proj_rows[:], proj_w), (router_rows[:], router_w),
                (vec_rows[0:3, :], b_in), (vec_rows[3:5, :], b_mid), (vec_rows[11:14, :], plog),
                *((vec_rows[VEC[name]:VEC[name] + 1, :], row.rearrange("(a d) -> a d", a=1)) for name, row in
                  (("w1b", w1_b), ("w2b", w2_b), ("l1w", ln1_w), ("l1b", ln1_b), ("l2w", ln2_w), ("l2b", ln2_b))),
                (rowv[:, 0, :], ln_g.rearrange("(a d) -> a d", a=1)), (rowv[:, 1, :], ln_b.rearrange("(a d) -> a d", a=1)),
                (ew1[:], moe_w1.rearrange("e d f -> d e f")),
                (ew2[:, 0:NE // 2], moe_w2[0:NE // 2].rearrange("e (g f) d -> f e g d", g=NF)),
                (ew2[:, NE // 2:NE], moe_w2[NE // 2:NE].rearrange("e (g f) d -> f e g d", g=NF)),
            ):
                sp.dma_start(dst, src).then_inc(w_loaded, 16)

            def iteration(i, do_mixer, do_attn, do_moe):
                if do_mixer and not (isinstance(i, int) and i == -1):
                    load_x(i + 1)
                if do_moe:
                    store(i - 1, 0)
                    store(i - 1, 1)

            pipeline(sp, iteration)
            for q in range(2):
                sp.wait_ge(stored[q].sem, stored[q].at(NB, 0))

        @block.gpsimd
        def _(pool):
            g = nc.gpsimd
            g.memset(ident[:], 0.0).then_inc(setup_pool, 1)
            g.memset(ones_row[:], 1.0)
            g.memset(minus_half[:], -0.5)
            g.memset(eps_tile[:], EPS)
            g.memset(init[:], 0.0)
            g.memset(scores[:], MASKED)
            for e in range(NE):
                g.memset(rank8[:, :, e:e + 1], float(NE - e))
            pool.wait_ge(setup_pool, 1)
            g.affine_select(out=ident[:], in_=ident[:], compare_op=ALU.not_equal, fill=1.0, base=0,
                            pattern=[[-1, P]], channel_multiplier=1).then_inc(setup_pool, 1)

            def sum_xb(b):
                pool.wait_ge(x_loaded.sem, x_loaded.at(b, 16))
                if has_earlier(b):
                    pool.wait_ge(z_done.sem, z_done.before(b, 2))
                if isinstance(b, int) and b == 0:
                    pool.wait_ge(setup_dve, SETUP_GB)
                g.tensor_tensor(xb[:], x_in[:], over_tiles(gb[:, 1, :], NS), ALU.add).then_inc(xb_done.sem, 1)

            def sum_drive(b, q):
                pool.wait_ge(rot_done.sem, rot_done.at(b, q + 1))
                if has_earlier(b):
                    pool.wait_ge(scan_done.sem, scan_done.before(b, 2))
                t = slice(HALF * q, HALF * q + HALF)
                r = [rot[:, n, :].rearrange("p (s t) -> p s t", t=P) for n in range(4)]
                g.tensor_tensor(drive[:, 0, t, :], r[0], r[1], ALU.add).then_inc(drive_done.sem, 1)
                g.tensor_tensor(drive[:, 1, t, :], r[2], r[3], ALU.subtract).then_inc(drive_done.sem, 1)

            def sum_hid(b, q):
                pool.wait_ge(post_done.sem, post_done.at(b, q + 1))
                if has_earlier(b):
                    pool.wait_ge(out_ps.sem, out_ps.before(b, 2))
                t = slice(HALF * q, HALF * q + HALF)
                g.tensor_tensor(hid[:, 0, t, :], post[:, 0, t, :], post[:, 1, t, :], ALU.subtract).then_inc(hid_done.sem, 1)
                g.tensor_tensor(hid[:, 1, t, :], post[:, 2, t, :], post[:, 3, t, :], ALU.add).then_inc(hid_done.sem, 1)

            def rstd(mean_sig, rstd_sig, mv, rs, blk, k, t):
                pool.wait_ge(mean_sig.sem, mean_sig.at(blk, k))
                g.tensor_tensor(rs[:, 0, t], mv[:, 2, t], minus_half[:, t], ALU.pow).then_inc(rstd_sig.sem, 1)

            def rstd_b(b):
                pool.wait_ge(meanB.sem, meanB.at(b, 1))
                g.tensor_tensor(rsB[:, 0, :], mvB[:, 2, :], minus_half[:], ALU.pow).then_inc(stepB.sem, 1)
                pool.wait_ge(stepB.sem, stepB.at(b, 1))
                g.tensor_tensor(rsB[:, 1, :], rsB[:, 0, :], rsB[:, 0, :], ALU.mult).then_inc(stepB.sem, 1)
                pool.wait_ge(stepB.sem, stepB.at(b, 2))
                g.tensor_tensor(rsB[:, 1, :], rsB[:, 1, :], mvB[:, 1, :], ALU.mult).then_inc(stepB.sem, 1)
                pool.wait_ge(stepB.sem, stepB.at(b, 3))
                g.tensor_tensor(rsB[:, 1, :], rsB[:, 1, :], eps_tile[:], ALU.add).then_inc(stepB.sem, 1)
                pool.wait_ge(stepB.sem, stepB.at(b, 4))
                g.tensor_tensor(rsB[:, 2, :], rsB[:, 1, :], minus_half[:], ALU.pow).then_inc(stepB.sem, 1)
                pool.wait_ge(stepB.sem, stepB.at(b, 5))
                g.tensor_tensor(rsB[:, 3, :], rsB[:, 2, :], rsB[:, 0, :], ALU.mult).then_inc(rstdB.sem, 1)

            def qk_products(j):
                pool.wait_ge(qkv_done.sem, qkv_done.at(j, 8))
                if has_earlier(j):
                    pool.wait_ge(att_done.sem, att_done.before(j, 1))
                for s in POOL_S:
                    last = qk_product(g, s)
                last.then_inc(qk_pool.sem, 1)

            def pv_products(j):
                pool.wait_ge(probs_done.sem, probs_done.at(j, 1))
                pool.wait_ge(scores_done.sem, scores_done.at(j, 1))
                for s in POOL_S:
                    last = pv_product(g, s)
                last.then_inc(pv_pool.sem, 1)

            def init_res(j):
                pool.wait_ge(h2_done.sem, h2_done.at(j, 2))
                pool.wait_ge(x1_done.sem, x1_done.at(j, 1))
                if has_earlier(j):
                    pool.wait_ge(y_done.sem, y_done.before(j, 2))
                g.tensor_tensor(res[:], x1[:], h2[:], ALU.add).then_inc(res_init.sem, 1)

            def iteration(i, do_mixer, do_attn, do_moe):
                b, j, k = i + 1, i, i - 1
                if do_mixer:
                    sum_drive(b, 0)
                    sum_drive(b, 1)
                    sum_xb(b)
                    sum_hid(b, 0)
                    sum_hid(b, 1)
                if do_attn:
                    qk_products(j)
                if do_moe:
                    rstd(meanD, rstdD, mvD, rsD, k, 1, slice(0, HALF))
                if do_attn:
                    pv_products(j)
                if do_mixer:
                    for q in range(2):
                        rstd(meanA, rstdA, mvA, rsA, b, q + 1, slice(HALF * q, HALF * q + HALF))
                if do_attn:
                    rstd(meanC, rstdC, mvC, rsC, j, 1, slice(0, NS))
                if do_mixer:
                    rstd_b(b)
                if do_moe:
                    rstd(meanD, rstdD, mvD, rsD, k, 2, slice(HALF, NS))
                if do_attn:
                    init_res(j)

            pipeline(pool, iteration)

        @block.vector
        def _(dve):
            v = nc.vector
            steps = [0]

            def link(ins):
                ins.then_inc(chain, 1)
                steps[0] += 1
                dve.wait_ge(chain, steps[0])

            dve.wait_ge(w_loaded, W_ALL)
            dve.wait_ge(setup_pe, 1)
            link(v.tensor_copy(vecs[:, 0:14], bF[:, 0:14]))
            link(v.tensor_scalar(wmid[:, 1, :], wmid[:, 1, :], -1.0, None, ALU.mult))
            link(v.tensor_tensor(vec("bo"), vec("m0"), vec("m1"), ALU.subtract))
            link(v.tensor_tensor(vec("bo"), vec("bo"), vec("b2"), ALU.add))
            link(v.tensor_tensor(vec("bo2"), vec("bo"), vec("w2b"), ALU.add))
            link(v.tensor_copy(proj_perm[:].rearrange("p (r g d) -> p r g d", g=NKV, d=HD),
                               proj_rows[:].rearrange("p (g r d) -> p r g d", r=REP, d=HD)))
            v.tensor_copy(lam[:, 15:16], vec("bo2")).then_inc(setup_dve, 1)
            dve.wait_ge(setup_pe, 2)
            link(v.tensor_copy(qkvT[:, 0:P].rearrange("p (r g d) -> p r g d", g=NKV, d=HD),
                               bD[:, 0:P].rearrange("p (g r d) -> p r g d", r=REP, d=HD)))
            link(v.tensor_copy(qkvT[:, P:QKV], bD[:, P:QKV]))
            link(v.tensor_copy(projT[:], bD[:, 256:384]))
            link(v.tensor_copy(routerT[:], bD[:, 384:384 + NE]))
            v.tensor_copy(gb[:].rearrange("p a d -> p (a d)"), bE[:, 0:2 * D]).then_inc(setup_dve, 1)

            dve.wait_ge(setup_act, 1)
            nu, theta, gamma = (lam[:, n:n + 1] for n in range(3))
            turns, absth = lam[:, 3:4], lam[:, 4:5]
            link(v.tensor_scalar(turns, theta, 0.15915494309189535, None, ALU.mult))
            link(v.tensor_scalar(turns, turns, ROUND, None, ALU.add))
            link(v.tensor_scalar(turns, turns, ROUND, None, ALU.subtract))
            link(v.scalar_tensor_tensor(theta, turns, -TWO_PI_HI, theta, ALU.mult, ALU.add))
            link(v.scalar_tensor_tensor(theta, turns, -TWO_PI_LO, theta, ALU.mult, ALU.add))
            link(v.tensor_scalar(theta, theta, 3.1415925, -3.1415925, ALU.min, ALU.max))
            link(v.tensor_scalar(absth, theta, -1.0, None, ALU.mult))
            link(v.tensor_tensor(absth, absth, theta, ALU.min))
            v.tensor_scalar(absth, absth, 1.5707963267948966, None, ALU.add).then_inc(setup_dve, 1)
            dve.wait_ge(setup_act, 2)
            r = lam[:, 5:6]
            link(v.memset(phase[:, 0, 0:1], 1.0))
            link(v.memset(phase[:, 1, 0:1], 0.0))
            n = 1
            while n <= P // 2:
                c, s = basis[:, n.bit_length() - 1, 0:1], basis[:, n.bit_length() - 1, 1:2]
                c2, s2 = basis[:, n.bit_length(), 0:1], basis[:, n.bit_length(), 1:2]
                for cc, ss, co, so in ((phase[:, 0, 0:n], phase[:, 1, 0:n], phase[:, 0, n:2 * n], phase[:, 1, n:2 * n]),
                                       (c, s, c2, s2)):
                    m = cc.shape[1]
                    link(v.tensor_scalar(ptmp[:, 0, 0:m], ss, s, None, ALU.mult))
                    link(v.tensor_scalar(ptmp[:, 1, 0:m], cc, s, None, ALU.mult))
                    link(v.scalar_tensor_tensor(co, cc, c, ptmp[:, 0, 0:m], ALU.mult, ALU.subtract))
                    link(v.scalar_tensor_tensor(so, ss, c, ptmp[:, 1, 0:m], ALU.mult, ALU.add))
                n *= 2
            link(v.tensor_scalar(gphase[:], phase[:], gamma, None, ALU.mult))
            link(v.memset(decay[:], 1.0))
            link(v.tensor_scalar(decay[:], decay[:], r, None, ALU.mult))
            link(v.memset(decay[:, :, 0:1], 0.0))
            dve.wait_ge(setup_pool, 2)
            turn_c, turn_s = basis[:, 7, 0:1], basis[:, 7, 1:2]

            def rotate_in(b, q):
                dve.wait_ge(u_ps.sem, u_ps.at(b, q + 1))
                if q == 0:
                    if has_earlier(b):
                        dve.wait_ge(drive_done.sem, drive_done.before(b, 4))
                else:
                    dve.wait_ge(drive_done.sem, drive_done.at(b, 2))
                gc, gs = (over_tiles(gphase[:, n, :], HALF) for n in range(2))
                ur, ui = (bk[:].rearrange("p (s t) -> p s t", t=P) for bk in (bB, bC))
                o = [rot[:, n, :].rearrange("p (s t) -> p s t", t=P) for n in range(4)]
                v.scalar_tensor_tensor(o[0], ur, vec("b0"), gc, ALU.add, ALU.mult)
                v.scalar_tensor_tensor(o[1], ui, vec("b1"), gs, ALU.add, ALU.mult)
                v.scalar_tensor_tensor(o[2], ui, vec("b1"), gc, ALU.add, ALU.mult)
                v.scalar_tensor_tensor(o[3], ur, vec("b0"), gs, ALU.add, ALU.mult).then_inc(rot_done.sem, 1)

            def inject(b):
                dve.wait_ge(drive_done.sem, drive_done.at(b, 4))
                if has_earlier(b):
                    dve.wait_ge(carry_done.sem, carry_done.before(b, 2))
                first = drive[:, :, :, 0]
                v.scalar_tensor_tensor(first, init[:], r, first, ALU.mult, ALU.add).then_inc(inject_done.sem, 1)

            def scan(b, part):
                if part == 0:
                    dve.wait_ge(inject_done.sem, inject_done.at(b, 1))
                v.tensor_tensor_scan(state[:, part].rearrange("p s t -> p (s t)"), decay[:].rearrange("p s t -> p (s t)"),
                                     drive[:, part].rearrange("p s t -> p (s t)"), 0.0, ALU.mult, ALU.add).then_inc(scan_done.sem, 1)

            def carry(b):
                dve.wait_ge(scan_done.sem, scan_done.at(b, 2))
                re, im = state[:, 0, :, P - 1], state[:, 1, :, P - 1]
                v.tensor_scalar(ctmp[:, 0, :], im, turn_s, None, ALU.mult).then_inc(carry_mul.sem, 1)
                v.tensor_scalar(ctmp[:, 1, :], re, turn_s, None, ALU.mult).then_inc(carry_mul.sem, 1)
                dve.wait_ge(carry_mul.sem, carry_mul.at(b, 2))
                v.scalar_tensor_tensor(init[:, 0, :], re, turn_c, ctmp[:, 0, :], ALU.mult, ALU.subtract).then_inc(carry_done.sem, 1)
                v.scalar_tensor_tensor(init[:, 1, :], im, turn_c, ctmp[:, 1, :], ALU.mult, ALU.add).then_inc(carry_done.sem, 1)

            def rotate_out(b, q):
                if q == 0:
                    if has_earlier(b):
                        dve.wait_ge(hid_done.sem, hid_done.before(b, 4))
                t = slice(HALF * q, HALF * q + HALF)
                c, s = (over_tiles(phase[:, n, :], HALF) for n in range(2))
                re, im = state[:, 0, t, :], state[:, 1, t, :]
                v.tensor_tensor(post[:, 0, t, :], re, c, ALU.mult)
                v.tensor_tensor(post[:, 1, t, :], im, s, ALU.mult)
                v.tensor_tensor(post[:, 2, t, :], re, s, ALU.mult)
                v.tensor_tensor(post[:, 3, t, :], im, c, ALU.mult).then_inc(post_done.sem, 1)

            def stats(src, st, mv, sigs, blk, k, ts):
                stat_sig, part_sig, spread_sig, mean_sig = sigs
                for n in ts:
                    last = v.bn_stats(st[:, n, :], src(n))
                last.then_inc(stat_sig.sem, 1)
                t = slice(ts[0], ts[-1] + 1)
                total, gap, dev, gap2, dev_eps = (tmpS[:, m, t] for m in range(5))
                dve.wait_ge(stat_sig.sem, stat_sig.at(blk, k))
                v.tensor_tensor(gap, st[:, t, 1], st[:, t, 4], ALU.subtract).then_inc(part_sig.sem, 1)
                v.tensor_tensor(dev, st[:, t, 2], st[:, t, 5], ALU.add).then_inc(part_sig.sem, 1)
                v.tensor_tensor(total, st[:, t, 1], st[:, t, 4], ALU.add).then_inc(part_sig.sem, 1)
                dve.wait_ge(part_sig.sem, part_sig.at(blk, 4 * k - 1))
                v.scalar_tensor_tensor(gap2, gap, 0.25, gap, ALU.mult, ALU.mult).then_inc(spread_sig.sem, 1)
                v.tensor_scalar(dev_eps, dev, 1.0 / D, EPS, ALU.mult, ALU.add).then_inc(spread_sig.sem, 1)
                v.tensor_scalar(mv[:, 0, t], total, 0.5, None, ALU.mult)
                dve.wait_ge(spread_sig.sem, spread_sig.at(blk, 2 * k))
                v.scalar_tensor_tensor(mv[:, 1, t], dev, 1.0 / D, gap2, ALU.mult, ALU.add).then_inc(part_sig.sem, 1)
                v.tensor_tensor(mv[:, 2, t], dev_eps, gap2, ALU.add).then_inc(mean_sig.sem, 1)

            def mean_a(b, q):
                dve.wait_ge(y_ps.sem, y_ps.at(b, q + 1))
                bk = (bB, bC)[q]
                stats(lambda n: bk[:, cols(n)], stA, mvA, (statA, partA, spreadA, meanA), b, q + 1, tiles(q))
                dve.wait_ge(meanA.sem, meanA.at(b, q + 1))
                for n in tiles(q):
                    last = v.scalar_tensor_tensor(z[:, n, :], bk[:, cols(n)], mvA[:, 0, n:n + 1], gb[:, 0, :],
                                                  ALU.subtract, ALU.mult)
                last.then_inc(centred.sem, 1)

            def finish_a(b, q):
                dve.wait_ge(rstdA.sem, rstdA.at(b, q + 1))
                dve.wait_ge(centred.sem, centred.at(b, q + 1))
                dve.wait_ge(xb_done.sem, xb_done.at(b, 1))
                for n in tiles(q):
                    last = v.scalar_tensor_tensor(z[:, n, :], z[:, n, :], rsA[:, 0, n:n + 1], xb[:, n, :],
                                                  ALU.mult, ALU.add)
                last.then_inc(z_done.sem, 1)

            def mean_b(b):
                dve.wait_ge(z_done.sem, z_done.at(b, 2))
                stats(lambda n: z[:, n, :], stB, mvB, (statB, partB, spreadB, meanB), b, 1, range(NS))

            def finish_b(b):
                dve.wait_ge(rstdB.sem, rstdB.at(b, 1))
                if has_earlier(b):
                    dve.wait_ge(res_init.sem, res_init.before(b, 1))
                for n in range(NS):
                    last = v.tensor_scalar(x1[:, n, :], z[:, n, :], mvB[:, 0, n:n + 1], rsB[:, 0, n:n + 1],
                                           ALU.subtract, ALU.mult)
                last.then_inc(x1_done.sem, 1)
                if has_earlier(b):
                    dve.wait_ge(xhT_ps.sem, xhT_ps.before(b, 2))
                for n in range(NS):
                    last = v.tensor_scalar(xh[:, n, :], z[:, n, :], mvB[:, 0, n:n + 1], rsB[:, 3, n:n + 1],
                                           ALU.subtract, ALU.mult)
                last.then_inc(xh_done.sem, 1)

            def qk_products(j):
                dve.wait_ge(qkv_done.sem, qkv_done.at(j, 8))
                for s in DVE_S:
                    last = qk_product(v, s)
                last.then_inc(qk_dve.sem, 1)

            def sum_scores(j):
                dve.wait_ge(qk_dve.sem, qk_dve.at(j, 1))
                for s in [*DVE_S, *POOL_S]:
                    if s == POOL_S[0]:
                        dve.wait_ge(qk_pool.sem, qk_pool.at(j, 1))
                    last = v.tensor_reduce(scores[:, s, 0:s + 1, :].rearrange("p t h -> p (t h)"),
                                           prod[:, row_of[s]:row_of[s + 1], :].rearrange("p t (h d) -> p (t h) d", d=HD),
                                           AX.X, ALU.add)
                last.then_inc(scores_done.sem, 1)

            def softmax_in(j):
                dve.wait_ge(scores_done.sem, scores_done.at(j, 1))
                v.tensor_reduce(smax[:], scores[:].rearrange("p s t h -> p s h t"), AX.X, ALU.max).then_inc(smax_done.sem, 1)
                dve.wait_ge(smax_done.sem, smax_done.at(j, 1))
                if has_earlier(j):
                    dve.wait_ge(pv_pool.sem, pv_pool.before(j, 1))
                v.tensor_tensor(probs[:], scores[:], smax[:].unsqueeze(2).to_broadcast([P, NS, NS, NH]),
                                ALU.subtract).then_inc(shift_done.sem, 1)

            def softmax_out(j):
                dve.wait_ge(exp_done.sem, exp_done.at(j, 1))
                v.tensor_reduce(ssum[:], probs[:].rearrange("p s t h -> p s h t"), AX.X, ALU.add).then_inc(ssum_done.sem, 1)
                dve.wait_ge(ssum_done.sem, ssum_done.at(j, 1))
                v.reciprocal(srec[:], ssum[:]).then_inc(srec_done.sem, 1)
                dve.wait_ge(srec_done.sem, srec_done.at(j, 1))
                v.tensor_tensor(probs[:], probs[:], srec[:].unsqueeze(2).to_broadcast([P, NS, NS, NH]),
                                ALU.mult).then_inc(probs_done.sem, 1)

            def pv_products(j):
                dve.wait_ge(probs_done.sem, probs_done.at(j, 1))
                for s in DVE_S:
                    last = pv_product(v, s)
                last.then_inc(pv_dve.sem, 1)

            def sum_pv(j):
                dve.wait_ge(pv_dve.sem, pv_dve.at(j, 1))
                if has_earlier(j):
                    dve.wait_ge(attT_ps.sem, attT_ps.before(j, 2))
                for s in [*DVE_S, *POOL_S]:
                    if s == POOL_S[0]:
                        dve.wait_ge(pv_pool.sem, pv_pool.at(j, 1))
                    last = v.tensor_reduce(att[:, s, :], prod[:, row_of[s]:row_of[s + 1], :].rearrange("p t c -> p c t"),
                                           AX.X, ALU.add)
                last.then_inc(att_done.sem, 1)

            def residual(j):
                if has_earlier(j):
                    dve.wait_ge(res_init.sem, res_init.before(j, 1))
                for q in range(2):
                    dve.wait_ge(proj_ps.sem, proj_ps.at(j, q + 1))
                    t = slice(HALF * q, HALF * q + HALF)
                    v.tensor_tensor(h2[:, t, :], (bD, bE)[q][:].rearrange("p (s t) -> p s t", t=P), x1[:, t, :],
                                    ALU.add).then_inc(h2_done.sem, 1)
                dve.wait_ge(h2_done.sem, h2_done.at(j, 2))
                stats(lambda n: h2[:, n, :], stC, mvC, (statC, partC, spreadC, meanC), j, 1, range(NS))

            def normalise_c(j):
                dve.wait_ge(rstdC.sem, rstdC.at(j, 1))
                dve.wait_ge(meanC.sem, meanC.at(j, 1))
                if has_earlier(j):
                    dve.wait_ge(l2_ps.sem, l2_ps.before(j, 2))
                for n in range(NS):
                    last = v.tensor_scalar(xh2[:, n, :], h2[:, n, :], mvC[:, 0, n:n + 1], rsC[:, 0, n:n + 1],
                                           ALU.subtract, ALU.mult)
                last.then_inc(xh2_done.sem, 1)

            def gate(j):
                count = [0]

                def step(ins):
                    ins.then_inc(gstep.sem, 1)
                    count[0] += 1
                    dve.wait_ge(gstep.sem, gstep.at(j, count[0]))

                def per_tile(a):
                    return a.unsqueeze(2).to_broadcast([P, NS, NE])

                dve.wait_ge(logit_ps.sem, logit_ps.at(j, 1))
                logits = bD[:, 0:NS * NE].rearrange("p (s e) -> p s e", e=NE)
                pr, key, one, two, left = (rt[:, n] for n in range(5))
                top, total, inv, best, second, k2 = (rt1[:, n] for n in range(6))
                step(v.tensor_reduce(top, logits, AX.X, ALU.max))
                v.tensor_tensor(pr, logits, per_tile(top), ALU.subtract).then_inc(lshift.sem, 1)
                dve.wait_ge(gexp.sem, gexp.at(j, 1))
                step(v.tensor_reduce(total, pr, AX.X, ALU.add))
                step(v.reciprocal(inv, total))
                step(v.tensor_tensor(pr, pr, per_tile(inv), ALU.mult))
                for src, winner, m, kk in ((pr, one, best, k2), (left, two, second, k2)):
                    step(v.tensor_reduce(m, src, AX.X, ALU.max))
                    step(v.tensor_tensor(key, src, per_tile(m), ALU.is_equal))
                    step(v.tensor_tensor(key, key, rank8[:], ALU.mult))
                    step(v.tensor_reduce(kk, key, AX.X, ALU.max))
                    if winner is one:
                        step(v.tensor_tensor(one, key, per_tile(kk), ALU.is_equal))
                        step(v.scalar_tensor_tensor(left, one, -2.0, pr, ALU.mult, ALU.add))
                v.tensor_tensor(two, key, per_tile(k2), ALU.is_equal).then_inc(two_done.sem, 1)
                dve.wait_ge(two_done.sem, two_done.at(j, 1))
                v.tensor_tensor(one, one, two, ALU.add).then_inc(both_done.sem, 1)
                dve.wait_ge(both_done.sem, both_done.at(j, 1))
                v.tensor_tensor(gates[:], pr, one, ALU.mult).then_inc(gates_done.sem, 1)

            def accumulate(k, g):
                q, e = divmod(g, NE)
                dve.wait_ge(moe_ps.sem, moe_ps.at(k, g + 1))
                if g == 0:
                    dve.wait_ge(res_init.sem, res_init.at(k, 1))
                    dve.wait_ge(gates_done.sem, gates_done.at(k, 1))
                else:
                    dve.wait_ge(acc_done.sem, acc_done.at(k, g))
                for n in tiles(q):
                    last = v.scalar_tensor_tensor(res[:, n, :], bH[:, cols(n)], gates[:, n, e:e + 1], res[:, n, :],
                                                  ALU.mult, ALU.add)
                last.then_inc(acc_done.sem, 1)

            def mean_d(k, q):
                dve.wait_ge(acc_done.sem, acc_done.at(k, NE * (q + 1)))
                stats(lambda n: res[:, n, :], stD, mvD, (statD, partD, spreadD, meanD), k, q + 1, tiles(q))

            def finish_d(k, q):
                dve.wait_ge(rstdD.sem, rstdD.at(k, q + 1))
                dve.wait_ge(meanD.sem, meanD.at(k, q + 1))
                if has_earlier(k):
                    dve.wait_ge(stored[q].sem, stored[q].before(k, 16))
                for n in tiles(q):
                    last = v.tensor_scalar(y[:, n, :], res[:, n, :], mvD[:, 0, n:n + 1], rsD[:, 0, n:n + 1],
                                           ALU.subtract, ALU.mult)
                last.then_inc(y_done.sem, 1)

            def iteration(i, do_mixer, do_attn, do_moe):
                b, j, k = i + 1, i, i - 1

                def acc(g):
                    if do_moe:
                        accumulate(k, g)

                if do_mixer:
                    rotate_in(b, 0)
                    rotate_in(b, 1)
                acc(0)
                if do_mixer:
                    inject(b)
                    scan(b, 0)
                acc(1)
                if do_mixer:
                    scan(b, 1)
                    carry(b)
                    rotate_out(b, 0)
                acc(2)
                if do_mixer:
                    rotate_out(b, 1)
                acc(3)
                if do_attn:
                    qk_products(j)
                acc(4)
                acc(5)
                if do_attn:
                    sum_scores(j)
                acc(6)
                if do_attn:
                    softmax_in(j)
                acc(7)
                if do_moe:
                    mean_d(k, 0)
                acc(8)
                if do_attn:
                    softmax_out(j)
                    pv_products(j)
                acc(9)
                if do_moe:
                    finish_d(k, 0)
                if do_attn:
                    sum_pv(j)
                acc(10)
                if do_mixer:
                    mean_a(b, 0)
                acc(11)
                if do_mixer:
                    mean_a(b, 1)
                acc(12)
                if do_attn:
                    residual(j)
                if do_mixer:
                    finish_a(b, 0)
                acc(13)
                if do_mixer:
                    finish_a(b, 1)
                    mean_b(b)
                acc(14)
                if do_attn:
                    normalise_c(j)
                acc(15)
                if do_moe:
                    mean_d(k, 1)
                    finish_d(k, 1)
                if do_mixer:
                    finish_b(b)
                if do_attn:
                    gate(j)

            pipeline(dve, iteration)

        @block.scalar
        def _(act):
            a = nc.scalar

            act.wait_ge(setup_dve, 1)
            a.activation(lam[:, 0:3], vecs[:, 11:14], ACT.Exp).then_inc(setup_act_own, 1)
            act.wait_ge(setup_act_own, 1)
            a.activation(lam[:, 5:6], lam[:, 0:1], ACT.Exp, scale=-1.0).then_inc(setup_act, 1)
            act.wait_ge(setup_dve, 3)
            a.activation(basis[:, 0, 0:1], lam[:, 4:5], ACT.Sin)
            a.activation(basis[:, 0, 1:2], lam[:, 1:2], ACT.Sin).then_inc(setup_act, 1)

            def evac_xT(b, q):
                act.wait_ge(xT_ps.sem, xT_ps.at(b, q + 1))
                if has_earlier(b):
                    act.wait_ge(out_ps.sem, out_ps.before(b, 2))
                a.activation(xT[:, q, :], bA[:], ACT.Copy).then_inc(xT_done.sem, 1)

            def evac_out(b, q):
                act.wait_ge(out_ps.sem, out_ps.at(b, q + 1))
                if has_earlier(b):
                    act.wait_ge(y_ps.sem, y_ps.before(b, 2))
                bk = (bA, bB)[q]
                a.activation(outT[:, q, :], bk[:], ACT.Identity, bias=vec("bo")).then_inc(outT_done.sem, 1)
                a.activation(outT2[:, q, :], bk[:], ACT.Identity, bias=vec("bo2")).then_inc(outT_done.sem, 1)

            def gelu_mixer(b, q):
                act.wait_ge(z_ps.sem, z_ps.at(b, q + 1))
                a.activation(gT[:, q, :], (bC, bA)[q][:], ACT.Gelu, bias=vec("w1b")).then_inc(gT_done.sem, 1)

            def evac_ln(j, q):
                act.wait_ge(xhT_ps.sem, xhT_ps.at(j, q + 1))
                if has_earlier(j):
                    act.wait_ge(qkv_ps.sem, qkv_ps.before(j, 4))
                a.activation(lnT[:, q, :], (bD, bE)[q][:], ACT.Identity, bias=vec("l1b"), scale=vec("l1w")).then_inc(lnT_done.sem, 1)

            def evac_qkv(j, n):
                act.wait_ge(qkv_ps.sem, qkv_ps.at(j, n + 1))
                if n == 0:
                    if has_earlier(j):
                        act.wait_ge(scores_done.sem, scores_done.before(j, 1))
                    if has_earlier(j):
                        act.wait_ge(att_done.sem, att_done.before(j, 1))
                bk = (bD, bE)[n % 2][:].rearrange("p (s c) -> p s c", s=2)
                t = slice(2 * n, 2 * n + 2)
                a.activation(qk[:, t, :], bk[:, :, 0:160], ACT.Copy).then_inc(qkv_done.sem, 1)
                a.activation(vx[:, t, :].rearrange("p s (r c) -> p s r c", r=REP),
                             bk[:, :, 160:QKV].unsqueeze(2).to_broadcast([P, 2, REP, NKV * HD]), ACT.Copy).then_inc(qkv_done.sem, 1)

            def exp_scores(j):
                act.wait_ge(shift_done.sem, shift_done.at(j, 1))
                a.activation(probs[:], probs[:], ACT.Exp, scale=float(HD) ** -0.5).then_inc(exp_done.sem, 1)

            def evac_att(j, q):
                act.wait_ge(attT_ps.sem, attT_ps.at(j, q + 1))
                if has_earlier(j):
                    act.wait_ge(proj_ps.sem, proj_ps.before(j, 2))
                a.activation(attT[:, q, :], (bD, bE)[q][:], ACT.Copy).then_inc(attT_done.sem, 1)

            def evac_l2(j, q):
                act.wait_ge(l2_ps.sem, l2_ps.at(j, q + 1))
                if has_earlier(j):
                    act.wait_ge(h_ps.sem, h_ps.before(j, NF * GROUPS))
                a.activation(l2T[:, q, :], (bD, bE)[q][:], ACT.Identity, bias=vec("l2b"), scale=vec("l2w")).then_inc(l2T_done.sem, 1)

            def exp_gates(j):
                act.wait_ge(lshift.sem, lshift.at(j, 1))
                a.activation(rt[:, 0], rt[:, 0], ACT.Exp).then_inc(gexp.sem, 1)

            def gelu_experts(k, g):
                for f in range(NF):
                    act.wait_ge(h_ps.sem, h_ps.at(k, NF * g + f + 1))
                    if g >= 2:
                        act.wait_ge(moe_ps.sem, moe_ps.at(k, g - 1))
                    else:
                        if has_earlier(k):
                            act.wait_ge(moe_ps.sem, moe_ps.before(k, GROUPS - 1 + g))
                    a.activation(hT[:, g % 2, f, :], (bF, bG)[f][:], ACT.Gelu_apprx_tanh).then_inc(hT_done.sem, 1)

            def iteration(i, do_mixer, do_attn, do_moe):
                b, j, k = i + 1, i, i - 1

                def experts(*gs):
                    if do_moe:
                        for g in gs:
                            gelu_experts(k, g)

                if do_mixer:
                    evac_xT(b, 0)
                    evac_xT(b, 1)
                if do_attn:
                    evac_ln(j, 0)
                    evac_ln(j, 1)
                experts(0)
                if do_attn:
                    evac_qkv(j, 0)
                    evac_qkv(j, 1)
                experts(1)
                if do_attn:
                    evac_qkv(j, 2)
                    evac_qkv(j, 3)
                experts(2, 3, 4, 5)
                if do_mixer:
                    evac_out(b, 0)
                    evac_out(b, 1)
                experts(6)
                if do_mixer:
                    gelu_mixer(b, 0)
                    gelu_mixer(b, 1)
                experts(7)
                if do_attn:
                    exp_scores(j)
                experts(8, 9, 10)
                if do_attn:
                    evac_att(j, 0)
                    evac_att(j, 1)
                experts(11, 12, 13, 14, 15)
                if do_attn:
                    evac_l2(j, 0)
                    evac_l2(j, 1)
                    exp_gates(j)

            pipeline(act, iteration)

        @block.tensor
        def _(pe):
            t = nc.tensor
            idn = ident[:]

            pe.wait_ge(w_loaded, W_ALL)
            pe.wait_ge(setup_pool, 2)
            t.transpose(bF[:, 0:14], vec_rows[:], ident[0:14, 0:14]).then_inc(setup_pe, 1)
            pe.wait_ge(setup_dve, 1)
            t.matmul(bE[:, 0:2 * D], ones_row[:], rowv[:].rearrange("p a d -> p (a d)"), start=True, stop=True)
            t.transpose(bD[:, 0:P], qkv_rows[:, 0, :], idn)
            t.transpose(bD[:, P:QKV], qkv_rows[0:QKV - P, 1, :], ident[0:QKV - P, 0:QKV - P])
            t.transpose(bD[:, 256:384], proj_perm[:], idn)
            t.transpose(bD[:, 384:384 + NE], router_rows[:], ident[0:NE, 0:NE]).then_inc(setup_pe, 1)

            def transposes(bk, src, q):
                for n in tiles(q):
                    last = t.transpose(bk[:, cols(n)], src[:, n, :], idn)
                return last

            def transpose_x(b, q):
                if q == 0:
                    pe.wait_ge(x_loaded.sem, x_loaded.at(b, 16))
                    if has_earlier(b):
                        pe.wait_ge(gT_done.sem, gT_done.before(b, 2))
                else:
                    pe.wait_ge(xT_done.sem, xT_done.at(b, 1))
                transposes(bA, x_in, q).then_inc(xT_ps.sem, 1)

            def project_in(b, q):
                pe.wait_ge(xT_done.sem, xT_done.at(b, q + 1))
                if q == 0:
                    if has_earlier(b):
                        pe.wait_ge(centred.sem, centred.before(b, 2))
                else:
                    pe.wait_ge(rot_done.sem, rot_done.at(b, 1))
                t.matmul(bB[:], win[:, 0, :], xT[:, q, :], start=True, stop=True)
                t.matmul(bC[:], win[:, 1, :], xT[:, q, :], start=True, stop=True).then_inc(u_ps.sem, 1)

            def mix(b, q):
                bk = (bA, bB)[q]
                if q == 0:
                    pe.wait_ge(xT_done.sem, xT_done.at(b, 2))
                else:
                    pe.wait_ge(rot_done.sem, rot_done.at(b, 2))
                t.matmul(bk[:], win[:, 2, :], xT[:, q, :], start=True, stop=False)
                pe.wait_ge(hid_done.sem, hid_done.at(b, 2 * q + 2))
                for n in range(2):
                    last = t.matmul(bk[:], wmid[:, n, :], hid[:, n, HALF * q:HALF * q + HALF, :].rearrange("p s t -> p (s t)"),
                                    start=False, stop=(n == 1))
                last.then_inc(out_ps.sem, 1)

            def mlp_in(b, q):
                pe.wait_ge(outT_done.sem, outT_done.at(b, 2 * q + 1))
                t.matmul((bC, bA)[q][:], w1[:], outT[:, q, :], start=True, stop=True).then_inc(z_ps.sem, 1)

            def mlp_out(b, q):
                pe.wait_ge(outT_done.sem, outT_done.at(b, 4))
                pe.wait_ge(gT_done.sem, gT_done.at(b, q + 1))
                bk = (bB, bC)[q]
                for n in tiles(q):
                    t.matmul(bk[:, cols(n)], gT[:, q, cols(n)], w2[:], start=True, stop=False)
                    last = t.matmul(bk[:, cols(n)], outT2[:, q, cols(n)], idn, start=False, stop=True)
                last.then_inc(y_ps.sem, 1)

            def transpose_xh(j, q):
                if q == 0:
                    pe.wait_ge(xh_done.sem, xh_done.at(j, 1))
                    if has_earlier(j):
                        pe.wait_ge(gates_done.sem, gates_done.before(j, 1))
                else:
                    if has_earlier(j):
                        pe.wait_ge(l2T_done.sem, l2T_done.before(j, 2))
                transposes((bD, bE)[q], xh, q).then_inc(xhT_ps.sem, 1)

            def project_qkv(j, n):
                if n < 2:
                    pe.wait_ge(lnT_done.sem, lnT_done.at(j, 2))
                else:
                    pe.wait_ge(qkv_done.sem, qkv_done.at(j, 2 * n - 2))
                bk = (bD, bE)[n % 2]
                for m in range(2):
                    s = 2 * n + m
                    last = t.matmul(bk[:, 256 * m:256 * m + QKV], lnT[:, s // HALF, cols(s)], qkvT[:], start=True, stop=True)
                last.then_inc(qkv_ps.sem, 1)

            def transpose_att(j, q):
                pe.wait_ge(att_done.sem, att_done.at(j, 1))
                pe.wait_ge(qkv_done.sem, qkv_done.at(j, 8))
                transposes((bD, bE)[q], att, q).then_inc(attT_ps.sem, 1)

            def project_att(j, q):
                pe.wait_ge(attT_done.sem, attT_done.at(j, q + 1))
                bk = (bD, bE)[q]
                for n in tiles(q):
                    last = t.matmul(bk[:, cols(n)], attT[:, q, cols(n)], projT[:], start=True, stop=True)
                last.then_inc(proj_ps.sem, 1)

            def transpose_xh2(j, q):
                pe.wait_ge(xh2_done.sem, xh2_done.at(j, 1))
                pe.wait_ge(h2_done.sem, h2_done.at(j, q + 1))
                transposes((bD, bE)[q], xh2, q).then_inc(l2_ps.sem, 1)

            def route(j):
                pe.wait_ge(l2T_done.sem, l2T_done.at(j, 2))
                for n in range(NS):
                    last = t.matmul(bD[:, NE * n:NE * n + NE], l2T[:, n // HALF, cols(n)], routerT[:], start=True, stop=True)
                last.then_inc(logit_ps.sem, 1)

            def experts_in(k, g):
                q, e = divmod(g, NE)
                pe.wait_ge(l2T_done.sem, l2T_done.at(k, 2))
                for f in range(NF):
                    if g:
                        pe.wait_ge(hT_done.sem, hT_done.at(k, NF * (g - 1) + f + 1))
                    else:
                        if has_earlier(k):
                            pe.wait_ge(hT_done.sem, hT_done.before(k, NF * (GROUPS - 1) + f + 1))
                    t.matmul((bF, bG)[f][:], ew1[:, e, 128 * f:128 * f + 128], l2T[:, q, :], start=True,
                             stop=True).then_inc(h_ps.sem, 1)

            def experts_out(k, g):
                q, e = divmod(g, NE)
                pe.wait_ge(hT_done.sem, hT_done.at(k, NF * (g + 1)))
                if g:
                    pe.wait_ge(acc_done.sem, acc_done.at(k, g))
                else:
                    if has_earlier(k):
                        pe.wait_ge(acc_done.sem, acc_done.before(k, GROUPS))
                for n in tiles(q):
                    for f in range(NF):
                        last = t.matmul(bH[:, cols(n)], hT[:, g % 2, f, cols(n)], ew2[:, e, f, :], start=(f == 0),
                                        stop=(f == NF - 1))
                last.then_inc(moe_ps.sem, 1)

            def iteration(i, do_mixer, do_attn, do_moe):
                b, j, k = i + 1, i, i - 1

                def experts(*gs):
                    if do_moe:
                        for g in gs:
                            if g < GROUPS:
                                experts_in(k, g)
                            if g:
                                experts_out(k, g - 1)

                if do_mixer:
                    transpose_x(b, 0)
                    transpose_x(b, 1)
                if do_attn:
                    transpose_xh(j, 0)
                    transpose_xh(j, 1)
                experts(0)
                if do_mixer:
                    project_in(b, 0)
                if do_attn:
                    project_qkv(j, 0)
                    project_qkv(j, 1)
                experts(1)
                if do_mixer:
                    project_in(b, 1)
                if do_attn:
                    project_qkv(j, 2)
                    project_qkv(j, 3)
                experts(2, 3, 4, 5)
                if do_mixer:
                    mix(b, 0)
                    mix(b, 1)
                experts(6)
                if do_mixer:
                    mlp_in(b, 0)
                    mlp_in(b, 1)
                experts(7)
                if do_mixer:
                    mlp_out(b, 0)
                    mlp_out(b, 1)
                experts(8, 9, 10)
                if do_attn:
                    transpose_att(j, 0)
                    transpose_att(j, 1)
                experts(11)
                if do_attn:
                    project_att(j, 0)
                    project_att(j, 1)
                experts(12, 13, 14, 15, 16)
                if do_attn:
                    transpose_xh2(j, 0)
                    transpose_xh2(j, 1)
                    route(j)

            pipeline(pe, iteration)


_INS = ["L0_attn_x", "L0_attn_W_in", "L0_attn_b_in", "L0_attn_params_log", "L0_attn_W_mid", "L0_attn_b_mid",
        "L0_attn_w1_w", "L0_attn_w1_b", "L0_attn_w2_w", "L0_attn_w2_b", "L0_attn_ln_g", "L0_attn_ln_b",
        "L0_ffn_ln1_weight", "L0_ffn_ln1_bias", "L0_ffn_ln2_weight", "L0_ffn_ln2_bias", "L0_ffn_qkv_weight",
        "L0_ffn_proj_weight", "L0_ffn_router_weight", "L0_ffn_moe_w1", "L0_ffn_moe_w2"]


def kernel(**inputs):
    import numpy as _np
    import concourse.bacc as _bacc
    from concourse.bass_utils import run_bass_kernel_spmd as _run

    nc = _bacc.Bacc("TRN2", target_bir_lowering=False, num_devices=1)
    arrays, args = {}, []
    for name in _INS:
        a = _np.ascontiguousarray(inputs[name])
        arrays[name] = a
        args.append(nc.dram_tensor(name, a.shape, F32, kind="ExternalInput").ap())
    args.append(nc.dram_tensor("out", arrays["L0_attn_x"].shape, F32, kind="ExternalOutput").ap())
    build(nc, *args)
    return _run(nc, [arrays], core_ids=[0]).results[0]["out"]
```

```python
import math
from contextlib import ExitStack

import concourse.bass as bass
from concourse import mybir

F32 = mybir.dt.float32
F32R = mybir.dt.float32r
ALU = mybir.AluOpType
ACT = mybir.ActivationFunctionType
AX = mybir.AxisListType

P = 128
D = 128
HALF = 4
EPS = 1e-5
TWO_PI_HI = 6.28125
TWO_PI_MID = 0.0019350051879882812
TWO_PI_LO = 3.019915981956752e-07
LN2_HI = 0.693359375
LN2_LO = -2.12194440e-4
SPLIT = 4097.0
ROUND = 12582912.0
MASKED = -3.4028234663852886e38
NKV, REP, HD = 4, 4, 8
NH = NKV * REP


class Signal:

    def __init__(self, sem, per_block):
        self.sem, self.per_block = sem, per_block

    def at(self, block, k):
        return self.per_block * block + k

    def before(self, block, k):
        return self.per_block * block - self.per_block + k


def has_earlier(block):
    return not (isinstance(block, int) and block == 0)


def build(nc, x, W_in, b_in, plog, W_mid, b_mid, w1_w, w1_b, w2_w, w2_b, ln_g, ln_b,
          ln1_w, ln1_b, ln2_w, ln2_b, qkv_w, proj_w, router_w, moe_w1, moe_w2, out):
    NS, T, _ = x.shape
    NB = T // P
    NE, _, FF = moe_w1.shape
    NF = FF // 128
    QKV = qkv_w.shape[0]
    GROUPS = 2 * NE
    ACT_E = 2
    row_of = [s * (s + 1) // 2 for s in range(NS + 1)]
    assert NS == 2 * HALF and NF == 2 and QKV == (NH + 2 * NKV) * HD
    POOL_S = range(0, 4)
    DVE_S = range(4, NS)

    with ExitStack() as ctx:
        def sb(name, *shape, dtype=F32):
            return ctx.enter_context(nc.sbuf_tensor(name, list(shape), dtype))

        def sem(name):
            return ctx.enter_context(nc.semaphore(name))

        def signal(name, per_block):
            return Signal(sem(name), per_block)

        win = sb("win", P, 3, D)
        wmid = sb("wmid", P, 2, D)
        w1 = sb("w1", P, D)
        w2 = sb("w2", P, D)
        qkvT = sb("qkvT", P, QKV)
        projT = sb("projT", P, D)
        proj_perm = sb("proj_perm", P, D)
        router_rows = sb("router_rows", NE, D)
        routerT = sb("routerT", P, NE)
        ew1_high = sb("ew1_high", P, NE, FF, dtype=F32R)
        ew1_low = sb("ew1_low", P, NE, FF, dtype=F32R)
        ew2 = sb("ew2", P, NE, NF, D)
        ident = sb("ident", P, P)
        vecs = sb("vecs", P, 18)
        vec_rows = sb("vec_rows", 14, D)
        rowv = sb("rowv", 1, 2, D)
        ones_row = sb("ones_row", 1, P)
        gb = sb("gb", P, 2, D)
        lam = sb("lam", P, 16)
        etmp = sb("etmp", P, 3, 4)
        power = sb("power", P, 4, dtype=mybir.dt.int32)
        basis = sb("basis", P, 8, 2)
        phase = sb("phase", P, 2, P)
        gphase = sb("gphase", P, 2, P)
        ptmp = sb("ptmp", P, 2, 64)
        decay = sb("decay", P, NS, P)
        minus_half = sb("minus_half", P, NS)
        rank8 = sb("rank8", P, NS, NE)

        VEC = dict(l2wS=16, l2bS=17, b0=0, b1=1, b2=2, m0=3, m1=4, w1b=5, w2b=6, l1w=7, l1b=8, l2w=9, l2b=10,
                   nu=11, theta=12, gamma=13, bo=14, bo2=15)

        def vec(name):
            return vecs[:, VEC[name]:VEC[name] + 1]

        x_in = sb("x_in", P, NS, D)
        xb = sb("xb", P, NS, D)
        xT = sb("xT", P, 2, HALF * P)
        rot = sb("rot", P, 4, HALF * P)
        drive = sb("drive", P, 2, NS, P)
        state = drive
        init = sb("init", P, 2, NS)
        ctmp = sb("ctmp", P, 2, NS)
        post = sb("post", P, 4, NS, P)
        outT = sb("outT", P, 2, HALF * P)
        outT2 = sb("outT2", P, 2, HALF * P)
        gT = sb("gT", P, 2, HALF * P)
        z = sb("z", P, NS, D)
        stA = sb("stA", P, NS, 6)
        mvA = sb("mvA", P, 3, NS)
        rsA = sb("rsA", P, 2, NS)
        stB = sb("stB", P, NS, 6)
        mvB = sb("mvB", P, 4, NS)
        rsB = sb("rsB", P, 2, 2, NS)
        x1 = sb("x1", P, NS, D)
        xh = sb("xh", P, NS, D)
        lnT = sb("lnT", P, 2, HALF * P)
        qk = sb("qk", P, NS, 160)
        vx = sb("vx", P, NS, NH * HD)
        prod = sb("prod", P, row_of[NS], NH * HD)
        scores = sb("scores", P, NS, NS, NH)
        probs = sb("probs", P, NS, NS, NH)
        smax = sb("smax", P, NS, NH)
        ssum = sb("ssum", P, NS, NH)
        srec = sb("srec", P, NS, NH)
        att = sb("att", P, NS, NH * HD)
        attT = sb("attT", P, 2, HALF * P)
        tmpS = sb("tmpS", P, 5, NS)
        h2 = sb("h2", P, NS, D)
        stC = sb("stC", P, NS, 6)
        mvC = sb("mvC", P, 3, NS)
        rsC = sb("rsC", P, 2, NS)
        xh2 = sb("xh2", P, NS, D)
        l2T = sb("l2T", P, 2, HALF * P)
        l2_scaled = sb("l2_scaled", P, HALF * P)
        l2_diff = sb("l2_diff", P, HALF * P)
        l2_high = sb("l2_high", P, 2, HALF * P, dtype=F32R)
        l2_low = sb("l2_low", P, 2, HALF * P, dtype=F32R)
        rt = sb("rt", P, 6, NS, NE)
        rt1 = sb("rt1", P, 6, NS)
        gates = sb("gates", P, NS, NE)
        base = sb("base", P, NS, D)
        weighed = sb("weighed", P, HALF * P)
        res = sb("res", P, NS, D)
        hT = sb("hT", P, 2, NF, HALF * P)
        stD = sb("stD", P, NS, 6)
        mvD = sb("mvD", P, 3, NS)
        rsD = sb("rsD", P, 2, NS)

        bank = [ctx.enter_context(nc.psum_tensor(f"bank{i}", [P, 512], F32)) for i in range(8)]
        bA, bB, bC, bD, bE, bF, bG, bH = bank

        ew1_diff = post[:].rearrange("p n s t -> p (n s t)")[:, 0:NE * FF].rearrange("p (e f) -> p e f", e=NE)
        qkv_rows, proj_rows = prod[:, 32:34, :], prod[:, 34, :]
        ew1 = prod[:].rearrange("p a c -> p (a c)")[:, 0:NE * FF].rearrange("p (e f) -> p e f", e=NE)
        ew1_scaled = prod[:].rearrange("p a c -> p (a c)")[:, NE * FF:2 * NE * FF].rearrange("p (e f) -> p e f", e=NE)

        group_bank = [bH] * GROUPS
        for g in (3, 5, 7):
            group_bank[g] = bE
        group_bank[9] = bA
        for g in (11, 13, 15):
            group_bank[g] = bC

        def earlier_in_bank(g):
            return max((n for n in range(g) if group_bank[n] is group_bank[g]), default=None)

        vec_loaded = sem("vec_loaded")
        w_loaded = sem("w_loaded")
        ew1_loaded = sem("ew1_loaded")
        late_loaded = sem("late_loaded")
        ew1_split = sem("ew1_split")
        setup_pool = sem("setup_pool")
        setup_dve = sem("setup_dve")
        setup_act = sem("setup_act")
        chain = sem("chain")
        setup_pe = sem("setup_pe")
        x_loaded = signal("x_loaded", 16)
        xb_done = signal("xb_done", 1)
        xT_ps = signal("xT_ps", 2)
        xT_done = signal("xT_done", 2)
        u_ps = signal("u_ps", 2)
        rot_done = signal("rot_done", 2)
        drive_done = signal("drive_done", 4)
        inject_done = signal("inject_done", 1)
        scan_done = signal("scan_done", 2)
        carry_mul = signal("carry_mul", 2)
        carry_done = signal("carry_done", 2)
        post_done = signal("post_done", 2)
        hid_done = signal("hid_done", 4)
        out_ps = signal("out_ps", 2)
        outT_done = signal("outT_done", 4)
        z_ps = signal("z_ps", 2)
        gT_done = signal("gT_done", 2)
        y_ps = signal("y_ps", 2)
        statA = signal("statA", 2)
        partA = signal("partA", 8)
        spreadA = signal("spreadA", 4)
        meanA = signal("meanA", 2)
        rstdA = signal("rstdA", 2)
        centred = signal("centred", 2)
        z_done = signal("z_done", 2)
        statB = signal("statB", 1)
        partB = signal("partB", 4)
        spreadB = signal("spreadB", 2)
        meanB = signal("meanB", 1)
        rstdB = signal("rstdB", 2)
        shiftB = signal("shiftB", 2)
        x1_done = signal("x1_done", 2)
        xh_done = signal("xh_done", 2)
        xhT_ps = signal("xhT_ps", 2)
        lnT_done = signal("lnT_done", 2)
        qkv_ps = signal("qkv_ps", 4)
        qkv_done = signal("qkv_done", 8)
        qk_pool = signal("qk_pool", len(POOL_S))
        qk_dve = signal("qk_dve", NS - len(POOL_S))
        scores_done = signal("scores_done", NS)
        smax_done = signal("smax_done", 1)
        shift_done = signal("shift_done", 1)
        exp_done = signal("exp_done", 1)
        ssum_done = signal("ssum_done", 1)
        srec_done = signal("srec_done", 1)
        probs_done = signal("probs_done", 1)
        pv_pool = signal("pv_pool", len(POOL_S))
        pv_dve = signal("pv_dve", NS - len(POOL_S))
        att_done = signal("att_done", NS)
        attT_ps = signal("attT_ps", 2)
        attT_done = signal("attT_done", 2)
        proj_ps = signal("proj_ps", 2)
        h2_done = signal("h2_done", 2)
        statC = signal("statC", 1)
        partC = signal("partC", 4)
        spreadC = signal("spreadC", 2)
        meanC = signal("meanC", 1)
        rstdC = signal("rstdC", 1)
        shiftC = signal("shiftC", 1)
        xh2_done = signal("xh2_done", 2)
        l2_ps = signal("l2_ps", 2)
        l2T_done = signal("l2T_done", 2)
        l2S_done = signal("l2S_done", 2)
        l2_diff_done = signal("l2_diff_done", 2)
        l2_high_done = signal("l2_high_done", 2)
        l2_low_done = signal("l2_low_done", 2)
        logit_ps = signal("logit_ps", 1)
        gstep = signal("gstep", 13)
        top_done = signal("top_done", 1)
        lshift = signal("lshift", 1)
        gexp = signal("gexp", 1)
        two_done = signal("two_done", 1)
        both_done = signal("both_done", 1)
        gates_done = signal("gates_done", 1)
        base_done = signal("base_done", 1)
        weighed_done = signal("weighed_done", 2 * ACT_E)
        added = signal("added", 2 * ACT_E)
        h_ps = signal("h_ps", NF * GROUPS)
        hT_done = signal("hT_done", NF * GROUPS)
        moe_ps = signal("moe_ps", GROUPS)
        acc_done = signal("acc_done", 2 * (NE - ACT_E))
        statD = signal("statD", 2)
        partD = signal("partD", 8)
        spreadD = signal("spreadD", 4)
        meanD = signal("meanD", 2)
        rstdD = signal("rstdD", 2)
        shiftD = signal("shiftD", 2)
        y_done = signal("y_done", 2)
        stored = [signal(f"stored{q}", 16) for q in range(2)]

        block = ctx.enter_context(nc.Block())

        def runs(blk):
            return not isinstance(blk, int) or 0 <= blk < NB

        def pipeline(eng, iteration):
            for i in range(-2, 2):
                iteration(i)
            with eng.Fori(2, NB - 2) as i:
                iteration(i)
            for i in range(NB - 2, NB + 1):
                iteration(i)

        def tiles(q):
            return range(HALF * q, HALF * q + HALF)

        def cols(n):
            return slice(n % HALF * P, n % HALF * P + P)

        def over_tiles(table, n):
            return table.unsqueeze(1).to_broadcast([P, n, P])

        SETUP_GB = 2
        VEC_ALL = 16 * 9
        W_ALL = 16 * 10
        LATE_ALL = 16 * 2

        def qk_product(g, s):
            n = s + 1
            o = prod[:, row_of[s]:row_of[s + 1], :].rearrange("p t (r c) -> p t r c", r=REP)
            q = qk[:, s, 0:NH * HD].rearrange("p (r c) -> p r c", r=REP).unsqueeze(1).to_broadcast([P, n, REP, NKV * HD])
            kk = qk[:, 0:n, NH * HD:160].unsqueeze(2).to_broadcast([P, n, REP, NKV * HD])
            return g.tensor_tensor(o, q, kk, ALU.mult)

        def pv_product(g, s):
            n = s + 1
            o = prod[:, row_of[s]:row_of[s + 1], :].rearrange("p t (h d) -> p (t h) d", d=HD)
            pr = probs[:, s, 0:n, :].rearrange("p t h -> p (t h)").unsqueeze(2).to_broadcast([P, n * NH, HD])
            v = vx[:, 0:n, :].rearrange("p t (h d) -> p (t h) d", d=HD)
            return g.tensor_tensor(o, pr, v, ALU.mult)


        @block.sync
        def _(sp):
            def load_x(b):
                if has_earlier(b):
                    sp.wait_ge(xT_ps.sem, xT_ps.before(b, 2))
                if has_earlier(b):
                    sp.wait_ge(xb_done.sem, xb_done.before(b, 1))
                sp.dma_start(x_in[:], x[:, bass.ts(b, P), :].rearrange("s p d -> p s d")).then_inc(x_loaded.sem, 16)

            def store(k, q):
                sp.wait_ge(y_done.sem, y_done.at(k, q + 1))
                sp.dma_start(out[HALF * q:HALF * q + HALF, bass.ts(k, P), :].rearrange("s p d -> p s d"),
                             res[:, HALF * q:HALF * q + HALF, :]).then_inc(stored[q].sem, 16)

            for n, src in (("nu", plog), ("b0", b_in), ("m0", b_mid)):
                sp.dma_start(vec_rows[VEC[n]:VEC[n] + src.shape[0], :], src).then_inc(vec_loaded, 16)
            for n, src in (("w1b", w1_b), ("w2b", w2_b), ("l1w", ln1_w), ("l1b", ln1_b), ("l2w", ln2_w), ("l2b", ln2_b)):
                sp.dma_start(vec_rows[VEC[n]:VEC[n] + 1, :], src.rearrange("(a d) -> a d", a=1)).then_inc(vec_loaded, 16)
            load_x(0)
            for dst, src in (
                (win[:], W_in.rearrange("e d h -> d e h")),
                (wmid[:], W_mid.rearrange("e d h -> d e h")),
                (w1[:], w1_w), (w2[:], w2_w),
                (qkv_rows[:, 0, :], qkv_w[0:P, :]), (qkv_rows[0:QKV - P, 1, :], qkv_w[P:QKV, :]),
                (proj_rows, proj_w), (router_rows[:], router_w),
                (rowv[:, 0, :], ln_g.rearrange("(a d) -> a d", a=1)), (rowv[:, 1, :], ln_b.rearrange("(a d) -> a d", a=1)),
            ):
                sp.dma_start(dst, src).then_inc(w_loaded, 16)
            sp.dma_start(ew1, moe_w1.rearrange("e d f -> d e f")).then_inc(ew1_loaded, 16)
            for dst, src in (
                (ew2[:, 0:NE // 2], moe_w2[0:NE // 2].rearrange("e (g f) d -> f e g d", g=NF)),
                (ew2[:, NE // 2:NE], moe_w2[NE // 2:NE].rearrange("e (g f) d -> f e g d", g=NF)),
            ):
                sp.dma_start(dst, src).then_inc(late_loaded, 16)

            load_x(1)
            load_x(2)
            load_x(3)
            store(0, 0)
            store(0, 1)
            with sp.Fori(1, NB - 3) as k:
                load_x(k + 3)
                store(k, 0)
                store(k, 1)
            with sp.Fori(NB - 3, NB) as k:
                store(k, 0)
                store(k, 1)
            for q in range(2):
                sp.wait_ge(stored[q].sem, stored[q].at(NB, 0))

        @block.gpsimd
        def _(pool):
            g = nc.gpsimd
            g.memset(ident[:], 0.0).then_inc(setup_pool, 1)
            g.memset(ones_row[:], 1.0)
            g.memset(minus_half[:], -0.5)
            g.memset(init[:], 0.0)
            g.memset(scores[:], MASKED)
            for e in range(NE):
                g.memset(rank8[:, :, e:e + 1], float(NE - e))
            pool.wait_ge(setup_pool, 1)
            g.affine_select(out=ident[:], in_=ident[:], compare_op=ALU.not_equal, fill=1.0, base=0,
                            pattern=[[-1, P]], channel_multiplier=1).then_inc(setup_pool, 1)

            def sum_xb(b):
                pool.wait_ge(x_loaded.sem, x_loaded.at(b, 16))
                if has_earlier(b):
                    pool.wait_ge(z_done.sem, z_done.before(b, 2))
                if isinstance(b, int) and b == 0:
                    pool.wait_ge(setup_act, SETUP_GB)
                g.tensor_tensor(xb[:], x_in[:], over_tiles(gb[:, 1, :], NS), ALU.add).then_inc(xb_done.sem, 1)

            def sum_drive(b, q):
                pool.wait_ge(rot_done.sem, rot_done.at(b, q + 1))
                if has_earlier(b):
                    pool.wait_ge(carry_done.sem, carry_done.before(b, 2))
                    pool.wait_ge(post_done.sem, post_done.before(b, 2))
                t = slice(HALF * q, HALF * q + HALF)
                r = [rot[:, n, :].rearrange("p (s t) -> p s t", t=P) for n in range(4)]
                g.tensor_tensor(drive[:, 0, t, :], r[0], r[1], ALU.add).then_inc(drive_done.sem, 1)
                g.tensor_tensor(drive[:, 1, t, :], r[2], r[3], ALU.subtract).then_inc(drive_done.sem, 1)

            def sum_hid(b, q):
                pool.wait_ge(post_done.sem, post_done.at(b, q + 1))
                t = slice(HALF * q, HALF * q + HALF)
                g.tensor_tensor(post[:, 0, t, :], post[:, 0, t, :], post[:, 1, t, :], ALU.subtract).then_inc(hid_done.sem, 1)
                g.tensor_tensor(post[:, 2, t, :], post[:, 2, t, :], post[:, 3, t, :], ALU.add).then_inc(hid_done.sem, 1)

            def rstd(mean_sig, rstd_sig, mv, rs, blk, k, t):
                pool.wait_ge(mean_sig.sem, mean_sig.at(blk, k))
                g.tensor_tensor(rs[:, 0, t], mv[:, 2, t], minus_half[:, t], ALU.pow).then_inc(rstd_sig.sem, 1)

            def shift(rstd_sig, shift_sig, mv, rs, blk, k, t):
                pool.wait_ge(rstd_sig.sem, rstd_sig.at(blk, k))
                g.tensor_tensor(rs[:, 1, t], mv[:, 0, t], rs[:, 0, t], ALU.mult).then_inc(shift_sig.sem, 1)

            def rstd_b(b, n):
                pool.wait_ge(meanB.sem, meanB.at(b, 1))
                g.tensor_tensor(rsB[:, 0, n], mvB[:, 2 + n, :], minus_half[:], ALU.pow).then_inc(rstdB.sem, 1)

            def shift_b(b, n):
                pool.wait_ge(rstdB.sem, rstdB.at(b, 2 - n))
                g.tensor_tensor(rsB[:, 1, n], rsB[:, 0, n], mvB[:, 0, :], ALU.mult).then_inc(shiftB.sem, 1)

            def qk_products(j):
                pool.wait_ge(qkv_done.sem, qkv_done.at(j, 8))
                if has_earlier(j):
                    pool.wait_ge(att_done.sem, att_done.before(j, NS))
                for s in POOL_S:
                    qk_product(g, s).then_inc(qk_pool.sem, 1)

            def pv_products(j):
                pool.wait_ge(probs_done.sem, probs_done.at(j, 1))
                pool.wait_ge(scores_done.sem, scores_done.at(j, NS))
                for s in POOL_S:
                    pv_product(g, s).then_inc(pv_pool.sem, 1)

            def sum_base(j):
                pool.wait_ge(h2_done.sem, h2_done.at(j, 2))
                pool.wait_ge(x1_done.sem, x1_done.at(j, 2))
                if has_earlier(j):
                    pool.wait_ge(acc_done.sem, acc_done.before(j, NE - ACT_E + 1))
                g.tensor_tensor(base[:], x1[:], h2[:], ALU.add).then_inc(base_done.sem, 1)

            def add_weighed(k, n):
                q, e = divmod(n, ACT_E)
                pool.wait_ge(weighed_done.sem, weighed_done.at(k, n + 1))
                if e:
                    pool.wait_ge(added.sem, added.at(k, n))
                else:
                    pool.wait_ge(base_done.sem, base_done.at(k, 1))
                half = base[:, HALF * q:HALF * q + HALF, :].rearrange("p s d -> p (s d)")
                g.tensor_tensor(half, half, weighed[:], ALU.add).then_inc(added.sem, 1)

            def iteration(i):
                if runs(i + 1):
                    sum_drive(i + 1, 0)
                    sum_xb(i + 1)
                    sum_drive(i + 1, 1)
                if runs(i - 1):
                    add_weighed(i - 1, 0)
                    add_weighed(i - 1, 1)
                if runs(i + 1):
                    sum_hid(i + 1, 0)
                    sum_hid(i + 1, 1)
                if runs(i):
                    qk_products(i)
                    pv_products(i)
                if runs(i + 1):
                    rstd(meanA, rstdA, mvA, rsA, i + 1, 1, slice(0, HALF))
                if runs(i - 1):
                    add_weighed(i - 1, 2)
                    rstd(meanD, rstdD, mvD, rsD, i - 1, 1, slice(0, HALF))
                if runs(i + 1):
                    rstd(meanA, rstdA, mvA, rsA, i + 1, 2, slice(HALF, NS))
                if runs(i - 1):
                    add_weighed(i - 1, 3)
                    shift(rstdD, shiftD, mvD, rsD, i - 1, 1, slice(0, HALF))
                if runs(i + 1):
                    rstd_b(i + 1, 1)
                    shift_b(i + 1, 1)
                    rstd_b(i + 1, 0)
                    shift_b(i + 1, 0)
                if runs(i):
                    rstd(meanC, rstdC, mvC, rsC, i, 1, slice(0, NS))
                    sum_base(i)
                    shift(rstdC, shiftC, mvC, rsC, i, 1, slice(0, NS))
                if runs(i - 1):
                    rstd(meanD, rstdD, mvD, rsD, i - 1, 2, slice(HALF, NS))
                    shift(rstdD, shiftD, mvD, rsD, i - 1, 2, slice(HALF, NS))

            pool.wait_ge(ew1_split, 1)
            g.tensor_tensor(ew1_diff, ew1_scaled, ew1, ALU.subtract).then_inc(ew1_split, 1)
            pool.wait_ge(ew1_split, 2)
            g.tensor_tensor(ew1_high[:], ew1_scaled, ew1_diff, ALU.subtract).then_inc(ew1_split, 1)
            pool.wait_ge(ew1_split, 3)
            g.tensor_tensor(ew1_low[:], ew1, ew1_high[:].bitcast(F32), ALU.subtract).then_inc(ew1_split, 1)

            pipeline(pool, iteration)

        @block.vector
        def _(dve):
            v = nc.vector
            steps = [0]

            def link(ins):
                ins.then_inc(chain, 1)
                steps[0] += 1
                dve.wait_ge(chain, steps[0])

            def links(*ins):
                for one in ins[:-1]:
                    one()
                link(ins[-1]())

            dve.wait_ge(setup_pe, 1)
            link(v.tensor_copy(vecs[:, 0:14], bF[:, 0:14]))
            link(v.tensor_tensor(vec("bo"), vec("m0"), vec("m1"), ALU.subtract))
            link(v.tensor_tensor(vec("bo"), vec("bo"), vec("b2"), ALU.add))
            v.tensor_scalar(vecs[:, 16:18], vecs[:, VEC["l2w"]:VEC["l2b"] + 1], SPLIT, None, ALU.mult)
            v.tensor_tensor(vec("bo2"), vec("bo"), vec("w2b"), ALU.add).then_inc(setup_dve, 1)

            def exp_steps(dst, src, n, tmp):
                arg, turns, series = (etmp[:, m, tmp:tmp + n] for m in range(3))
                bits = power[:, tmp:tmp + n]
                yield lambda: v.tensor_scalar(arg, src, 88.0, -86.0, ALU.min, ALU.max)
                yield lambda: v.tensor_scalar(turns, arg, 1.4426950408889634, None, ALU.mult)
                yield lambda: v.tensor_scalar(turns, turns, ROUND, None, ALU.add)
                yield lambda: v.tensor_scalar(turns, turns, ROUND, None, ALU.subtract)
                yield lambda: v.scalar_tensor_tensor(arg, turns, -LN2_HI, arg, ALU.mult, ALU.add)
                yield lambda: v.scalar_tensor_tensor(arg, turns, -LN2_LO, arg, ALU.mult, ALU.add)
                yield lambda: v.tensor_scalar(series, arg, 1.0 / math.factorial(7), None, ALU.mult)
                for m in range(6, 0, -1):
                    yield lambda m=m: v.scalar_tensor_tensor(series, series, 1.0 / math.factorial(m), arg, ALU.add, ALU.mult)
                yield lambda: v.tensor_scalar(turns, turns, 127.0, 8388608.0, ALU.add, ALU.mult)
                yield lambda: v.tensor_copy(bits, turns)
                yield lambda: v.scalar_tensor_tensor(dst, series, 1.0, bits.bitcast(F32), ALU.add, ALU.mult)

            nu, theta, gamma, r = (lam[:, n:n + 1] for n in range(4))
            turns, angle, square = (lam[:, n:n + 1] for n in (5, 6, 7))
            sine, cosm1, double, sine1 = (lam[:, n:n + 1] for n in (8, 9, 10, 11))

            def r_steps():
                yield lambda: v.tensor_scalar(lam[:, 4:5], nu, -1.0, None, ALU.mult)
                yield from exp_steps(r, lam[:, 4:5], 1, 3)
                yield lambda: v.memset(decay[:], 1.0)
                yield lambda: v.tensor_scalar(decay[:], decay[:], r, None, ALU.mult)
                yield lambda: v.memset(decay[:, :, 0:1], 0.0)

            def series_steps(dst, first):
                sign = 1.0 if first % 4 in (0, 1) else -1.0
                yield lambda: v.tensor_scalar(dst, square, sign / math.factorial(first), None, ALU.mult)
                for m in range(first - 2, 1, -2):
                    sign = 1.0 if m % 4 in (0, 1) else -1.0
                    yield lambda c=sign / math.factorial(m): v.scalar_tensor_tensor(dst, dst, c, square, ALU.add, ALU.mult)

            def phase_steps():
                yield (lambda: v.tensor_scalar(turns, theta, 0.15915494309189535, None, ALU.mult),)
                yield (lambda: v.tensor_scalar(turns, turns, ROUND, None, ALU.add),)
                yield (lambda: v.tensor_scalar(turns, turns, ROUND, None, ALU.subtract),)
                yield (lambda: v.scalar_tensor_tensor(theta, turns, -TWO_PI_HI, theta, ALU.mult, ALU.add),)
                yield (lambda: v.scalar_tensor_tensor(theta, turns, -TWO_PI_MID, theta, ALU.mult, ALU.add),)
                yield (lambda: v.scalar_tensor_tensor(theta, turns, -TWO_PI_LO, theta, ALU.mult, ALU.add),)
                yield (lambda: v.tensor_scalar(angle, theta, 0.125, None, ALU.mult),)
                yield (lambda: v.tensor_tensor(square, angle, angle, ALU.mult),)
                for pair in zip(series_steps(cosm1, 10), [*series_steps(sine, 9), None]):
                    yield tuple(p for p in pair if p)
                yield (lambda: v.scalar_tensor_tensor(sine, sine, 1.0, angle, ALU.add, ALU.mult),)
                for _ in range(3):
                    yield (lambda: v.scalar_tensor_tensor(double, sine, -2.0, sine, ALU.mult, ALU.mult),
                           lambda: v.scalar_tensor_tensor(sine1, cosm1, 1.0, sine, ALU.add, ALU.mult))
                    yield (lambda: v.tensor_scalar(sine, sine1, 2.0, None, ALU.mult),
                           lambda: v.tensor_copy(cosm1, double))
                yield (lambda: v.memset(phase[:, 0, 0:1], 1.0), lambda: v.memset(phase[:, 1, 0:1], 0.0),
                       lambda: v.tensor_scalar(basis[:, 0, 0:1], cosm1, 1.0, None, ALU.add),
                       lambda: v.tensor_copy(basis[:, 0, 1:2], sine))
                for n in range(7):
                    m = 2 ** n
                    c, s = basis[:, n, 0:1], basis[:, n, 1:2]
                    cc, ss = phase[:, 0, 0:m], phase[:, 1, 0:m]
                    yield (lambda: v.tensor_scalar(ptmp[:, 0, 0:m], ss, s, None, ALU.mult),
                           lambda: v.tensor_scalar(ptmp[:, 1, 0:m], cc, s, None, ALU.mult),
                           lambda: v.tensor_scalar(lam[:, 12:14], basis[:, n, :], s, None, ALU.mult))
                    yield (lambda: v.scalar_tensor_tensor(phase[:, 0, m:2 * m], cc, c, ptmp[:, 0, 0:m], ALU.mult, ALU.subtract),
                           lambda: v.scalar_tensor_tensor(phase[:, 1, m:2 * m], ss, c, ptmp[:, 1, 0:m], ALU.mult, ALU.add),
                           lambda: v.scalar_tensor_tensor(basis[:, n + 1, 0:1], c, c, lam[:, 13:14], ALU.mult, ALU.subtract),
                           lambda: v.scalar_tensor_tensor(basis[:, n + 1, 1:2], s, c, lam[:, 12:13], ALU.mult, ALU.add))
                yield (lambda: v.tensor_scalar(gphase[:], phase[:], gamma, None, ALU.mult),)

            for one in exp_steps(lam[:, 0:3], vecs[:, 11:14], 3, 0):
                link(one())
            radius = [*r_steps()]
            for n, now in enumerate(phase_steps()):
                links(*radius[n:n + 1], *now)

            dve.wait_ge(setup_pool, 2)
            dve.wait_ge(setup_act, SETUP_GB)
            turn_c, turn_s = basis[:, 7, 0:1], basis[:, 7, 1:2]

            def rotate_in(b, q):
                dve.wait_ge(u_ps.sem, u_ps.at(b, q + 1))
                if q == 0:
                    if has_earlier(b):
                        dve.wait_ge(drive_done.sem, drive_done.before(b, 4))
                else:
                    dve.wait_ge(drive_done.sem, drive_done.at(b, 2))
                gc, gs = (over_tiles(gphase[:, n, :], HALF) for n in range(2))
                ur, ui = (bk[:].rearrange("p (s t) -> p s t", t=P) for bk in (bB, bC))
                o = [rot[:, n, :].rearrange("p (s t) -> p s t", t=P) for n in range(4)]
                v.scalar_tensor_tensor(o[0], ur, vec("b0"), gc, ALU.add, ALU.mult)
                v.scalar_tensor_tensor(o[1], ui, vec("b1"), gs, ALU.add, ALU.mult)
                v.scalar_tensor_tensor(o[2], ui, vec("b1"), gc, ALU.add, ALU.mult)
                v.scalar_tensor_tensor(o[3], ur, vec("b0"), gs, ALU.add, ALU.mult).then_inc(rot_done.sem, 1)

            def inject(b):
                dve.wait_ge(drive_done.sem, drive_done.at(b, 4))
                if has_earlier(b):
                    dve.wait_ge(carry_done.sem, carry_done.before(b, 2))
                first = drive[:, :, :, 0]
                v.scalar_tensor_tensor(first, init[:], r, first, ALU.mult, ALU.add).then_inc(inject_done.sem, 1)

            def scan(b, part):
                if part == 0:
                    dve.wait_ge(inject_done.sem, inject_done.at(b, 1))
                v.tensor_tensor_scan(state[:, part].rearrange("p s t -> p (s t)"), decay[:].rearrange("p s t -> p (s t)"),
                                     drive[:, part].rearrange("p s t -> p (s t)"), 0.0, ALU.mult, ALU.add).then_inc(scan_done.sem, 1)

            def carry(b):
                dve.wait_ge(scan_done.sem, scan_done.at(b, 2))
                re, im = state[:, 0, :, P - 1], state[:, 1, :, P - 1]
                v.tensor_scalar(ctmp[:, 0, :], im, turn_s, None, ALU.mult).then_inc(carry_mul.sem, 1)
                v.tensor_scalar(ctmp[:, 1, :], re, turn_s, None, ALU.mult).then_inc(carry_mul.sem, 1)
                dve.wait_ge(carry_mul.sem, carry_mul.at(b, 2))
                v.scalar_tensor_tensor(init[:, 0, :], re, turn_c, ctmp[:, 0, :], ALU.mult, ALU.subtract).then_inc(carry_done.sem, 1)
                v.scalar_tensor_tensor(init[:, 1, :], im, turn_c, ctmp[:, 1, :], ALU.mult, ALU.add).then_inc(carry_done.sem, 1)

            def rotate_out(b, q):
                if q == 0:
                    if has_earlier(b):
                        dve.wait_ge(out_ps.sem, out_ps.before(b, 2))
                t = slice(HALF * q, HALF * q + HALF)
                c, s = (over_tiles(phase[:, n, :], HALF) for n in range(2))
                re, im = state[:, 0, t, :], state[:, 1, t, :]
                v.tensor_tensor(post[:, 0, t, :], re, c, ALU.mult)
                v.tensor_tensor(post[:, 1, t, :], im, s, ALU.mult)
                v.tensor_tensor(post[:, 2, t, :], re, s, ALU.mult)
                v.tensor_tensor(post[:, 3, t, :], im, c, ALU.mult).then_inc(post_done.sem, 1)

            def stats(src, st, mv, sigs, blk, k, ts, twice=False):
                stat_sig, part_sig, spread_sig, mean_sig = sigs
                for n in ts:
                    last = v.bn_stats(st[:, n, :], src(n))
                last.then_inc(stat_sig.sem, 1)
                t = slice(ts[0], ts[-1] + 1)
                total, gap, dev, gap2, dev_eps = (tmpS[:, m, t] for m in range(5))
                dve.wait_ge(stat_sig.sem, stat_sig.at(blk, k))
                v.tensor_tensor(gap, st[:, t, 1], st[:, t, 4], ALU.subtract).then_inc(part_sig.sem, 1)
                v.tensor_tensor(dev, st[:, t, 2], st[:, t, 5], ALU.add).then_inc(part_sig.sem, 1)
                v.tensor_tensor(total, st[:, t, 1], st[:, t, 4], ALU.add).then_inc(part_sig.sem, 1)
                dve.wait_ge(part_sig.sem, part_sig.at(blk, 4 * k - 1))
                v.scalar_tensor_tensor(gap2, gap, 0.25, gap, ALU.mult, ALU.mult).then_inc(spread_sig.sem, 1)
                v.tensor_scalar(dev_eps, dev, 1.0 / D, EPS, ALU.mult, ALU.add).then_inc(spread_sig.sem, 1)
                v.tensor_scalar(mv[:, 0, t], total, -0.5, None, ALU.mult)
                dve.wait_ge(spread_sig.sem, spread_sig.at(blk, 2 * k))
                v.scalar_tensor_tensor(mv[:, 1, t], dev, 1.0 / D, gap2, ALU.mult, ALU.add).then_inc(part_sig.sem, 1)
                if twice:
                    v.tensor_tensor(mv[:, 2, t], dev_eps, gap2, ALU.add)
                    dve.wait_ge(part_sig.sem, part_sig.at(blk, 4 * k))
                    v.tensor_scalar(mv[:, 3, t], mv[:, 1, t], 1.0 + EPS, EPS * EPS, ALU.mult, ALU.add).then_inc(mean_sig.sem, 1)
                else:
                    v.tensor_tensor(mv[:, 2, t], dev_eps, gap2, ALU.add).then_inc(mean_sig.sem, 1)

            def mean_a(b, q):
                dve.wait_ge(y_ps.sem, y_ps.at(b, q + 1))
                bk = (bB, bC)[q]
                stats(lambda n: bk[:, cols(n)], stA, mvA, (statA, partA, spreadA, meanA), b, q + 1, tiles(q))

            def centre(b, q):
                if has_earlier(b) and q == 0:
                    dve.wait_ge(xh_done.sem, xh_done.before(b, 2))
                    dve.wait_ge(x1_done.sem, x1_done.before(b, 2))
                bk = (bB, bC)[q]
                dve.wait_ge(meanA.sem, meanA.at(b, q + 1))
                for n in tiles(q):
                    last = v.scalar_tensor_tensor(z[:, n, :], bk[:, cols(n)], mvA[:, 0, n:n + 1], gb[:, 0, :],
                                                  ALU.add, ALU.mult)
                last.then_inc(centred.sem, 1)

            def finish_a(b, q):
                dve.wait_ge(rstdA.sem, rstdA.at(b, q + 1))
                dve.wait_ge(centred.sem, centred.at(b, q + 1))
                dve.wait_ge(xb_done.sem, xb_done.at(b, 1))
                for n in tiles(q):
                    last = v.scalar_tensor_tensor(z[:, n, :], z[:, n, :], rsA[:, 0, n:n + 1], xb[:, n, :],
                                                  ALU.mult, ALU.add)
                last.then_inc(z_done.sem, 1)

            def mean_b(b):
                dve.wait_ge(z_done.sem, z_done.at(b, 2))
                stats(lambda n: z[:, n, :], stB, mvB, (statB, partB, spreadB, meanB), b, 1, range(NS), True)

            def qk_products(j, s):
                dve.wait_ge(qkv_done.sem, qkv_done.at(j, 8))
                qk_product(v, s).then_inc(qk_dve.sem, 1)

            def sum_scores(j, s):
                if s in DVE_S:
                    dve.wait_ge(qk_dve.sem, qk_dve.at(j, s - DVE_S[0] + 1))
                else:
                    dve.wait_ge(qk_pool.sem, qk_pool.at(j, s + 1))
                v.tensor_reduce(scores[:, s, 0:s + 1, :].rearrange("p t h -> p (t h)"),
                                prod[:, row_of[s]:row_of[s + 1], :].rearrange("p t (h d) -> p (t h) d", d=HD),
                                AX.X, ALU.add).then_inc(scores_done.sem, 1)

            def softmax_in(j):
                dve.wait_ge(scores_done.sem, scores_done.at(j, NS))
                v.tensor_reduce(smax[:], scores[:].rearrange("p s t h -> p s h t"), AX.X, ALU.max).then_inc(smax_done.sem, 1)
                dve.wait_ge(smax_done.sem, smax_done.at(j, 1))
                if has_earlier(j):
                    dve.wait_ge(pv_pool.sem, pv_pool.before(j, len(POOL_S)))
                v.tensor_tensor(probs[:], scores[:], smax[:].unsqueeze(2).to_broadcast([P, NS, NS, NH]),
                                ALU.subtract).then_inc(shift_done.sem, 1)

            def softmax_out(j):
                dve.wait_ge(exp_done.sem, exp_done.at(j, 1))
                v.tensor_reduce(ssum[:], probs[:].rearrange("p s t h -> p s h t"), AX.X, ALU.add).then_inc(ssum_done.sem, 1)
                dve.wait_ge(ssum_done.sem, ssum_done.at(j, 1))
                v.reciprocal(srec[:], ssum[:]).then_inc(srec_done.sem, 1)
                dve.wait_ge(srec_done.sem, srec_done.at(j, 1))
                v.tensor_tensor(probs[:], probs[:], srec[:].unsqueeze(2).to_broadcast([P, NS, NS, NH]),
                                ALU.mult).then_inc(probs_done.sem, 1)

            def pv_products(j, s):
                dve.wait_ge(probs_done.sem, probs_done.at(j, 1))
                pv_product(v, s).then_inc(pv_dve.sem, 1)

            def sum_pv(j, s):
                if has_earlier(j):
                    dve.wait_ge(attT_ps.sem, attT_ps.before(j, 2))
                if s in DVE_S:
                    dve.wait_ge(pv_dve.sem, pv_dve.at(j, s - DVE_S[0] + 1))
                else:
                    dve.wait_ge(pv_pool.sem, pv_pool.at(j, s + 1))
                v.tensor_reduce(att[:, s, :], prod[:, row_of[s]:row_of[s + 1], :].rearrange("p t c -> p c t"),
                                AX.X, ALU.add).then_inc(att_done.sem, 1)

            def residual(j, q):
                if has_earlier(j):
                    dve.wait_ge(base_done.sem, base_done.before(j, 1))
                    dve.wait_ge(xh2_done.sem, xh2_done.before(j, 2))
                dve.wait_ge(x1_done.sem, x1_done.at(j, 2))
                dve.wait_ge(proj_ps.sem, proj_ps.at(j, q + 1))
                t = slice(HALF * q, HALF * q + HALF)
                v.tensor_tensor(h2[:, t, :], (bD, bE)[q][:].rearrange("p (s t) -> p s t", t=P), x1[:, t, :],
                                ALU.add).then_inc(h2_done.sem, 1)

            def mean_c(j):
                dve.wait_ge(h2_done.sem, h2_done.at(j, 2))
                stats(lambda n: h2[:, n, :], stC, mvC, (statC, partC, spreadC, meanC), j, 1, range(NS))

            def top_logit(j):
                dve.wait_ge(logit_ps.sem, logit_ps.at(j, 1))
                v.tensor_reduce(rt1[:, 0], bA[:, 0:NS * NE].rearrange("p (s e) -> p s e", e=NE), AX.X,
                                ALU.max).then_inc(top_done.sem, 1)
                dve.wait_ge(top_done.sem, top_done.at(j, 1))
                v.tensor_tensor(rt[:, 0], bA[:, 0:NS * NE].rearrange("p (s e) -> p s e", e=NE),
                                rt1[:, 0].unsqueeze(2).to_broadcast([P, NS, NE]), ALU.subtract).then_inc(lshift.sem, 1)

            def gate(j):
                count = [0]

                def step(ins):
                    ins.then_inc(gstep.sem, 1)
                    count[0] += 1
                    dve.wait_ge(gstep.sem, gstep.at(j, count[0]))

                def per_tile(a):
                    return a.unsqueeze(2).to_broadcast([P, NS, NE])

                pr, key, one, two, left = (rt[:, n] for n in range(5))
                total, inv, best, second, k2 = (rt1[:, n] for n in range(1, 6))
                dve.wait_ge(gexp.sem, gexp.at(j, 1))
                step(v.tensor_reduce(total, pr, AX.X, ALU.add))
                step(v.reciprocal(inv, total))
                step(v.tensor_tensor(pr, pr, per_tile(inv), ALU.mult))
                for src, winner, m, kk in ((pr, one, best, k2), (left, two, second, k2)):
                    step(v.tensor_reduce(m, src, AX.X, ALU.max))
                    step(v.tensor_tensor(key, src, per_tile(m), ALU.is_equal))
                    step(v.tensor_tensor(key, key, rank8[:], ALU.mult))
                    step(v.tensor_reduce(kk, key, AX.X, ALU.max))
                    if winner is one:
                        step(v.tensor_tensor(one, key, per_tile(kk), ALU.is_equal))
                        step(v.scalar_tensor_tensor(left, one, -2.0, pr, ALU.mult, ALU.add))
                v.tensor_tensor(two, key, per_tile(k2), ALU.is_equal).then_inc(two_done.sem, 1)
                dve.wait_ge(two_done.sem, two_done.at(j, 1))
                v.tensor_tensor(one, one, two, ALU.add).then_inc(both_done.sem, 1)
                dve.wait_ge(both_done.sem, both_done.at(j, 1))
                v.tensor_tensor(gates[:], pr, one, ALU.mult).then_inc(gates_done.sem, 1)

            def accumulate(k, g):
                q, e = divmod(g, NE)
                n_done = q * (NE - ACT_E) + e - ACT_E
                dve.wait_ge(moe_ps.sem, moe_ps.at(k, g + 1))
                if e == ACT_E:
                    dve.wait_ge(added.sem, added.at(k, ACT_E * (q + 1)))
                    if has_earlier(k):
                        dve.wait_ge(stored[q].sem, stored[q].before(k, 16))
                else:
                    dve.wait_ge(acc_done.sem, acc_done.at(k, n_done))
                so_far = base if e == ACT_E else res
                for n in tiles(q):
                    last = v.scalar_tensor_tensor(res[:, n, :], group_bank[g][:, cols(n)], gates[:, n, e:e + 1], so_far[:, n, :],
                                                  ALU.mult, ALU.add)
                last.then_inc(acc_done.sem, 1)

            def split_l2(k, q):
                dve.wait_ge(l2S_done.sem, l2S_done.at(k, q + 1))
                if has_earlier(k):
                    dve.wait_ge(h_ps.sem, h_ps.before(k, NF * GROUPS))
                v.tensor_tensor(l2_diff[:], l2_scaled[:], l2T[:, q, :], ALU.subtract).then_inc(l2_diff_done.sem, 1)
                dve.wait_ge(l2_diff_done.sem, l2_diff_done.at(k, q + 1))
                v.tensor_tensor(l2_high[:, q, :], l2_scaled[:], l2_diff[:], ALU.subtract).then_inc(l2_high_done.sem, 1)
                dve.wait_ge(l2_high_done.sem, l2_high_done.at(k, q + 1))
                v.tensor_tensor(l2_low[:, q, :], l2T[:, q, :], l2_high[:, q, :].bitcast(F32), ALU.subtract).then_inc(l2_low_done.sem, 1)

            def mean_d(k, q):
                dve.wait_ge(acc_done.sem, acc_done.at(k, (NE - ACT_E) * (q + 1)))
                stats(lambda n: res[:, n, :], stD, mvD, (statD, partD, spreadD, meanD), k, q + 1, tiles(q))

            def iteration(i):
                if runs(i - 1):
                    split_l2(i - 1, 0)
                if runs(i + 1):
                    rotate_in(i + 1, 0)
                if runs(i - 1):
                    top_logit(i - 1)
                    gate(i - 1)
                if runs(i + 1):
                    rotate_in(i + 1, 1)
                if runs(i - 1):
                    split_l2(i - 1, 1)
                if runs(i + 1):
                    inject(i + 1)
                    scan(i + 1, 0)
                    scan(i + 1, 1)
                    carry(i + 1)
                    rotate_out(i + 1, 0)
                if runs(i):
                    qk_products(i, 4)
                    qk_products(i, 6)
                if runs(i + 1):
                    rotate_out(i + 1, 1)
                if runs(i - 1):
                    accumulate(i - 1, 2)
                if runs(i):
                    qk_products(i, 5)
                    qk_products(i, 7)
                    sum_scores(i, 6)
                    sum_scores(i, 7)
                if runs(i - 1):
                    accumulate(i - 1, 3)
                if runs(i):
                    sum_scores(i, 3)
                    sum_scores(i, 4)
                if runs(i - 1):
                    accumulate(i - 1, 4)
                if runs(i):
                    sum_scores(i, 0)
                    sum_scores(i, 1)
                    sum_scores(i, 5)
                    sum_scores(i, 2)
                if runs(i - 1):
                    accumulate(i - 1, 5)
                if runs(i):
                    softmax_in(i)
                if runs(i - 1):
                    accumulate(i - 1, 6)
                if runs(i):
                    softmax_out(i)
                    pv_products(i, 4)
                    pv_products(i, 5)
                    pv_products(i, 6)
                    pv_products(i, 7)
                    sum_pv(i, 0)
                    sum_pv(i, 5)
                if runs(i - 1):
                    accumulate(i - 1, 7)
                if runs(i):
                    sum_pv(i, 4)
                    sum_pv(i, 7)
                    sum_pv(i, 3)
                    sum_pv(i, 2)
                    sum_pv(i, 6)
                    sum_pv(i, 1)
                if runs(i + 1):
                    mean_a(i + 1, 0)
                if runs(i - 1):
                    mean_d(i - 1, 0)
                if runs(i + 1):
                    centre(i + 1, 0)
                    mean_a(i + 1, 1)
                    centre(i + 1, 1)
                    finish_a(i + 1, 0)
                    finish_a(i + 1, 1)
                if runs(i):
                    residual(i, 0)
                if runs(i + 1):
                    mean_b(i + 1)
                if runs(i):
                    residual(i, 1)
                if runs(i - 1):
                    accumulate(i - 1, 10)
                if runs(i):
                    mean_c(i)
                if runs(i - 1):
                    accumulate(i - 1, 11)
                    accumulate(i - 1, 12)
                    accumulate(i - 1, 13)
                    accumulate(i - 1, 14)
                    accumulate(i - 1, 15)
                    mean_d(i - 1, 1)

            pipeline(dve, iteration)

        @block.scalar
        def _(act):
            a = nc.scalar

            act.wait_ge(w_loaded, W_ALL)
            a.activation(wmid[:, 1, :], wmid[:, 1, :], ACT.Copy, scale=-1.0)
            a.activation(proj_perm[:].rearrange("p (r g d) -> p r g d", g=NKV, d=HD),
                         proj_rows.rearrange("p (g r d) -> p r g d", r=REP, d=HD), ACT.Copy).then_inc(setup_act, 1)
            act.wait_ge(setup_pe, 2)
            a.activation(qkvT[:, 0:P].rearrange("p (r g d) -> p r g d", g=NKV, d=HD),
                         bD[:, 0:P].rearrange("p (g r d) -> p r g d", r=REP, d=HD), ACT.Copy)
            a.activation(qkvT[:, P:QKV], bD[:, P:QKV], ACT.Copy)
            a.activation(projT[:], bD[:, 256:384], ACT.Copy)
            a.activation(routerT[:], bD[:, 384:384 + NE], ACT.Copy)
            a.activation(gb[:].rearrange("p a d -> p (a d)"), bE[:, 0:2 * D], ACT.Copy).then_inc(setup_act, 1)
            act.wait_ge(ew1_loaded, 16)
            a.activation(ew1_scaled, ew1, ACT.Copy, scale=SPLIT).then_inc(ew1_split, 1)
            act.wait_ge(setup_dve, 1)

            def evac_xT(b, q):
                act.wait_ge(xT_ps.sem, xT_ps.at(b, q + 1))
                if has_earlier(b):
                    act.wait_ge(out_ps.sem, out_ps.before(b, 2))
                a.activation(xT[:, q, :], bA[:], ACT.Copy).then_inc(xT_done.sem, 1)

            def evac_out(b, q):
                act.wait_ge(out_ps.sem, out_ps.at(b, q + 1))
                if has_earlier(b):
                    act.wait_ge(y_ps.sem, y_ps.before(b, 2))
                bk = (bA, bB)[q]
                a.activation(outT[:, q, :], bk[:], ACT.Identity, bias=vec("bo")).then_inc(outT_done.sem, 1)
                a.activation(outT2[:, q, :], bk[:], ACT.Identity, bias=vec("bo2")).then_inc(outT_done.sem, 1)

            def gelu_mixer(b, q):
                act.wait_ge(z_ps.sem, z_ps.at(b, q + 1))
                a.activation(gT[:, q, :], (bC, bA)[q][:], ACT.Gelu, bias=vec("w1b")).then_inc(gT_done.sem, 1)

            def evac_ln(j, q):
                act.wait_ge(xhT_ps.sem, xhT_ps.at(j, q + 1))
                if has_earlier(j):
                    act.wait_ge(qkv_ps.sem, qkv_ps.before(j, 4))
                a.activation(lnT[:, q, :], (bD, bE)[q][:], ACT.Identity, bias=vec("l1b"), scale=vec("l1w")).then_inc(lnT_done.sem, 1)

            def evac_qkv(j, n):
                act.wait_ge(qkv_ps.sem, qkv_ps.at(j, n + 1))
                if n == 0:
                    if has_earlier(j):
                        act.wait_ge(scores_done.sem, scores_done.before(j, NS))
                    if has_earlier(j):
                        act.wait_ge(att_done.sem, att_done.before(j, NS))
                bk = (bD, bE)[n % 2][:].rearrange("p (s c) -> p s c", s=2)
                t = slice(2 * n, 2 * n + 2)
                a.activation(qk[:, t, :], bk[:, :, 0:160], ACT.Copy).then_inc(qkv_done.sem, 1)
                a.activation(vx[:, t, :].rearrange("p s (r c) -> p s r c", r=REP),
                             bk[:, :, 160:QKV].unsqueeze(2).to_broadcast([P, 2, REP, NKV * HD]), ACT.Copy).then_inc(qkv_done.sem, 1)

            def exp_scores(j):
                act.wait_ge(shift_done.sem, shift_done.at(j, 1))
                a.activation(probs[:], probs[:], ACT.Exp, scale=float(HD) ** -0.5).then_inc(exp_done.sem, 1)

            def evac_att(j, q):
                act.wait_ge(attT_ps.sem, attT_ps.at(j, q + 1))
                if has_earlier(j):
                    act.wait_ge(proj_ps.sem, proj_ps.before(j, 2))
                a.activation(attT[:, q, :], (bD, bE)[q][:], ACT.Copy).then_inc(attT_done.sem, 1)

            def evac_l2(j, q):
                act.wait_ge(l2_ps.sem, l2_ps.at(j, q + 1))
                if has_earlier(j):
                    act.wait_ge(h_ps.sem, h_ps.before(j, NF * GROUPS))
                if has_earlier(j):
                    act.wait_ge(l2_low_done.sem, l2_low_done.before(j, q + 1))
                a.activation(l2T[:, q, :], (bD, bE)[q][:], ACT.Identity, bias=vec("l2b"), scale=vec("l2w")).then_inc(l2T_done.sem, 1)
                if q:
                    act.wait_ge(l2_high_done.sem, l2_high_done.at(j, 1))
                a.activation(l2_scaled[:], (bD, bE)[q][:], ACT.Identity, bias=vec("l2bS"), scale=vec("l2wS")).then_inc(l2S_done.sem, 1)

            def normalise(dst, src, scale, shift, ts):
                for n in ts:
                    last = a.activation(dst[:, n, :], src[:, n, :], ACT.Identity, bias=shift[:, n:n + 1], scale=scale[:, n:n + 1])
                return last

            def normalise_xh(b, q):
                act.wait_ge(shiftB.sem, shiftB.at(b, 1))
                if has_earlier(b):
                    act.wait_ge(xhT_ps.sem, xhT_ps.before(b, 2))
                normalise(xh, z, rsB[:, 0, 1], rsB[:, 1, 1], tiles(q)).then_inc(xh_done.sem, 1)

            def normalise_x1(b, q):
                act.wait_ge(shiftB.sem, shiftB.at(b, 2))
                if has_earlier(b):
                    act.wait_ge(base_done.sem, base_done.before(b, 1))
                normalise(x1, z, rsB[:, 0, 0], rsB[:, 1, 0], tiles(q)).then_inc(x1_done.sem, 1)

            def normalise_c(j, q):
                act.wait_ge(shiftC.sem, shiftC.at(j, 1))
                if has_earlier(j):
                    act.wait_ge(l2_ps.sem, l2_ps.before(j, 2))
                normalise(xh2, h2, rsC[:, 0], rsC[:, 1], tiles(q)).then_inc(xh2_done.sem, 1)

            def normalise_d(k, q):
                act.wait_ge(shiftD.sem, shiftD.at(k, q + 1))
                normalise(res, res, rsD[:, 0], rsD[:, 1], tiles(q)).then_inc(y_done.sem, 1)

            def weigh(k, g):
                q, e = divmod(g, NE)
                act.wait_ge(moe_ps.sem, moe_ps.at(k, g + 1))
                if g == 0:
                    act.wait_ge(gates_done.sem, gates_done.at(k, 1))
                n_weighed = q * ACT_E + e
                if n_weighed:
                    act.wait_ge(added.sem, added.at(k, n_weighed))
                elif has_earlier(k):
                    act.wait_ge(added.sem, added.before(k, 2 * ACT_E))
                for n in tiles(q):
                    last = a.activation(weighed[:, cols(n)], group_bank[g][:, cols(n)], ACT.Copy, scale=gates[:, n, e:e + 1])
                last.then_inc(weighed_done.sem, 1)

            def exp_gates(j):
                act.wait_ge(lshift.sem, lshift.at(j, 1))
                a.activation(rt[:, 0], rt[:, 0], ACT.Exp).then_inc(gexp.sem, 1)

            def gelu_experts(k, g):
                for f in range(NF):
                    act.wait_ge(h_ps.sem, h_ps.at(k, NF * g + f + 1))
                    if g >= 2:
                        act.wait_ge(moe_ps.sem, moe_ps.at(k, g - 1))
                    else:
                        if has_earlier(k):
                            act.wait_ge(moe_ps.sem, moe_ps.before(k, GROUPS - 1 + g))
                    a.activation(hT[:, g % 2, f, :], (bF, bG)[f][:], ACT.Gelu_apprx_tanh).then_inc(hT_done.sem, 1)

            def iteration(i):
                if runs(i + 1):
                    evac_xT(i + 1, 0)
                if runs(i - 1):
                    evac_l2(i - 1, 1)
                if runs(i):
                    normalise_x1(i, 1)
                if runs(i + 1):
                    evac_xT(i + 1, 1)
                if runs(i):
                    evac_ln(i, 0)
                    evac_ln(i, 1)
                if runs(i - 1):
                    exp_gates(i - 1)
                    gelu_experts(i - 1, 0)
                    gelu_experts(i - 1, 1)
                if runs(i):
                    evac_qkv(i, 0)
                    evac_qkv(i, 1)
                if runs(i - 1):
                    weigh(i - 1, 0)
                if runs(i):
                    evac_qkv(i, 3)
                if runs(i - 1):
                    gelu_experts(i - 1, 2)
                    weigh(i - 1, 1)
                if runs(i):
                    evac_qkv(i, 2)
                if runs(i - 1):
                    gelu_experts(i - 1, 3)
                if runs(i + 1):
                    evac_out(i + 1, 0)
                    evac_out(i + 1, 1)
                if runs(i - 1):
                    gelu_experts(i - 1, 4)
                if runs(i + 1):
                    gelu_mixer(i + 1, 0)
                if runs(i - 1):
                    gelu_experts(i - 1, 5)
                    gelu_experts(i - 1, 6)
                if runs(i + 1):
                    gelu_mixer(i + 1, 1)
                if runs(i - 1):
                    gelu_experts(i - 1, 7)
                if runs(i):
                    exp_scores(i)
                if runs(i - 1):
                    gelu_experts(i - 1, 8)
                    gelu_experts(i - 1, 9)
                if runs(i):
                    evac_att(i, 0)
                    evac_att(i, 1)
                if runs(i - 1):
                    weigh(i - 1, 8)
                    gelu_experts(i - 1, 10)
                    gelu_experts(i - 1, 11)
                    weigh(i - 1, 9)
                    gelu_experts(i - 1, 12)
                    normalise_d(i - 1, 0)
                    gelu_experts(i - 1, 13)
                if runs(i + 1):
                    normalise_xh(i + 1, 0)
                if runs(i - 1):
                    gelu_experts(i - 1, 14)
                if runs(i + 1):
                    normalise_x1(i + 1, 0)
                if runs(i - 1):
                    gelu_experts(i - 1, 15)
                if runs(i):
                    normalise_c(i, 0)
                    normalise_c(i, 1)
                    evac_l2(i, 0)
                if runs(i + 1):
                    normalise_xh(i + 1, 1)
                if runs(i - 1):
                    normalise_d(i - 1, 1)

            pipeline(act, iteration)

        @block.tensor
        def _(pe):
            t = nc.tensor
            idn = ident[:]

            pe.wait_ge(vec_loaded, VEC_ALL)
            pe.wait_ge(setup_pool, 2)
            t.transpose(bF[:, 0:14], vec_rows[:], ident[0:14, 0:14]).then_inc(setup_pe, 1)
            pe.wait_ge(w_loaded, W_ALL)
            pe.wait_ge(setup_act, 1)
            t.matmul(bE[:, 0:2 * D], ones_row[:], rowv[:].rearrange("p a d -> p (a d)"), start=True, stop=True)
            t.transpose(bD[:, 0:P], qkv_rows[:, 0, :], idn)
            t.transpose(bD[:, P:QKV], qkv_rows[0:QKV - P, 1, :], ident[0:QKV - P, 0:QKV - P])
            t.transpose(bD[:, 256:384], proj_perm[:], idn)
            t.transpose(bD[:, 384:384 + NE], router_rows[:], ident[0:NE, 0:NE]).then_inc(setup_pe, 1)

            def transposes(bk, src, q):
                for n in tiles(q):
                    last = t.transpose(bk[:, cols(n)], src[:, n, :], idn)
                return last

            def transpose_x(b, q):
                if q == 0:
                    pe.wait_ge(x_loaded.sem, x_loaded.at(b, 16))
                    if has_earlier(b):
                        pe.wait_ge(gT_done.sem, gT_done.before(b, 2))
                    if runs(b - 3):
                        pe.wait_ge(weighed_done.sem, weighed_done.at(b - 3, ACT_E + 2))
                else:
                    pe.wait_ge(xT_done.sem, xT_done.at(b, 1))
                transposes(bA, x_in, q).then_inc(xT_ps.sem, 1)

            def project_in(b, q):
                pe.wait_ge(xT_done.sem, xT_done.at(b, q + 1))
                if q == 0:
                    if has_earlier(b):
                        pe.wait_ge(centred.sem, centred.before(b, 2))
                    if runs(b - 3):
                        pe.wait_ge(acc_done.sem, acc_done.at(b - 3, 2 * (NE - ACT_E)))
                else:
                    pe.wait_ge(rot_done.sem, rot_done.at(b, 1))
                t.matmul(bB[:], win[:, 0, :], xT[:, q, :], start=True, stop=True)
                t.matmul(bC[:], win[:, 1, :], xT[:, q, :], start=True, stop=True).then_inc(u_ps.sem, 1)

            def mix(b, q):
                bk = (bA, bB)[q]
                if q == 0 and runs(b - 2):
                    pe.wait_ge(lshift.sem, lshift.at(b - 2, 1))
                if q == 0:
                    pe.wait_ge(xT_done.sem, xT_done.at(b, 2))
                else:
                    pe.wait_ge(rot_done.sem, rot_done.at(b, 2))
                t.matmul(bk[:], win[:, 2, :], xT[:, q, :], start=True, stop=False)
                pe.wait_ge(hid_done.sem, hid_done.at(b, 2 * q + 2))
                for n in range(2):
                    last = t.matmul(bk[:], wmid[:, n, :], post[:, 2 * n, HALF * q:HALF * q + HALF, :].rearrange("p s t -> p (s t)"),
                                    start=False, stop=(n == 1))
                last.then_inc(out_ps.sem, 1)

            def mlp_in(b, q):
                pe.wait_ge(outT_done.sem, outT_done.at(b, 2 * q + 1))
                t.matmul((bC, bA)[q][:], w1[:], outT[:, q, :], start=True, stop=True).then_inc(z_ps.sem, 1)

            def mlp_out(b, q):
                pe.wait_ge(outT_done.sem, outT_done.at(b, 4))
                pe.wait_ge(gT_done.sem, gT_done.at(b, q + 1))
                bk = (bB, bC)[q]
                for n in tiles(q):
                    t.matmul(bk[:, cols(n)], gT[:, q, cols(n)], w2[:], start=True, stop=False)
                    last = t.matmul(bk[:, cols(n)], outT2[:, q, cols(n)], idn, start=False, stop=True)
                last.then_inc(y_ps.sem, 1)

            def transpose_xh(j, q):
                pe.wait_ge(xh_done.sem, xh_done.at(j, q + 1))
                if has_earlier(j):
                    pe.wait_ge(l2S_done.sem, l2S_done.before(j, q + 1))
                transposes((bD, bE)[q], xh, q).then_inc(xhT_ps.sem, 1)

            def project_qkv(j, n):
                if n < 2:
                    pe.wait_ge(lnT_done.sem, lnT_done.at(j, 2))
                else:
                    pe.wait_ge(qkv_done.sem, qkv_done.at(j, 2 * n - 2))
                bk = (bD, bE)[n % 2]
                for m in range(2):
                    s = 2 * n + m
                    last = t.matmul(bk[:, 256 * m:256 * m + QKV], lnT[:, s // HALF, cols(s)], qkvT[:], start=True, stop=True)
                last.then_inc(qkv_ps.sem, 1)

            def transpose_att(j, q):
                pe.wait_ge(att_done.sem, att_done.at(j, NS))
                pe.wait_ge(qkv_done.sem, qkv_done.at(j, 8))
                if q and runs(j - 1):
                    pe.wait_ge(acc_done.sem, acc_done.at(j - 1, 7 - ACT_E + 1))
                transposes((bD, bE)[q], att, q).then_inc(attT_ps.sem, 1)

            def project_att(j, q):
                pe.wait_ge(attT_done.sem, attT_done.at(j, q + 1))
                bk = (bD, bE)[q]
                for n in tiles(q):
                    last = t.matmul(bk[:, cols(n)], attT[:, q, cols(n)], projT[:], start=True, stop=True)
                last.then_inc(proj_ps.sem, 1)

            def transpose_xh2(j, q):
                pe.wait_ge(xh2_done.sem, xh2_done.at(j, q + 1))
                pe.wait_ge(h2_done.sem, h2_done.at(j, q + 1))
                transposes((bD, bE)[q], xh2, q).then_inc(l2_ps.sem, 1)

            def route(j):
                if runs(j + 2):
                    pe.wait_ge(xT_done.sem, xT_done.at(j + 2, 2))
                pe.wait_ge(l2T_done.sem, l2T_done.at(j, 2))
                for n in range(NS):
                    last = t.matmul(bA[:, NE * n:NE * n + NE], l2T[:, n // HALF, cols(n)], routerT[:], start=True, stop=True)
                last.then_inc(logit_ps.sem, 1)

            def experts_in(k, g):
                q, e = divmod(g, NE)
                if g == 0 and not has_earlier(k):
                    pe.wait_ge(late_loaded, LATE_ALL)
                    pe.wait_ge(ew1_split, 4)
                if e == 0:
                    pe.wait_ge(l2_low_done.sem, l2_low_done.at(k, q + 1))
                for f in range(NF):
                    if g:
                        pe.wait_ge(hT_done.sem, hT_done.at(k, NF * (g - 1) + f + 1))
                    else:
                        if has_earlier(k):
                            pe.wait_ge(hT_done.sem, hT_done.before(k, NF * (GROUPS - 1) + f + 1))
                    wh, wl = (w[:, e, 128 * f:128 * f + 128] for w in (ew1_high, ew1_low))
                    t.matmul((bF, bG)[f][:], wl, l2_high[:, q, :], start=True, stop=False)
                    t.matmul((bF, bG)[f][:], wh, l2_low[:, q, :], start=False, stop=False)
                    t.matmul((bF, bG)[f][:], wh, l2_high[:, q, :], start=False, stop=True).then_inc(h_ps.sem, 1)

            def experts_out(k, g):
                q, e = divmod(g, NE)
                pe.wait_ge(hT_done.sem, hT_done.at(k, NF * (g + 1)))
                bk, earlier = group_bank[g], earlier_in_bank(g)
                if earlier is None:
                    if bk is bH:
                        if has_earlier(k):
                            pe.wait_ge(acc_done.sem, acc_done.before(k, 2 * (NE - ACT_E) - 1))
                    elif bk is bE:
                        if runs(k + 1):
                            pe.wait_ge(qkv_done.sem, qkv_done.at(k + 1, 8))
                    elif runs(k + 2):
                        if bk is bA:
                            pe.wait_ge(gT_done.sem, gT_done.at(k + 2, 2))
                        else:
                            pe.wait_ge(centred.sem, centred.at(k + 2, 2))
                elif earlier % NE < ACT_E:
                    pe.wait_ge(weighed_done.sem, weighed_done.at(k, ACT_E * (earlier // NE) + earlier % NE + 1))
                else:
                    pe.wait_ge(acc_done.sem, acc_done.at(k, (NE - ACT_E) * (earlier // NE) + earlier % NE - ACT_E + 1))
                for n in tiles(q):
                    for f in range(NF):
                        last = t.matmul(bk[:, cols(n)], hT[:, g % 2, f, cols(n)], ew2[:, e, f, :], start=(f == 0),
                                        stop=(f == NF - 1))
                last.then_inc(moe_ps.sem, 1)

            def iteration(i):
                if runs(i - 1):
                    transpose_xh2(i - 1, 1)
                if runs(i + 1):
                    transpose_x(i + 1, 0)
                if runs(i):
                    transpose_xh(i, 0)
                if runs(i + 1):
                    project_in(i + 1, 0)
                    transpose_x(i + 1, 1)
                if runs(i):
                    transpose_xh(i, 1)
                if runs(i - 1):
                    route(i - 1)
                    experts_in(i - 1, 0)
                if runs(i + 1):
                    project_in(i + 1, 1)
                if runs(i):
                    project_qkv(i, 0)
                    project_qkv(i, 1)
                if runs(i - 1):
                    experts_in(i - 1, 1)
                if runs(i):
                    project_qkv(i, 2)
                if runs(i - 1):
                    experts_out(i - 1, 0)
                    experts_in(i - 1, 2)
                if runs(i):
                    project_qkv(i, 3)
                if runs(i - 1):
                    experts_out(i - 1, 1)
                    experts_in(i - 1, 3)
                    experts_out(i - 1, 2)
                if runs(i + 1):
                    mix(i + 1, 0)
                if runs(i - 1):
                    experts_out(i - 1, 3)
                if runs(i + 1):
                    mix(i + 1, 1)
                if runs(i - 1):
                    experts_in(i - 1, 4)
                if runs(i + 1):
                    mlp_in(i + 1, 0)
                    mlp_in(i + 1, 1)
                if runs(i - 1):
                    experts_in(i - 1, 5)
                    experts_out(i - 1, 4)
                    experts_in(i - 1, 6)
                    experts_out(i - 1, 5)
                    experts_in(i - 1, 7)
                if runs(i + 1):
                    mlp_out(i + 1, 0)
                if runs(i - 1):
                    experts_out(i - 1, 6)
                    experts_in(i - 1, 8)
                    experts_out(i - 1, 7)
                if runs(i + 1):
                    mlp_out(i + 1, 1)
                if runs(i - 1):
                    experts_out(i - 1, 8)
                    experts_in(i - 1, 9)
                if runs(i):
                    transpose_att(i, 0)
                    transpose_att(i, 1)
                    project_att(i, 0)
                if runs(i - 1):
                    experts_in(i - 1, 10)
                    experts_out(i - 1, 9)
                    experts_in(i - 1, 11)
                if runs(i):
                    project_att(i, 1)
                if runs(i - 1):
                    experts_out(i - 1, 10)
                    experts_in(i - 1, 12)
                    experts_out(i - 1, 11)
                    experts_in(i - 1, 13)
                    experts_out(i - 1, 12)
                    experts_in(i - 1, 14)
                    experts_out(i - 1, 13)
                    experts_in(i - 1, 15)
                    experts_out(i - 1, 14)
                    experts_out(i - 1, 15)
                if runs(i):
                    transpose_xh2(i, 0)

            pipeline(pe, iteration)


_INS = ["L0_attn_x", "L0_attn_W_in", "L0_attn_b_in", "L0_attn_params_log", "L0_attn_W_mid", "L0_attn_b_mid",
        "L0_attn_w1_w", "L0_attn_w1_b", "L0_attn_w2_w", "L0_attn_w2_b", "L0_attn_ln_g", "L0_attn_ln_b",
        "L0_ffn_ln1_weight", "L0_ffn_ln1_bias", "L0_ffn_ln2_weight", "L0_ffn_ln2_bias", "L0_ffn_qkv_weight",
        "L0_ffn_proj_weight", "L0_ffn_router_weight", "L0_ffn_moe_w1", "L0_ffn_moe_w2"]


def kernel(**inputs):
    import numpy as _np
    import concourse.bacc as _bacc
    from concourse.bass_utils import run_bass_kernel_spmd as _run

    nc = _bacc.Bacc("TRN2", target_bir_lowering=False, num_devices=1)
    arrays, args = {}, []
    for name in _INS:
        a = _np.ascontiguousarray(inputs[name])
        arrays[name] = a
        args.append(nc.dram_tensor(name, a.shape, F32, kind="ExternalInput").ap())
    args.append(nc.dram_tensor("out", arrays["L0_attn_x"].shape, F32, kind="ExternalOutput").ap())
    build(nc, *args)
    return _run(nc, [arrays], core_ids=[0]).results[0]["out"]
```

```python
import math
from contextlib import ExitStack

import concourse.bass as bass
from concourse import mybir

F32 = mybir.dt.float32
F32R = mybir.dt.float32r
ALU = mybir.AluOpType
ACT = mybir.ActivationFunctionType
AX = mybir.AxisListType

P = 128
D = 128
HALF = 4
EPS = 1e-5
TWO_PI_HI = 6.28125
TWO_PI_MID = 0.0019350051879882812
TWO_PI_LO = 3.019915981956752e-07
LN2_HI = 0.693359375
LN2_LO = -2.12194440e-4
SPLIT = 4097.0
ROUND = 12582912.0
MASKED = -3.4028234663852886e38
NKV, REP, HD = 4, 4, 8
NH = NKV * REP


class Signal:

    def __init__(self, sem, per_block):
        self.sem, self.per_block = sem, per_block

    def at(self, block, k):
        return self.per_block * block + k

    def before(self, block, k):
        return self.per_block * block - self.per_block + k


def has_earlier(block):
    return not (isinstance(block, int) and block == 0)


def build(nc, x, W_in, b_in, plog, W_mid, b_mid, w1_w, w1_b, w2_w, w2_b, ln_g, ln_b,
          ln1_w, ln1_b, ln2_w, ln2_b, qkv_w, proj_w, router_w, moe_w1, moe_w2, out):
    NS, T, _ = x.shape
    NB = T // P
    NE, _, FF = moe_w1.shape
    NF = FF // 128
    QKV = qkv_w.shape[0]
    GROUPS = 2 * NE
    ACT_E = 2
    row_of = [s * (s + 1) // 2 for s in range(NS + 1)]
    assert NS == 2 * HALF and NF == 2 and QKV == (NH + 2 * NKV) * HD
    POOL_S = range(0, 5)
    DVE_S = range(5, NS)

    with ExitStack() as ctx:
        def sb(name, *shape, dtype=F32):
            return ctx.enter_context(nc.sbuf_tensor(name, list(shape), dtype))

        def sem(name):
            return ctx.enter_context(nc.semaphore(name))

        def signal(name, per_block):
            return Signal(sem(name), per_block)

        win = sb("win", P, 3, D)
        wmid = sb("wmid", P, 2, D)
        w1 = sb("w1", P, D)
        w2 = sb("w2", P, D)
        qkvT = sb("qkvT", P, QKV)
        projT = sb("projT", P, D)
        proj_perm = sb("proj_perm", P, D)
        router_rows = sb("router_rows", NE, D)
        routerT = sb("routerT", P, NE)
        ew1_high = sb("ew1_high", P, NE, FF, dtype=F32R)
        ew1_low = sb("ew1_low", P, NE, FF, dtype=F32R)
        ew2 = sb("ew2", P, NE, NF, D)
        ident = sb("ident", P, P)
        vecs = sb("vecs", P, 18)
        vec_rows = sb("vec_rows", 14, D)
        rowv = sb("rowv", 1, 2, D)
        ones_row = sb("ones_row", 1, P)
        gb = sb("gb", P, 2, D)
        lam = sb("lam", P, 16)
        etmp = sb("etmp", P, 3, 4)
        power = sb("power", P, 4, dtype=mybir.dt.int32)
        basis = sb("basis", P, 8, 2)
        phase = sb("phase", P, 2, P)
        gphase = sb("gphase", P, 2, P)
        ptmp = sb("ptmp", P, 2, 64)
        decay = sb("decay", P, NS, P)
        minus_half = sb("minus_half", P, NS)
        rank8 = sb("rank8", P, NS, NE)

        VEC = dict(l2wS=16, l2bS=17, b0=0, b1=1, b2=2, m0=3, m1=4, w1b=5, w2b=6, l1w=7, l1b=8, l2w=9, l2b=10,
                   nu=11, theta=12, gamma=13, bo=14, bo2=15)

        def vec(name):
            return vecs[:, VEC[name]:VEC[name] + 1]

        x_in = sb("x_in", P, NS, D)
        xb = sb("xb", P, NS, D)
        xT = sb("xT", P, 2, HALF * P)
        rot = sb("rot", P, 4, HALF * P)
        drive = sb("drive", P, 2, NS, P)
        state = drive
        init = sb("init", P, 2, NS)
        ctmp = sb("ctmp", P, 2, NS)
        post = sb("post", P, 4, NS, P)
        outT = sb("outT", P, 2, HALF * P)
        outT2 = sb("outT2", P, 2, HALF * P)
        gT = sb("gT", P, 2, HALF * P)
        z = sb("z", P, NS, D)
        stA = sb("stA", P, NS, 6)
        mvA = sb("mvA", P, 3, NS)
        rsA = sb("rsA", P, 2, NS)
        stB = sb("stB", P, NS, 6)
        mvB = sb("mvB", P, 4, NS)
        rsB = sb("rsB", P, 2, 2, NS)
        x1 = sb("x1", P, NS, D)
        xh = sb("xh", P, NS, D)
        lnT = sb("lnT", P, 2, HALF * P)
        qk = sb("qk", P, NS, 160)
        vx = sb("vx", P, NS, NH * HD)
        prod = sb("prod", P, row_of[NS], NH * HD)
        scores = sb("scores", P, NS, NS, NH)
        probs = sb("probs", P, NS, NS, NH)
        smax = sb("smax", P, NS, NH)
        ssum = sb("ssum", P, NS, NH)
        srec = sb("srec", P, NS, NH)
        att = sb("att", P, NS, NH * HD)
        attT = sb("attT", P, 2, HALF * P)
        tmpS = sb("tmpS", P, 5, NS)
        h2 = sb("h2", P, NS, D)
        stC = sb("stC", P, NS, 6)
        mvC = sb("mvC", P, 3, NS)
        rsC = sb("rsC", P, 2, NS)
        xh2 = sb("xh2", P, NS, D)
        l2T = sb("l2T", P, 2, HALF * P)
        l2_scaled = sb("l2_scaled", P, HALF * P)
        l2_diff = sb("l2_diff", P, 2, HALF * P)
        l2_high = sb("l2_high", P, 2, HALF * P, dtype=F32R)
        l2_low = sb("l2_low", P, 2, HALF * P, dtype=F32R)
        rt = sb("rt", P, 6, NS, NE)
        rt1 = sb("rt1", P, 6, NS)
        gates = sb("gates", P, NS, NE)
        base = sb("base", P, NS, D)
        weighed = sb("weighed", P, HALF * P)
        res = sb("res", P, NS, D)
        hT = sb("hT", P, 2, NF, HALF * P)
        stD = sb("stD", P, NS, 6)
        mvD = sb("mvD", P, 3, NS)
        rsD = sb("rsD", P, 2, NS)

        bank = [ctx.enter_context(nc.psum_tensor(f"bank{i}", [P, 512], F32)) for i in range(8)]
        bA, bB, bC, bD, bE, bF, bG, bH = bank

        ew1_diff = post[:].rearrange("p n s t -> p (n s t)")[:, 0:NE * FF].rearrange("p (e f) -> p e f", e=NE)
        qkv_rows, proj_rows = prod[:, 32:34, :], prod[:, 34, :]
        ew1 = prod[:].rearrange("p a c -> p (a c)")[:, 0:NE * FF].rearrange("p (e f) -> p e f", e=NE)
        ew1_scaled = prod[:].rearrange("p a c -> p (a c)")[:, NE * FF:2 * NE * FF].rearrange("p (e f) -> p e f", e=NE)

        group_bank = [bH] * GROUPS
        for g in (3, 5, 7):
            group_bank[g] = bE
        group_bank[9] = bA
        for g in (11, 13, 15):
            group_bank[g] = bC

        def earlier_in_bank(g):
            return max((n for n in range(g) if group_bank[n] is group_bank[g]), default=None)

        vec_loaded = sem("vec_loaded")
        w_loaded = sem("w_loaded")
        ew1_loaded = sem("ew1_loaded")
        late_loaded = sem("late_loaded")
        ew1_split = sem("ew1_split")
        setup_pool = sem("setup_pool")
        setup_dve = sem("setup_dve")
        setup_act = sem("setup_act")
        chain = sem("chain")
        setup_pe = sem("setup_pe")
        x_loaded = signal("x_loaded", 16)
        xb_done = signal("xb_done", 1)
        xT_ps = signal("xT_ps", 2)
        xT_done = signal("xT_done", 2)
        u_ps = signal("u_ps", 2)
        rot_done = signal("rot_done", 2)
        drive_done = signal("drive_done", 4)
        inject_done = signal("inject_done", 1)
        scan_done = signal("scan_done", 2)
        carry_mul = signal("carry_mul", 2)
        carry_done = signal("carry_done", 2)
        post_done = signal("post_done", 2)
        hid_done = signal("hid_done", 4)
        out_ps = signal("out_ps", 2)
        outT_done = signal("outT_done", 4)
        z_ps = signal("z_ps", 2)
        gT_done = signal("gT_done", 2)
        y_ps = signal("y_ps", 2)
        statA = signal("statA", 2)
        partA = signal("partA", 8)
        spreadA = signal("spreadA", 4)
        meanA = signal("meanA", 2)
        rstdA = signal("rstdA", 2)
        centred = signal("centred", 2)
        z_done = signal("z_done", 2)
        statB = signal("statB", 1)
        partB = signal("partB", 4)
        spreadB = signal("spreadB", 2)
        meanB = signal("meanB", 1)
        rstdB = signal("rstdB", 2)
        shiftB = signal("shiftB", 2)
        x1_done = signal("x1_done", 2)
        xh_done = signal("xh_done", 2)
        xhT_ps = signal("xhT_ps", 2)
        lnT_done = signal("lnT_done", 2)
        qkv_ps = signal("qkv_ps", 4)
        qkv_done = signal("qkv_done", 8)
        qk_pool = signal("qk_pool", len(POOL_S))
        qk_dve = signal("qk_dve", NS - len(POOL_S))
        scores_done = signal("scores_done", NS)
        smax_done = signal("smax_done", 1)
        shift_done = signal("shift_done", 1)
        exp_done = signal("exp_done", 1)
        ssum_done = signal("ssum_done", 1)
        srec_done = signal("srec_done", 1)
        probs_done = signal("probs_done", 1)
        pv_pool = signal("pv_pool", len(POOL_S))
        pv_dve = signal("pv_dve", NS - len(POOL_S))
        att_done = signal("att_done", NS)
        attT_ps = signal("attT_ps", 2)
        attT_done = signal("attT_done", 2)
        proj_ps = signal("proj_ps", 2)
        h2_done = signal("h2_done", 2)
        statC = signal("statC", 1)
        partC = signal("partC", 4)
        spreadC = signal("spreadC", 2)
        meanC = signal("meanC", 1)
        rstdC = signal("rstdC", 1)
        shiftC = signal("shiftC", 1)
        xh2_done = signal("xh2_done", 2)
        l2_ps = signal("l2_ps", 2)
        l2T_done = signal("l2T_done", 2)
        l2S_done = signal("l2S_done", 2)
        l2_diff_done = [signal(f"l2_diff_done{q}", 1) for q in range(2)]
        l2_high_done = [signal(f"l2_high_done{q}", 1) for q in range(2)]
        l2_low_done = [signal(f"l2_low_done{q}", 1) for q in range(2)]
        logit_ps = signal("logit_ps", 1)
        gstep = signal("gstep", 13)
        top_done = signal("top_done", 1)
        lshift = signal("lshift", 1)
        gexp = signal("gexp", 1)
        two_done = signal("two_done", 1)
        both_done = signal("both_done", 1)
        gates_done = signal("gates_done", 1)
        base_done = signal("base_done", 1)
        weighed_done = signal("weighed_done", 2 * ACT_E)
        added = signal("added", 2 * ACT_E)
        h_ps = signal("h_ps", NF * GROUPS)
        hT_done = signal("hT_done", NF * GROUPS)
        moe_ps = signal("moe_ps", GROUPS)
        acc_done = signal("acc_done", 2 * (NE - ACT_E))
        statD = signal("statD", 2)
        partD = signal("partD", 8)
        spreadD = signal("spreadD", 4)
        meanD = signal("meanD", 2)
        rstdD = signal("rstdD", 2)
        shiftD = signal("shiftD", 2)
        y_done = signal("y_done", 2)
        stored = [signal(f"stored{q}", 16) for q in range(2)]

        block = ctx.enter_context(nc.Block())

        def runs(blk):
            return not isinstance(blk, int) or 0 <= blk < NB

        def pipeline(eng, warm_up, iteration, wind_down):
            for i in range(-2, 2):
                warm_up(i)
            with eng.Fori(2, NB - 2) as i:
                iteration(i)
            iteration(NB - 2)
            for i in range(NB - 1, NB + 1):
                wind_down(i)

        def tiles(q):
            return range(HALF * q, HALF * q + HALF)

        def cols(n):
            return slice(n % HALF * P, n % HALF * P + P)

        def over_tiles(table, n):
            return table.unsqueeze(1).to_broadcast([P, n, P])

        SETUP_GB = 2
        VEC_ALL = 16 * 9
        W_ALL = 16 * 10
        LATE_ALL = 16 * 2

        def qk_product(g, s):
            n = s + 1
            o = prod[:, row_of[s]:row_of[s + 1], :].rearrange("p t (r c) -> p t r c", r=REP)
            q = qk[:, s, 0:NH * HD].rearrange("p (r c) -> p r c", r=REP).unsqueeze(1).to_broadcast([P, n, REP, NKV * HD])
            kk = qk[:, 0:n, NH * HD:160].unsqueeze(2).to_broadcast([P, n, REP, NKV * HD])
            return g.tensor_tensor(o, q, kk, ALU.mult)

        def pv_product(g, s):
            n = s + 1
            o = prod[:, row_of[s]:row_of[s + 1], :].rearrange("p t (h d) -> p (t h) d", d=HD)
            pr = probs[:, s, 0:n, :].rearrange("p t h -> p (t h)").unsqueeze(2).to_broadcast([P, n * NH, HD])
            v = vx[:, 0:n, :].rearrange("p t (h d) -> p (t h) d", d=HD)
            return g.tensor_tensor(o, pr, v, ALU.mult)


        @block.sync
        def _(sp):
            def load_x(b):
                if has_earlier(b):
                    sp.wait_ge(xT_ps.sem, xT_ps.before(b, 2))
                if has_earlier(b):
                    sp.wait_ge(xb_done.sem, xb_done.before(b, 1))
                sp.dma_start(x_in[:], x[:, bass.ts(b, P), :].rearrange("s p d -> p s d")).then_inc(x_loaded.sem, 16)

            def store(k, q):
                sp.wait_ge(y_done.sem, y_done.at(k, q + 1))
                sp.dma_start(out[HALF * q:HALF * q + HALF, bass.ts(k, P), :].rearrange("s p d -> p s d"),
                             res[:, HALF * q:HALF * q + HALF, :]).then_inc(stored[q].sem, 16)

            for n, src in (("nu", plog), ("b0", b_in), ("m0", b_mid)):
                sp.dma_start(vec_rows[VEC[n]:VEC[n] + src.shape[0], :], src).then_inc(vec_loaded, 16)
            for n, src in (("w1b", w1_b), ("w2b", w2_b), ("l1w", ln1_w), ("l1b", ln1_b), ("l2w", ln2_w), ("l2b", ln2_b)):
                sp.dma_start(vec_rows[VEC[n]:VEC[n] + 1, :], src.rearrange("(a d) -> a d", a=1)).then_inc(vec_loaded, 16)
            load_x(0)
            for dst, src in (
                (win[:], W_in.rearrange("e d h -> d e h")),
                (wmid[:], W_mid.rearrange("e d h -> d e h")),
                (w1[:], w1_w), (w2[:], w2_w),
                (qkv_rows[:, 0, :], qkv_w[0:P, :]), (qkv_rows[0:QKV - P, 1, :], qkv_w[P:QKV, :]),
                (proj_rows, proj_w), (router_rows[:], router_w),
                (rowv[:, 0, :], ln_g.rearrange("(a d) -> a d", a=1)), (rowv[:, 1, :], ln_b.rearrange("(a d) -> a d", a=1)),
            ):
                sp.dma_start(dst, src).then_inc(w_loaded, 16)
            sp.dma_start(ew1, moe_w1.rearrange("e d f -> d e f")).then_inc(ew1_loaded, 16)
            for dst, src in (
                (ew2[:, 0:NE // 2], moe_w2[0:NE // 2].rearrange("e (g f) d -> f e g d", g=NF)),
                (ew2[:, NE // 2:NE], moe_w2[NE // 2:NE].rearrange("e (g f) d -> f e g d", g=NF)),
            ):
                sp.dma_start(dst, src).then_inc(late_loaded, 16)

            load_x(1)
            load_x(2)
            load_x(3)
            store(0, 0)
            store(0, 1)
            with sp.Fori(1, NB - 3) as k:
                load_x(k + 3)
                store(k, 0)
                store(k, 1)
            with sp.Fori(NB - 3, NB) as k:
                store(k, 0)
                store(k, 1)
            for q in range(2):
                sp.wait_ge(stored[q].sem, stored[q].at(NB, 0))

        @block.gpsimd
        def _(pool):
            g = nc.gpsimd
            g.memset(ident[:], 0.0).then_inc(setup_pool, 1)
            g.memset(ones_row[:], 1.0)
            g.memset(minus_half[:], -0.5)
            g.memset(init[:], 0.0)
            g.memset(scores[:], MASKED)
            for e in range(NE):
                g.memset(rank8[:, :, e:e + 1], float(NE - e))
            pool.wait_ge(setup_pool, 1)
            g.affine_select(out=ident[:], in_=ident[:], compare_op=ALU.not_equal, fill=1.0, base=0,
                            pattern=[[-1, P]], channel_multiplier=1).then_inc(setup_pool, 1)

            def sum_xb(b):
                pool.wait_ge(x_loaded.sem, x_loaded.at(b, 16))
                if has_earlier(b):
                    pool.wait_ge(z_done.sem, z_done.before(b, 2))
                if isinstance(b, int) and b == 0:
                    pool.wait_ge(setup_act, SETUP_GB)
                g.tensor_tensor(xb[:], x_in[:], over_tiles(gb[:, 1, :], NS), ALU.add).then_inc(xb_done.sem, 1)

            def sum_drive(b, q):
                pool.wait_ge(rot_done.sem, rot_done.at(b, q + 1))
                if has_earlier(b):
                    pool.wait_ge(carry_done.sem, carry_done.before(b, 2))
                    pool.wait_ge(post_done.sem, post_done.before(b, 2))
                t = slice(HALF * q, HALF * q + HALF)
                r = [rot[:, n, :].rearrange("p (s t) -> p s t", t=P) for n in range(4)]
                g.tensor_tensor(drive[:, 0, t, :], r[0], r[1], ALU.add).then_inc(drive_done.sem, 1)
                g.tensor_tensor(drive[:, 1, t, :], r[2], r[3], ALU.subtract).then_inc(drive_done.sem, 1)

            def sum_hid(b, q):
                pool.wait_ge(post_done.sem, post_done.at(b, q + 1))
                t = slice(HALF * q, HALF * q + HALF)
                g.tensor_tensor(post[:, 0, t, :], post[:, 0, t, :], post[:, 1, t, :], ALU.subtract).then_inc(hid_done.sem, 1)
                g.tensor_tensor(post[:, 2, t, :], post[:, 2, t, :], post[:, 3, t, :], ALU.add).then_inc(hid_done.sem, 1)

            def rstd(mean_sig, rstd_sig, mv, rs, blk, k, t):
                pool.wait_ge(mean_sig.sem, mean_sig.at(blk, k))
                g.tensor_tensor(rs[:, 0, t], mv[:, 2, t], minus_half[:, t], ALU.pow).then_inc(rstd_sig.sem, 1)

            def shift(rstd_sig, shift_sig, mv, rs, blk, k, t):
                pool.wait_ge(rstd_sig.sem, rstd_sig.at(blk, k))
                g.tensor_tensor(rs[:, 1, t], mv[:, 0, t], rs[:, 0, t], ALU.mult).then_inc(shift_sig.sem, 1)

            def rstd_b(b, n):
                pool.wait_ge(meanB.sem, meanB.at(b, 1))
                g.tensor_tensor(rsB[:, 0, n], mvB[:, 2 + n, :], minus_half[:], ALU.pow).then_inc(rstdB.sem, 1)

            def shift_b(b, n):
                pool.wait_ge(rstdB.sem, rstdB.at(b, 2 - n))
                g.tensor_tensor(rsB[:, 1, n], rsB[:, 0, n], mvB[:, 0, :], ALU.mult).then_inc(shiftB.sem, 1)

            def qk_products(j):
                pool.wait_ge(qkv_done.sem, qkv_done.at(j, 8))
                if has_earlier(j):
                    pool.wait_ge(att_done.sem, att_done.before(j, NS))
                for s in POOL_S:
                    qk_product(g, s).then_inc(qk_pool.sem, 1)

            def pv_products(j):
                pool.wait_ge(probs_done.sem, probs_done.at(j, 1))
                pool.wait_ge(scores_done.sem, scores_done.at(j, NS))
                for s in POOL_S:
                    pv_product(g, s).then_inc(pv_pool.sem, 1)

            def sum_base(j):
                pool.wait_ge(h2_done.sem, h2_done.at(j, 2))
                pool.wait_ge(x1_done.sem, x1_done.at(j, 2))
                if has_earlier(j):
                    pool.wait_ge(acc_done.sem, acc_done.before(j, NE - ACT_E + 1))
                g.tensor_tensor(base[:], x1[:], h2[:], ALU.add).then_inc(base_done.sem, 1)

            def split_l2(k):
                pool.wait_ge(l2S_done.sem, l2S_done.at(k, 2))
                if has_earlier(k):
                    pool.wait_ge(h_ps.sem, h_ps.before(k, NF * GROUPS))
                g.tensor_tensor(l2_diff[:, 1, :], l2_scaled[:], l2T[:, 1, :], ALU.subtract).then_inc(l2_diff_done[1].sem, 1)
                pool.wait_ge(l2_diff_done[1].sem, l2_diff_done[1].at(k, 1))
                g.tensor_tensor(l2_high[:, 1, :], l2_scaled[:], l2_diff[:, 1, :], ALU.subtract).then_inc(l2_high_done[1].sem, 1)
                pool.wait_ge(l2_high_done[1].sem, l2_high_done[1].at(k, 1))
                g.tensor_tensor(l2_low[:, 1, :], l2T[:, 1, :], l2_high[:, 1, :].bitcast(F32), ALU.subtract).then_inc(l2_low_done[1].sem, 1)

            def add_weighed(k, n):
                q, e = divmod(n, ACT_E)
                pool.wait_ge(weighed_done.sem, weighed_done.at(k, n + 1))
                if e:
                    pool.wait_ge(added.sem, added.at(k, n))
                else:
                    pool.wait_ge(base_done.sem, base_done.at(k, 1))
                half = base[:, HALF * q:HALF * q + HALF, :].rearrange("p s d -> p (s d)")
                g.tensor_tensor(half, half, weighed[:], ALU.add).then_inc(added.sem, 1)

            def warm_up(i):
                if runs(i + 1):
                    sum_drive(i + 1, 0)
                    sum_xb(i + 1)
                    sum_drive(i + 1, 1)
                if runs(i - 1):
                    add_weighed(i - 1, 0)
                if runs(i + 1):
                    sum_hid(i + 1, 0)
                if runs(i - 1):
                    add_weighed(i - 1, 1)
                if runs(i + 1):
                    sum_hid(i + 1, 1)
                if runs(i - 1):
                    split_l2(i - 1)
                if runs(i):
                    qk_products(i)
                    pv_products(i)
                if runs(i - 1):
                    rstd(meanD, rstdD, mvD, rsD, i - 1, 1, slice(0, HALF))
                    add_weighed(i - 1, 2)
                    shift(rstdD, shiftD, mvD, rsD, i - 1, 1, slice(0, HALF))
                if runs(i + 1):
                    rstd(meanA, rstdA, mvA, rsA, i + 1, 1, slice(0, HALF))
                    rstd(meanA, rstdA, mvA, rsA, i + 1, 2, slice(HALF, NS))
                if runs(i - 1):
                    add_weighed(i - 1, 3)
                if runs(i + 1):
                    rstd_b(i + 1, 1)
                    shift_b(i + 1, 1)
                    rstd_b(i + 1, 0)
                if runs(i):
                    rstd(meanC, rstdC, mvC, rsC, i, 1, slice(0, NS))
                    shift(rstdC, shiftC, mvC, rsC, i, 1, slice(0, NS))
                if runs(i + 1):
                    shift_b(i + 1, 0)
                if runs(i):
                    sum_base(i)
                if runs(i - 1):
                    rstd(meanD, rstdD, mvD, rsD, i - 1, 2, slice(HALF, NS))
                    shift(rstdD, shiftD, mvD, rsD, i - 1, 2, slice(HALF, NS))

            def iteration(i):
                if runs(i + 1):
                    sum_drive(i + 1, 0)
                    sum_drive(i + 1, 1)
                if runs(i - 1):
                    add_weighed(i - 1, 0)
                    add_weighed(i - 1, 1)
                if runs(i + 1):
                    sum_xb(i + 1)
                    sum_hid(i + 1, 0)
                    sum_hid(i + 1, 1)
                if runs(i - 1):
                    split_l2(i - 1)
                if runs(i):
                    qk_products(i)
                    pv_products(i)
                if runs(i - 1):
                    add_weighed(i - 1, 2)
                if runs(i + 1):
                    rstd(meanA, rstdA, mvA, rsA, i + 1, 1, slice(0, HALF))
                if runs(i - 1):
                    rstd(meanD, rstdD, mvD, rsD, i - 1, 1, slice(0, HALF))
                    shift(rstdD, shiftD, mvD, rsD, i - 1, 1, slice(0, HALF))
                if runs(i + 1):
                    rstd(meanA, rstdA, mvA, rsA, i + 1, 2, slice(HALF, NS))
                if runs(i - 1):
                    add_weighed(i - 1, 3)
                if runs(i + 1):
                    rstd_b(i + 1, 1)
                    rstd_b(i + 1, 0)
                    shift_b(i + 1, 1)
                    shift_b(i + 1, 0)
                if runs(i):
                    sum_base(i)
                    rstd(meanC, rstdC, mvC, rsC, i, 1, slice(0, NS))
                    shift(rstdC, shiftC, mvC, rsC, i, 1, slice(0, NS))
                if runs(i - 1):
                    rstd(meanD, rstdD, mvD, rsD, i - 1, 2, slice(HALF, NS))
                    shift(rstdD, shiftD, mvD, rsD, i - 1, 2, slice(HALF, NS))

            def wind_down(i):
                if runs(i - 1):
                    split_l2(i - 1)
                    add_weighed(i - 1, 0)
                    add_weighed(i - 1, 1)
                if runs(i):
                    qk_products(i)
                    pv_products(i)
                if runs(i - 1):
                    rstd(meanD, rstdD, mvD, rsD, i - 1, 1, slice(0, HALF))
                    shift(rstdD, shiftD, mvD, rsD, i - 1, 1, slice(0, HALF))
                    add_weighed(i - 1, 2)
                    add_weighed(i - 1, 3)
                if runs(i):
                    rstd(meanC, rstdC, mvC, rsC, i, 1, slice(0, NS))
                    shift(rstdC, shiftC, mvC, rsC, i, 1, slice(0, NS))
                if runs(i - 1):
                    rstd(meanD, rstdD, mvD, rsD, i - 1, 2, slice(HALF, NS))
                    shift(rstdD, shiftD, mvD, rsD, i - 1, 2, slice(HALF, NS))
                if runs(i):
                    sum_base(i)

            pool.wait_ge(ew1_split, 1)
            g.tensor_tensor(ew1_diff, ew1_scaled, ew1, ALU.subtract).then_inc(ew1_split, 1)
            pool.wait_ge(ew1_split, 2)
            g.tensor_tensor(ew1_high[:], ew1_scaled, ew1_diff, ALU.subtract).then_inc(ew1_split, 1)
            pool.wait_ge(ew1_split, 3)
            g.tensor_tensor(ew1_low[:], ew1, ew1_high[:].bitcast(F32), ALU.subtract).then_inc(ew1_split, 1)

            pipeline(pool, warm_up, iteration, wind_down)

        @block.vector
        def _(dve):
            v = nc.vector
            steps = [0]

            def link(ins):
                ins.then_inc(chain, 1)
                steps[0] += 1
                dve.wait_ge(chain, steps[0])

            def links(*ins):
                for one in ins[:-1]:
                    one()
                link(ins[-1]())

            dve.wait_ge(setup_pe, 1)
            link(v.tensor_copy(vecs[:, 0:14], bF[:, 0:14]))
            link(v.tensor_tensor(vec("bo"), vec("m0"), vec("m1"), ALU.subtract))
            link(v.tensor_tensor(vec("bo"), vec("bo"), vec("b2"), ALU.add))
            v.tensor_scalar(vecs[:, 16:18], vecs[:, VEC["l2w"]:VEC["l2b"] + 1], SPLIT, None, ALU.mult)
            v.tensor_tensor(vec("bo2"), vec("bo"), vec("w2b"), ALU.add).then_inc(setup_dve, 1)

            def exp_steps(dst, src, n, tmp):
                arg, turns, series = (etmp[:, m, tmp:tmp + n] for m in range(3))
                bits = power[:, tmp:tmp + n]
                yield lambda: v.tensor_scalar(arg, src, 88.0, -86.0, ALU.min, ALU.max)
                yield lambda: v.tensor_scalar(turns, arg, 1.4426950408889634, None, ALU.mult)
                yield lambda: v.tensor_scalar(turns, turns, ROUND, None, ALU.add)
                yield lambda: v.tensor_scalar(turns, turns, ROUND, None, ALU.subtract)
                yield lambda: v.scalar_tensor_tensor(arg, turns, -LN2_HI, arg, ALU.mult, ALU.add)
                yield lambda: v.scalar_tensor_tensor(arg, turns, -LN2_LO, arg, ALU.mult, ALU.add)
                yield lambda: v.tensor_scalar(series, arg, 1.0 / math.factorial(7), None, ALU.mult)
                for m in range(6, 0, -1):
                    yield lambda m=m: v.scalar_tensor_tensor(series, series, 1.0 / math.factorial(m), arg, ALU.add, ALU.mult)
                yield lambda: v.tensor_scalar(turns, turns, 127.0, 8388608.0, ALU.add, ALU.mult)
                yield lambda: v.tensor_copy(bits, turns)
                yield lambda: v.scalar_tensor_tensor(dst, series, 1.0, bits.bitcast(F32), ALU.add, ALU.mult)

            nu, theta, gamma, r = (lam[:, n:n + 1] for n in range(4))
            turns, angle, square = (lam[:, n:n + 1] for n in (5, 6, 7))
            sine, cosm1, double, sine1 = (lam[:, n:n + 1] for n in (8, 9, 10, 11))

            def r_steps():
                yield lambda: v.tensor_scalar(lam[:, 4:5], nu, -1.0, None, ALU.mult)
                yield from exp_steps(r, lam[:, 4:5], 1, 3)
                yield lambda: v.memset(decay[:], 1.0)
                yield lambda: v.tensor_scalar(decay[:], decay[:], r, None, ALU.mult)
                yield lambda: v.memset(decay[:, :, 0:1], 0.0)

            def series_steps(dst, first):
                sign = 1.0 if first % 4 in (0, 1) else -1.0
                yield lambda: v.tensor_scalar(dst, square, sign / math.factorial(first), None, ALU.mult)
                for m in range(first - 2, 1, -2):
                    sign = 1.0 if m % 4 in (0, 1) else -1.0
                    yield lambda c=sign / math.factorial(m): v.scalar_tensor_tensor(dst, dst, c, square, ALU.add, ALU.mult)

            def phase_steps():
                yield (lambda: v.tensor_scalar(turns, theta, 0.15915494309189535, None, ALU.mult),)
                yield (lambda: v.tensor_scalar(turns, turns, ROUND, None, ALU.add),)
                yield (lambda: v.tensor_scalar(turns, turns, ROUND, None, ALU.subtract),)
                yield (lambda: v.scalar_tensor_tensor(theta, turns, -TWO_PI_HI, theta, ALU.mult, ALU.add),)
                yield (lambda: v.scalar_tensor_tensor(theta, turns, -TWO_PI_MID, theta, ALU.mult, ALU.add),)
                yield (lambda: v.scalar_tensor_tensor(theta, turns, -TWO_PI_LO, theta, ALU.mult, ALU.add),)
                yield (lambda: v.tensor_scalar(angle, theta, 0.125, None, ALU.mult),)
                yield (lambda: v.tensor_tensor(square, angle, angle, ALU.mult),)
                for pair in zip(series_steps(cosm1, 10), [*series_steps(sine, 9), None]):
                    yield tuple(p for p in pair if p)
                yield (lambda: v.scalar_tensor_tensor(sine, sine, 1.0, angle, ALU.add, ALU.mult),)
                for _ in range(3):
                    yield (lambda: v.scalar_tensor_tensor(double, sine, -2.0, sine, ALU.mult, ALU.mult),
                           lambda: v.scalar_tensor_tensor(sine1, cosm1, 1.0, sine, ALU.add, ALU.mult))
                    yield (lambda: v.tensor_scalar(sine, sine1, 2.0, None, ALU.mult),
                           lambda: v.tensor_copy(cosm1, double))
                yield (lambda: v.memset(phase[:, 0, 0:1], 1.0), lambda: v.memset(phase[:, 1, 0:1], 0.0),
                       lambda: v.tensor_scalar(basis[:, 0, 0:1], cosm1, 1.0, None, ALU.add),
                       lambda: v.tensor_copy(basis[:, 0, 1:2], sine))
                for n in range(7):
                    m = 2 ** n
                    c, s = basis[:, n, 0:1], basis[:, n, 1:2]
                    cc, ss = phase[:, 0, 0:m], phase[:, 1, 0:m]
                    yield (lambda: v.tensor_scalar(ptmp[:, 0, 0:m], ss, s, None, ALU.mult),
                           lambda: v.tensor_scalar(ptmp[:, 1, 0:m], cc, s, None, ALU.mult),
                           lambda: v.tensor_scalar(lam[:, 12:14], basis[:, n, :], s, None, ALU.mult))
                    yield (lambda: v.scalar_tensor_tensor(phase[:, 0, m:2 * m], cc, c, ptmp[:, 0, 0:m], ALU.mult, ALU.subtract),
                           lambda: v.scalar_tensor_tensor(phase[:, 1, m:2 * m], ss, c, ptmp[:, 1, 0:m], ALU.mult, ALU.add),
                           lambda: v.scalar_tensor_tensor(basis[:, n + 1, 0:1], c, c, lam[:, 13:14], ALU.mult, ALU.subtract),
                           lambda: v.scalar_tensor_tensor(basis[:, n + 1, 1:2], s, c, lam[:, 12:13], ALU.mult, ALU.add))
                yield (lambda: v.tensor_scalar(gphase[:], phase[:], gamma, None, ALU.mult),)

            for one in exp_steps(lam[:, 0:3], vecs[:, 11:14], 3, 0):
                link(one())
            radius = [*r_steps()]
            for n, now in enumerate(phase_steps()):
                links(*radius[n:n + 1], *now)

            dve.wait_ge(setup_pool, 2)
            dve.wait_ge(setup_act, SETUP_GB)
            turn_c, turn_s = basis[:, 7, 0:1], basis[:, 7, 1:2]

            def rotate_in(b, q):
                dve.wait_ge(u_ps.sem, u_ps.at(b, q + 1))
                if q == 0:
                    if has_earlier(b):
                        dve.wait_ge(drive_done.sem, drive_done.before(b, 4))
                else:
                    dve.wait_ge(drive_done.sem, drive_done.at(b, 2))
                gc, gs = (over_tiles(gphase[:, n, :], HALF) for n in range(2))
                ur, ui = (bk[:].rearrange("p (s t) -> p s t", t=P) for bk in (bB, bC))
                o = [rot[:, n, :].rearrange("p (s t) -> p s t", t=P) for n in range(4)]
                v.scalar_tensor_tensor(o[0], ur, vec("b0"), gc, ALU.add, ALU.mult)
                v.scalar_tensor_tensor(o[1], ui, vec("b1"), gs, ALU.add, ALU.mult)
                v.scalar_tensor_tensor(o[2], ui, vec("b1"), gc, ALU.add, ALU.mult)
                v.scalar_tensor_tensor(o[3], ur, vec("b0"), gs, ALU.add, ALU.mult).then_inc(rot_done.sem, 1)

            def inject(b):
                dve.wait_ge(drive_done.sem, drive_done.at(b, 4))
                if has_earlier(b):
                    dve.wait_ge(carry_done.sem, carry_done.before(b, 2))
                first = drive[:, :, :, 0]
                v.scalar_tensor_tensor(first, init[:], r, first, ALU.mult, ALU.add).then_inc(inject_done.sem, 1)

            def scan(b, part):
                if part == 0:
                    dve.wait_ge(inject_done.sem, inject_done.at(b, 1))
                v.tensor_tensor_scan(state[:, part].rearrange("p s t -> p (s t)"), decay[:].rearrange("p s t -> p (s t)"),
                                     drive[:, part].rearrange("p s t -> p (s t)"), 0.0, ALU.mult, ALU.add).then_inc(scan_done.sem, 1)

            def carry(b):
                dve.wait_ge(scan_done.sem, scan_done.at(b, 2))
                re, im = state[:, 0, :, P - 1], state[:, 1, :, P - 1]
                v.tensor_scalar(ctmp[:, 0, :], im, turn_s, None, ALU.mult).then_inc(carry_mul.sem, 1)
                v.tensor_scalar(ctmp[:, 1, :], re, turn_s, None, ALU.mult).then_inc(carry_mul.sem, 1)
                dve.wait_ge(carry_mul.sem, carry_mul.at(b, 2))
                v.scalar_tensor_tensor(init[:, 0, :], re, turn_c, ctmp[:, 0, :], ALU.mult, ALU.subtract).then_inc(carry_done.sem, 1)
                v.scalar_tensor_tensor(init[:, 1, :], im, turn_c, ctmp[:, 1, :], ALU.mult, ALU.add).then_inc(carry_done.sem, 1)

            def rotate_out(b, q):
                if q == 0:
                    if has_earlier(b):
                        dve.wait_ge(out_ps.sem, out_ps.before(b, 2))
                t = slice(HALF * q, HALF * q + HALF)
                c, s = (over_tiles(phase[:, n, :], HALF) for n in range(2))
                re, im = state[:, 0, t, :], state[:, 1, t, :]
                v.tensor_tensor(post[:, 0, t, :], re, c, ALU.mult)
                v.tensor_tensor(post[:, 1, t, :], im, s, ALU.mult)
                v.tensor_tensor(post[:, 2, t, :], re, s, ALU.mult)
                v.tensor_tensor(post[:, 3, t, :], im, c, ALU.mult).then_inc(post_done.sem, 1)

            def stats(src, st, mv, sigs, blk, k, ts, twice=False):
                stat_sig, part_sig, spread_sig, mean_sig = sigs
                for n in ts:
                    last = v.bn_stats(st[:, n, :], src(n))
                last.then_inc(stat_sig.sem, 1)
                t = slice(ts[0], ts[-1] + 1)
                total, gap, dev, gap2, dev_eps = (tmpS[:, m, t] for m in range(5))
                dve.wait_ge(stat_sig.sem, stat_sig.at(blk, k))
                v.tensor_tensor(gap, st[:, t, 1], st[:, t, 4], ALU.subtract).then_inc(part_sig.sem, 1)
                v.tensor_tensor(dev, st[:, t, 2], st[:, t, 5], ALU.add).then_inc(part_sig.sem, 1)
                v.tensor_tensor(total, st[:, t, 1], st[:, t, 4], ALU.add).then_inc(part_sig.sem, 1)
                dve.wait_ge(part_sig.sem, part_sig.at(blk, 4 * k - 1))
                v.scalar_tensor_tensor(gap2, gap, 0.25, gap, ALU.mult, ALU.mult).then_inc(spread_sig.sem, 1)
                v.tensor_scalar(dev_eps, dev, 1.0 / D, EPS, ALU.mult, ALU.add).then_inc(spread_sig.sem, 1)
                v.tensor_scalar(mv[:, 0, t], total, -0.5, None, ALU.mult)
                dve.wait_ge(spread_sig.sem, spread_sig.at(blk, 2 * k))
                v.scalar_tensor_tensor(mv[:, 1, t], dev, 1.0 / D, gap2, ALU.mult, ALU.add).then_inc(part_sig.sem, 1)
                if twice:
                    v.tensor_tensor(mv[:, 2, t], dev_eps, gap2, ALU.add)
                    dve.wait_ge(part_sig.sem, part_sig.at(blk, 4 * k))
                    v.tensor_scalar(mv[:, 3, t], mv[:, 1, t], 1.0 + EPS, EPS * EPS, ALU.mult, ALU.add).then_inc(mean_sig.sem, 1)
                else:
                    v.tensor_tensor(mv[:, 2, t], dev_eps, gap2, ALU.add).then_inc(mean_sig.sem, 1)

            def mean_a(b, q):
                dve.wait_ge(y_ps.sem, y_ps.at(b, q + 1))
                bk = (bB, bC)[q]
                stats(lambda n: bk[:, cols(n)], stA, mvA, (statA, partA, spreadA, meanA), b, q + 1, tiles(q))

            def centre(b, q):
                if has_earlier(b) and q == 0:
                    dve.wait_ge(xh_done.sem, xh_done.before(b, 2))
                    dve.wait_ge(x1_done.sem, x1_done.before(b, 2))
                bk = (bB, bC)[q]
                dve.wait_ge(meanA.sem, meanA.at(b, q + 1))
                for n in tiles(q):
                    last = v.scalar_tensor_tensor(z[:, n, :], bk[:, cols(n)], mvA[:, 0, n:n + 1], gb[:, 0, :],
                                                  ALU.add, ALU.mult)
                last.then_inc(centred.sem, 1)

            def finish_a(b, q):
                dve.wait_ge(rstdA.sem, rstdA.at(b, q + 1))
                dve.wait_ge(centred.sem, centred.at(b, q + 1))
                dve.wait_ge(xb_done.sem, xb_done.at(b, 1))
                for n in tiles(q):
                    last = v.scalar_tensor_tensor(z[:, n, :], z[:, n, :], rsA[:, 0, n:n + 1], xb[:, n, :],
                                                  ALU.mult, ALU.add)
                last.then_inc(z_done.sem, 1)

            def mean_b(b):
                dve.wait_ge(z_done.sem, z_done.at(b, 2))
                stats(lambda n: z[:, n, :], stB, mvB, (statB, partB, spreadB, meanB), b, 1, range(NS), True)

            def qk_products(j, s):
                dve.wait_ge(qkv_done.sem, qkv_done.at(j, 8))
                qk_product(v, s).then_inc(qk_dve.sem, 1)

            def sum_scores(j, s):
                if s in DVE_S:
                    dve.wait_ge(qk_dve.sem, qk_dve.at(j, s - DVE_S[0] + 1))
                else:
                    dve.wait_ge(qk_pool.sem, qk_pool.at(j, s + 1))
                v.tensor_reduce(scores[:, s, 0:s + 1, :].rearrange("p t h -> p (t h)"),
                                prod[:, row_of[s]:row_of[s + 1], :].rearrange("p t (h d) -> p (t h) d", d=HD),
                                AX.X, ALU.add).then_inc(scores_done.sem, 1)

            def softmax_in(j):
                dve.wait_ge(scores_done.sem, scores_done.at(j, NS))
                v.tensor_reduce(smax[:], scores[:].rearrange("p s t h -> p s h t"), AX.X, ALU.max).then_inc(smax_done.sem, 1)
                dve.wait_ge(smax_done.sem, smax_done.at(j, 1))
                if has_earlier(j):
                    dve.wait_ge(pv_pool.sem, pv_pool.before(j, len(POOL_S)))
                v.tensor_tensor(probs[:], scores[:], smax[:].unsqueeze(2).to_broadcast([P, NS, NS, NH]),
                                ALU.subtract).then_inc(shift_done.sem, 1)

            def softmax_out(j):
                dve.wait_ge(exp_done.sem, exp_done.at(j, 1))
                v.tensor_reduce(ssum[:], probs[:].rearrange("p s t h -> p s h t"), AX.X, ALU.add).then_inc(ssum_done.sem, 1)
                dve.wait_ge(ssum_done.sem, ssum_done.at(j, 1))
                v.reciprocal(srec[:], ssum[:]).then_inc(srec_done.sem, 1)
                dve.wait_ge(srec_done.sem, srec_done.at(j, 1))
                v.tensor_tensor(probs[:], probs[:], srec[:].unsqueeze(2).to_broadcast([P, NS, NS, NH]),
                                ALU.mult).then_inc(probs_done.sem, 1)

            def pv_products(j, s):
                dve.wait_ge(probs_done.sem, probs_done.at(j, 1))
                pv_product(v, s).then_inc(pv_dve.sem, 1)

            def sum_pv(j, s):
                if has_earlier(j):
                    dve.wait_ge(attT_ps.sem, attT_ps.before(j, 2))
                if s in DVE_S:
                    dve.wait_ge(pv_dve.sem, pv_dve.at(j, s - DVE_S[0] + 1))
                else:
                    dve.wait_ge(pv_pool.sem, pv_pool.at(j, s + 1))
                v.tensor_reduce(att[:, s, :], prod[:, row_of[s]:row_of[s + 1], :].rearrange("p t c -> p c t"),
                                AX.X, ALU.add).then_inc(att_done.sem, 1)

            def residual(j, q):
                if has_earlier(j):
                    dve.wait_ge(base_done.sem, base_done.before(j, 1))
                    dve.wait_ge(xh2_done.sem, xh2_done.before(j, 2))
                dve.wait_ge(x1_done.sem, x1_done.at(j, 2))
                dve.wait_ge(proj_ps.sem, proj_ps.at(j, q + 1))
                t = slice(HALF * q, HALF * q + HALF)
                v.tensor_tensor(h2[:, t, :], (bD, bE)[q][:].rearrange("p (s t) -> p s t", t=P), x1[:, t, :],
                                ALU.add).then_inc(h2_done.sem, 1)

            def mean_c(j):
                dve.wait_ge(h2_done.sem, h2_done.at(j, 2))
                stats(lambda n: h2[:, n, :], stC, mvC, (statC, partC, spreadC, meanC), j, 1, range(NS))

            def top_logit(j):
                dve.wait_ge(logit_ps.sem, logit_ps.at(j, 1))
                v.tensor_reduce(rt1[:, 0], bA[:, 0:NS * NE].rearrange("p (s e) -> p s e", e=NE), AX.X,
                                ALU.max).then_inc(top_done.sem, 1)
                dve.wait_ge(top_done.sem, top_done.at(j, 1))
                v.tensor_tensor(rt[:, 0], bA[:, 0:NS * NE].rearrange("p (s e) -> p s e", e=NE),
                                rt1[:, 0].unsqueeze(2).to_broadcast([P, NS, NE]), ALU.subtract).then_inc(lshift.sem, 1)

            def gate(j):
                count = [0]

                def step(ins):
                    ins.then_inc(gstep.sem, 1)
                    count[0] += 1
                    dve.wait_ge(gstep.sem, gstep.at(j, count[0]))

                def per_tile(a):
                    return a.unsqueeze(2).to_broadcast([P, NS, NE])

                pr, key, one, two, left = (rt[:, n] for n in range(5))
                total, inv, best, second, k2 = (rt1[:, n] for n in range(1, 6))
                dve.wait_ge(gexp.sem, gexp.at(j, 1))
                step(v.tensor_reduce(total, pr, AX.X, ALU.add))
                step(v.reciprocal(inv, total))
                step(v.tensor_tensor(pr, pr, per_tile(inv), ALU.mult))
                for src, winner, m, kk in ((pr, one, best, k2), (left, two, second, k2)):
                    step(v.tensor_reduce(m, src, AX.X, ALU.max))
                    step(v.tensor_tensor(key, src, per_tile(m), ALU.is_equal))
                    step(v.tensor_tensor(key, key, rank8[:], ALU.mult))
                    step(v.tensor_reduce(kk, key, AX.X, ALU.max))
                    if winner is one:
                        step(v.tensor_tensor(one, key, per_tile(kk), ALU.is_equal))
                        step(v.scalar_tensor_tensor(left, one, -2.0, pr, ALU.mult, ALU.add))
                v.tensor_tensor(two, key, per_tile(k2), ALU.is_equal).then_inc(two_done.sem, 1)
                dve.wait_ge(two_done.sem, two_done.at(j, 1))
                v.tensor_tensor(one, one, two, ALU.add).then_inc(both_done.sem, 1)
                dve.wait_ge(both_done.sem, both_done.at(j, 1))
                v.tensor_tensor(gates[:], pr, one, ALU.mult).then_inc(gates_done.sem, 1)

            def accumulate(k, g):
                q, e = divmod(g, NE)
                n_done = q * (NE - ACT_E) + e - ACT_E
                dve.wait_ge(moe_ps.sem, moe_ps.at(k, g + 1))
                if e == ACT_E:
                    dve.wait_ge(added.sem, added.at(k, ACT_E * (q + 1)))
                    if has_earlier(k):
                        dve.wait_ge(stored[q].sem, stored[q].before(k, 16))
                else:
                    dve.wait_ge(acc_done.sem, acc_done.at(k, n_done))
                so_far = base if e == ACT_E else res
                for n in tiles(q):
                    last = v.scalar_tensor_tensor(res[:, n, :], group_bank[g][:, cols(n)], gates[:, n, e:e + 1], so_far[:, n, :],
                                                  ALU.mult, ALU.add)
                last.then_inc(acc_done.sem, 1)

            def split_l2(k):
                dve.wait_ge(l2S_done.sem, l2S_done.at(k, 1))
                if has_earlier(k):
                    dve.wait_ge(h_ps.sem, h_ps.before(k, NF * NE))
                v.tensor_tensor(l2_diff[:, 0, :], l2_scaled[:], l2T[:, 0, :], ALU.subtract).then_inc(l2_diff_done[0].sem, 1)
                dve.wait_ge(l2_diff_done[0].sem, l2_diff_done[0].at(k, 1))
                v.tensor_tensor(l2_high[:, 0, :], l2_scaled[:], l2_diff[:, 0, :], ALU.subtract).then_inc(l2_high_done[0].sem, 1)
                dve.wait_ge(l2_high_done[0].sem, l2_high_done[0].at(k, 1))
                v.tensor_tensor(l2_low[:, 0, :], l2T[:, 0, :], l2_high[:, 0, :].bitcast(F32), ALU.subtract).then_inc(l2_low_done[0].sem, 1)

            def mean_d(k, q):
                dve.wait_ge(acc_done.sem, acc_done.at(k, (NE - ACT_E) * (q + 1)))
                stats(lambda n: res[:, n, :], stD, mvD, (statD, partD, spreadD, meanD), k, q + 1, tiles(q))

            def warm_up(i):
                if runs(i - 1):
                    split_l2(i - 1)
                if runs(i + 1):
                    rotate_in(i + 1, 0)
                if runs(i - 1):
                    top_logit(i - 1)
                    gate(i - 1)
                if runs(i + 1):
                    rotate_in(i + 1, 1)
                    inject(i + 1)
                    scan(i + 1, 0)
                    scan(i + 1, 1)
                    carry(i + 1)
                    rotate_out(i + 1, 0)
                    rotate_out(i + 1, 1)
                if runs(i - 1):
                    accumulate(i - 1, 2)
                if runs(i):
                    qk_products(i, 5)
                    qk_products(i, 6)
                    qk_products(i, 7)
                    sum_scores(i, 6)
                if runs(i - 1):
                    accumulate(i - 1, 3)
                if runs(i):
                    sum_scores(i, 7)
                    sum_scores(i, 5)
                    sum_scores(i, 1)
                if runs(i - 1):
                    accumulate(i - 1, 4)
                if runs(i):
                    sum_scores(i, 3)
                    sum_scores(i, 4)
                    sum_scores(i, 0)
                    sum_scores(i, 2)
                if runs(i - 1):
                    accumulate(i - 1, 5)
                if runs(i):
                    softmax_in(i)
                if runs(i - 1):
                    accumulate(i - 1, 6)
                if runs(i):
                    softmax_out(i)
                    pv_products(i, 5)
                    pv_products(i, 6)
                    sum_pv(i, 5)
                    pv_products(i, 7)
                if runs(i + 1):
                    mean_a(i + 1, 0)
                if runs(i - 1):
                    accumulate(i - 1, 7)
                if runs(i):
                    sum_pv(i, 0)
                    sum_pv(i, 4)
                    sum_pv(i, 2)
                    sum_pv(i, 7)
                    sum_pv(i, 6)
                    sum_pv(i, 3)
                if runs(i - 1):
                    mean_d(i - 1, 0)
                if runs(i):
                    sum_pv(i, 1)
                if runs(i + 1):
                    mean_a(i + 1, 1)
                    centre(i + 1, 0)
                    centre(i + 1, 1)
                    finish_a(i + 1, 0)
                if runs(i):
                    residual(i, 0)
                    residual(i, 1)
                if runs(i + 1):
                    finish_a(i + 1, 1)
                    mean_b(i + 1)
                if runs(i - 1):
                    accumulate(i - 1, 10)
                    accumulate(i - 1, 11)
                    accumulate(i - 1, 12)
                if runs(i):
                    mean_c(i)
                if runs(i - 1):
                    accumulate(i - 1, 13)
                    accumulate(i - 1, 14)
                    accumulate(i - 1, 15)
                    mean_d(i - 1, 1)

            def iteration(i):
                if runs(i - 1):
                    split_l2(i - 1)
                if runs(i + 1):
                    rotate_in(i + 1, 0)
                if runs(i - 1):
                    top_logit(i - 1)
                    gate(i - 1)
                if runs(i + 1):
                    rotate_in(i + 1, 1)
                    inject(i + 1)
                    scan(i + 1, 0)
                    scan(i + 1, 1)
                    carry(i + 1)
                    rotate_out(i + 1, 0)
                    rotate_out(i + 1, 1)
                if runs(i):
                    qk_products(i, 5)
                if runs(i - 1):
                    accumulate(i - 1, 2)
                if runs(i):
                    qk_products(i, 6)
                    qk_products(i, 7)
                    sum_scores(i, 6)
                    sum_scores(i, 7)
                    sum_scores(i, 2)
                if runs(i - 1):
                    accumulate(i - 1, 3)
                if runs(i):
                    sum_scores(i, 3)
                if runs(i - 1):
                    accumulate(i - 1, 4)
                if runs(i):
                    sum_scores(i, 4)
                    sum_scores(i, 1)
                    sum_scores(i, 5)
                    sum_scores(i, 0)
                if runs(i - 1):
                    accumulate(i - 1, 5)
                if runs(i):
                    softmax_in(i)
                if runs(i - 1):
                    accumulate(i - 1, 6)
                if runs(i):
                    softmax_out(i)
                    pv_products(i, 5)
                    pv_products(i, 6)
                    sum_pv(i, 5)
                    sum_pv(i, 2)
                if runs(i - 1):
                    accumulate(i - 1, 7)
                if runs(i):
                    pv_products(i, 7)
                    sum_pv(i, 6)
                    sum_pv(i, 3)
                    sum_pv(i, 7)
                    sum_pv(i, 4)
                    sum_pv(i, 1)
                    sum_pv(i, 0)
                if runs(i + 1):
                    mean_a(i + 1, 0)
                if runs(i - 1):
                    mean_d(i - 1, 0)
                if runs(i + 1):
                    mean_a(i + 1, 1)
                    centre(i + 1, 0)
                    centre(i + 1, 1)
                    finish_a(i + 1, 0)
                if runs(i):
                    residual(i, 0)
                if runs(i + 1):
                    finish_a(i + 1, 1)
                if runs(i):
                    residual(i, 1)
                if runs(i + 1):
                    mean_b(i + 1)
                if runs(i - 1):
                    accumulate(i - 1, 10)
                if runs(i):
                    mean_c(i)
                if runs(i - 1):
                    accumulate(i - 1, 11)
                    accumulate(i - 1, 12)
                    accumulate(i - 1, 13)
                    accumulate(i - 1, 14)
                    accumulate(i - 1, 15)
                    mean_d(i - 1, 1)

            def wind_down(i):
                if runs(i - 1):
                    split_l2(i - 1)
                    top_logit(i - 1)
                    gate(i - 1)
                if runs(i):
                    qk_products(i, 5)
                    qk_products(i, 6)
                    qk_products(i, 7)
                if runs(i - 1):
                    accumulate(i - 1, 2)
                if runs(i):
                    sum_scores(i, 7)
                    sum_scores(i, 3)
                    sum_scores(i, 6)
                if runs(i - 1):
                    accumulate(i - 1, 3)
                if runs(i):
                    sum_scores(i, 4)
                    sum_scores(i, 2)
                    sum_scores(i, 0)
                    sum_scores(i, 5)
                    sum_scores(i, 1)
                if runs(i - 1):
                    accumulate(i - 1, 4)
                if runs(i):
                    softmax_in(i)
                if runs(i - 1):
                    accumulate(i - 1, 5)
                if runs(i):
                    softmax_out(i)
                    pv_products(i, 5)
                if runs(i - 1):
                    accumulate(i - 1, 6)
                if runs(i):
                    pv_products(i, 6)
                    sum_pv(i, 5)
                if runs(i - 1):
                    accumulate(i - 1, 7)
                if runs(i):
                    sum_pv(i, 0)
                    sum_pv(i, 3)
                    pv_products(i, 7)
                    sum_pv(i, 2)
                    sum_pv(i, 7)
                    sum_pv(i, 4)
                    sum_pv(i, 1)
                    sum_pv(i, 6)
                if runs(i - 1):
                    mean_d(i - 1, 0)
                if runs(i):
                    residual(i, 0)
                    residual(i, 1)
                if runs(i - 1):
                    accumulate(i - 1, 10)
                    accumulate(i - 1, 11)
                if runs(i):
                    mean_c(i)
                if runs(i - 1):
                    accumulate(i - 1, 12)
                    accumulate(i - 1, 13)
                    accumulate(i - 1, 14)
                    accumulate(i - 1, 15)
                    mean_d(i - 1, 1)

            pipeline(dve, warm_up, iteration, wind_down)

        @block.scalar
        def _(act):
            a = nc.scalar

            act.wait_ge(w_loaded, W_ALL)
            a.activation(wmid[:, 1, :], wmid[:, 1, :], ACT.Copy, scale=-1.0)
            a.activation(proj_perm[:].rearrange("p (r g d) -> p r g d", g=NKV, d=HD),
                         proj_rows.rearrange("p (g r d) -> p r g d", r=REP, d=HD), ACT.Copy).then_inc(setup_act, 1)
            act.wait_ge(setup_pe, 2)
            a.activation(qkvT[:, 0:P].rearrange("p (r g d) -> p r g d", g=NKV, d=HD),
                         bD[:, 0:P].rearrange("p (g r d) -> p r g d", r=REP, d=HD), ACT.Copy)
            a.activation(qkvT[:, P:QKV], bD[:, P:QKV], ACT.Copy)
            a.activation(projT[:], bD[:, 256:384], ACT.Copy)
            a.activation(routerT[:], bD[:, 384:384 + NE], ACT.Copy)
            a.activation(gb[:].rearrange("p a d -> p (a d)"), bE[:, 0:2 * D], ACT.Copy).then_inc(setup_act, 1)
            act.wait_ge(ew1_loaded, 16)
            a.activation(ew1_scaled, ew1, ACT.Copy, scale=SPLIT).then_inc(ew1_split, 1)
            act.wait_ge(setup_dve, 1)

            def evac_xT(b, q):
                act.wait_ge(xT_ps.sem, xT_ps.at(b, q + 1))
                if has_earlier(b):
                    act.wait_ge(out_ps.sem, out_ps.before(b, 2))
                a.activation(xT[:, q, :], bA[:], ACT.Copy).then_inc(xT_done.sem, 1)

            def evac_out(b, q):
                act.wait_ge(out_ps.sem, out_ps.at(b, q + 1))
                if has_earlier(b):
                    act.wait_ge(y_ps.sem, y_ps.before(b, 2))
                bk = (bA, bB)[q]
                a.activation(outT[:, q, :], bk[:], ACT.Identity, bias=vec("bo")).then_inc(outT_done.sem, 1)
                a.activation(outT2[:, q, :], bk[:], ACT.Identity, bias=vec("bo2")).then_inc(outT_done.sem, 1)

            def gelu_mixer(b, q):
                act.wait_ge(z_ps.sem, z_ps.at(b, q + 1))
                a.activation(gT[:, q, :], (bC, bA)[q][:], ACT.Gelu, bias=vec("w1b")).then_inc(gT_done.sem, 1)

            def evac_ln(j, q):
                act.wait_ge(xhT_ps.sem, xhT_ps.at(j, q + 1))
                if has_earlier(j):
                    act.wait_ge(qkv_ps.sem, qkv_ps.before(j, 4))
                a.activation(lnT[:, q, :], (bD, bE)[q][:], ACT.Identity, bias=vec("l1b"), scale=vec("l1w")).then_inc(lnT_done.sem, 1)

            def evac_qkv(j, n):
                act.wait_ge(qkv_ps.sem, qkv_ps.at(j, n + 1))
                if n == 0:
                    if has_earlier(j):
                        act.wait_ge(scores_done.sem, scores_done.before(j, NS))
                    if has_earlier(j):
                        act.wait_ge(att_done.sem, att_done.before(j, NS))
                bk = (bD, bE)[n % 2][:].rearrange("p (s c) -> p s c", s=2)
                t = slice(2 * n, 2 * n + 2)
                a.activation(qk[:, t, :], bk[:, :, 0:160], ACT.Copy).then_inc(qkv_done.sem, 1)
                a.activation(vx[:, t, :].rearrange("p s (r c) -> p s r c", r=REP),
                             bk[:, :, 160:QKV].unsqueeze(2).to_broadcast([P, 2, REP, NKV * HD]), ACT.Copy).then_inc(qkv_done.sem, 1)

            def exp_scores(j):
                act.wait_ge(shift_done.sem, shift_done.at(j, 1))
                a.activation(probs[:], probs[:], ACT.Exp, scale=float(HD) ** -0.5).then_inc(exp_done.sem, 1)

            def evac_att(j, q):
                act.wait_ge(attT_ps.sem, attT_ps.at(j, q + 1))
                if has_earlier(j):
                    act.wait_ge(proj_ps.sem, proj_ps.before(j, 2))
                a.activation(attT[:, q, :], (bD, bE)[q][:], ACT.Copy).then_inc(attT_done.sem, 1)

            def evac_l2(j, q):
                act.wait_ge(l2_ps.sem, l2_ps.at(j, q + 1))
                if has_earlier(j):
                    act.wait_ge(h_ps.sem, h_ps.before(j, NF * GROUPS))
                if has_earlier(j):
                    act.wait_ge(l2_low_done[q].sem, l2_low_done[q].before(j, 1))
                    act.wait_ge(l2_low_done[1].sem, l2_low_done[1].before(j, 1))
                a.activation(l2T[:, q, :], (bD, bE)[q][:], ACT.Identity, bias=vec("l2b"), scale=vec("l2w")).then_inc(l2T_done.sem, 1)
                if q:
                    act.wait_ge(l2_high_done[0].sem, l2_high_done[0].at(j, 1))
                a.activation(l2_scaled[:], (bD, bE)[q][:], ACT.Identity, bias=vec("l2bS"), scale=vec("l2wS")).then_inc(l2S_done.sem, 1)

            def normalise(dst, src, scale, shift, ts):
                for n in ts:
                    last = a.activation(dst[:, n, :], src[:, n, :], ACT.Identity, bias=shift[:, n:n + 1], scale=scale[:, n:n + 1])
                return last

            def normalise_xh(b, q):
                act.wait_ge(shiftB.sem, shiftB.at(b, 1))
                if has_earlier(b):
                    act.wait_ge(xhT_ps.sem, xhT_ps.before(b, 2))
                normalise(xh, z, rsB[:, 0, 1], rsB[:, 1, 1], tiles(q)).then_inc(xh_done.sem, 1)

            def normalise_x1(b, q):
                act.wait_ge(shiftB.sem, shiftB.at(b, 2))
                if has_earlier(b):
                    act.wait_ge(base_done.sem, base_done.before(b, 1))
                normalise(x1, z, rsB[:, 0, 0], rsB[:, 1, 0], tiles(q)).then_inc(x1_done.sem, 1)

            def normalise_c(j, q):
                act.wait_ge(shiftC.sem, shiftC.at(j, 1))
                if has_earlier(j):
                    act.wait_ge(l2_ps.sem, l2_ps.before(j, 2))
                normalise(xh2, h2, rsC[:, 0], rsC[:, 1], tiles(q)).then_inc(xh2_done.sem, 1)

            def normalise_d(k, q):
                act.wait_ge(shiftD.sem, shiftD.at(k, q + 1))
                normalise(res, res, rsD[:, 0], rsD[:, 1], tiles(q)).then_inc(y_done.sem, 1)

            def weigh(k, g):
                q, e = divmod(g, NE)
                act.wait_ge(moe_ps.sem, moe_ps.at(k, g + 1))
                if g == 0:
                    act.wait_ge(gates_done.sem, gates_done.at(k, 1))
                n_weighed = q * ACT_E + e
                if n_weighed:
                    act.wait_ge(added.sem, added.at(k, n_weighed))
                elif has_earlier(k):
                    act.wait_ge(added.sem, added.before(k, 2 * ACT_E))
                for n in tiles(q):
                    last = a.activation(weighed[:, cols(n)], group_bank[g][:, cols(n)], ACT.Copy, scale=gates[:, n, e:e + 1])
                last.then_inc(weighed_done.sem, 1)

            def exp_gates(j):
                act.wait_ge(lshift.sem, lshift.at(j, 1))
                a.activation(rt[:, 0], rt[:, 0], ACT.Exp).then_inc(gexp.sem, 1)

            def gelu_experts(k, g):
                for f in range(NF):
                    act.wait_ge(h_ps.sem, h_ps.at(k, NF * g + f + 1))
                    if g >= 2:
                        act.wait_ge(moe_ps.sem, moe_ps.at(k, g - 1))
                    else:
                        if has_earlier(k):
                            act.wait_ge(moe_ps.sem, moe_ps.before(k, GROUPS - 1 + g))
                    a.activation(hT[:, g % 2, f, :], (bF, bG)[f][:], ACT.Gelu_apprx_tanh).then_inc(hT_done.sem, 1)

            def warm_up(i):
                if runs(i - 1):
                    evac_l2(i - 1, 1)
                if runs(i):
                    evac_ln(i, 0)
                if runs(i + 1):
                    evac_xT(i + 1, 1)
                if runs(i):
                    normalise_x1(i, 1)
                    evac_ln(i, 1)
                if runs(i - 1):
                    exp_gates(i - 1)
                    gelu_experts(i - 1, 0)
                    gelu_experts(i - 1, 1)
                if runs(i):
                    evac_qkv(i, 0)
                    evac_qkv(i, 1)
                if runs(i - 1):
                    weigh(i - 1, 0)
                if runs(i):
                    evac_qkv(i, 2)
                    evac_qkv(i, 3)
                if runs(i - 1):
                    weigh(i - 1, 1)
                    gelu_experts(i - 1, 2)
                    gelu_experts(i - 1, 3)
                if runs(i + 1):
                    evac_out(i + 1, 0)
                    evac_out(i + 1, 1)
                if runs(i - 1):
                    gelu_experts(i - 1, 4)
                if runs(i + 1):
                    gelu_mixer(i + 1, 0)
                if runs(i - 1):
                    gelu_experts(i - 1, 5)
                    gelu_experts(i - 1, 6)
                if runs(i + 1):
                    gelu_mixer(i + 1, 1)
                if runs(i):
                    exp_scores(i)
                if runs(i - 1):
                    gelu_experts(i - 1, 7)
                    gelu_experts(i - 1, 8)
                    gelu_experts(i - 1, 9)
                    weigh(i - 1, 8)
                if runs(i):
                    evac_att(i, 0)
                if runs(i - 1):
                    gelu_experts(i - 1, 10)
                if runs(i):
                    evac_att(i, 1)
                if runs(i - 1):
                    gelu_experts(i - 1, 11)
                    weigh(i - 1, 9)
                    gelu_experts(i - 1, 12)
                    normalise_d(i - 1, 0)
                    gelu_experts(i - 1, 13)
                if runs(i + 1):
                    normalise_xh(i + 1, 0)
                if runs(i - 1):
                    gelu_experts(i - 1, 14)
                if runs(i):
                    normalise_c(i, 0)
                if runs(i - 1):
                    gelu_experts(i - 1, 15)
                if runs(i):
                    normalise_c(i, 1)
                    evac_l2(i, 0)
                if runs(i + 1):
                    normalise_xh(i + 1, 1)
                if runs(i + 2):
                    evac_xT(i + 2, 0)
                if runs(i + 1):
                    normalise_x1(i + 1, 0)
                if runs(i - 1):
                    normalise_d(i - 1, 1)

            def iteration(i):
                if runs(i - 1):
                    evac_l2(i - 1, 1)
                if runs(i + 1):
                    evac_xT(i + 1, 1)
                if runs(i):
                    normalise_x1(i, 1)
                if runs(i - 1):
                    exp_gates(i - 1)
                if runs(i):
                    evac_ln(i, 0)
                    evac_ln(i, 1)
                if runs(i - 1):
                    gelu_experts(i - 1, 0)
                if runs(i):
                    evac_qkv(i, 0)
                if runs(i - 1):
                    gelu_experts(i - 1, 1)
                if runs(i):
                    evac_qkv(i, 1)
                if runs(i - 1):
                    weigh(i - 1, 0)
                    weigh(i - 1, 1)
                    gelu_experts(i - 1, 2)
                if runs(i):
                    evac_qkv(i, 2)
                    evac_qkv(i, 3)
                if runs(i - 1):
                    gelu_experts(i - 1, 3)
                if runs(i + 1):
                    evac_out(i + 1, 0)
                if runs(i - 1):
                    gelu_experts(i - 1, 4)
                if runs(i + 1):
                    gelu_mixer(i + 1, 0)
                if runs(i - 1):
                    gelu_experts(i - 1, 5)
                if runs(i + 1):
                    evac_out(i + 1, 1)
                if runs(i - 1):
                    gelu_experts(i - 1, 6)
                if runs(i + 1):
                    gelu_mixer(i + 1, 1)
                if runs(i):
                    exp_scores(i)
                if runs(i - 1):
                    gelu_experts(i - 1, 7)
                    gelu_experts(i - 1, 8)
                    gelu_experts(i - 1, 9)
                    weigh(i - 1, 8)
                if runs(i):
                    evac_att(i, 0)
                    evac_att(i, 1)
                if runs(i - 1):
                    gelu_experts(i - 1, 10)
                    normalise_d(i - 1, 0)
                    gelu_experts(i - 1, 11)
                    weigh(i - 1, 9)
                    gelu_experts(i - 1, 12)
                    gelu_experts(i - 1, 13)
                if runs(i + 1):
                    normalise_xh(i + 1, 0)
                if runs(i - 1):
                    gelu_experts(i - 1, 14)
                if runs(i + 1):
                    normalise_x1(i + 1, 0)
                if runs(i - 1):
                    gelu_experts(i - 1, 15)
                if runs(i):
                    normalise_c(i, 0)
                    normalise_c(i, 1)
                    evac_l2(i, 0)
                if runs(i + 1):
                    normalise_xh(i + 1, 1)
                if runs(i + 2):
                    evac_xT(i + 2, 0)
                if runs(i - 1):
                    normalise_d(i - 1, 1)

            def wind_down(i):
                if runs(i - 1):
                    evac_l2(i - 1, 1)
                if runs(i):
                    normalise_x1(i, 1)
                    evac_ln(i, 0)
                    evac_ln(i, 1)
                if runs(i - 1):
                    exp_gates(i - 1)
                    gelu_experts(i - 1, 0)
                    gelu_experts(i - 1, 1)
                if runs(i):
                    evac_qkv(i, 0)
                    evac_qkv(i, 1)
                if runs(i - 1):
                    weigh(i - 1, 0)
                if runs(i):
                    evac_qkv(i, 2)
                if runs(i - 1):
                    gelu_experts(i - 1, 2)
                if runs(i):
                    evac_qkv(i, 3)
                if runs(i - 1):
                    weigh(i - 1, 1)
                    gelu_experts(i - 1, 3)
                    gelu_experts(i - 1, 4)
                    gelu_experts(i - 1, 5)
                    gelu_experts(i - 1, 6)
                if runs(i):
                    exp_scores(i)
                if runs(i - 1):
                    gelu_experts(i - 1, 7)
                    gelu_experts(i - 1, 8)
                    gelu_experts(i - 1, 9)
                    weigh(i - 1, 8)
                if runs(i):
                    evac_att(i, 0)
                if runs(i - 1):
                    gelu_experts(i - 1, 10)
                if runs(i):
                    evac_att(i, 1)
                if runs(i - 1):
                    gelu_experts(i - 1, 11)
                    weigh(i - 1, 9)
                    normalise_d(i - 1, 0)
                    gelu_experts(i - 1, 12)
                    gelu_experts(i - 1, 13)
                    gelu_experts(i - 1, 14)
                    gelu_experts(i - 1, 15)
                if runs(i):
                    normalise_c(i, 0)
                    evac_l2(i, 0)
                    normalise_c(i, 1)
                if runs(i - 1):
                    normalise_d(i - 1, 1)

            pipeline(act, warm_up, iteration, wind_down)

        @block.tensor
        def _(pe):
            t = nc.tensor
            idn = ident[:]

            pe.wait_ge(vec_loaded, VEC_ALL)
            pe.wait_ge(setup_pool, 2)
            t.transpose(bF[:, 0:14], vec_rows[:], ident[0:14, 0:14]).then_inc(setup_pe, 1)
            pe.wait_ge(w_loaded, W_ALL)
            pe.wait_ge(setup_act, 1)
            t.matmul(bE[:, 0:2 * D], ones_row[:], rowv[:].rearrange("p a d -> p (a d)"), start=True, stop=True)
            t.transpose(bD[:, 0:P], qkv_rows[:, 0, :], idn)
            t.transpose(bD[:, P:QKV], qkv_rows[0:QKV - P, 1, :], ident[0:QKV - P, 0:QKV - P])
            t.transpose(bD[:, 256:384], proj_perm[:], idn)
            t.transpose(bD[:, 384:384 + NE], router_rows[:], ident[0:NE, 0:NE]).then_inc(setup_pe, 1)

            def transposes(bk, src, q):
                for n in tiles(q):
                    last = t.transpose(bk[:, cols(n)], src[:, n, :], idn)
                return last

            def transpose_x(b, q):
                if q == 0:
                    pe.wait_ge(x_loaded.sem, x_loaded.at(b, 16))
                    if has_earlier(b):
                        pe.wait_ge(gT_done.sem, gT_done.before(b, 2))
                    if runs(b - 3):
                        pe.wait_ge(weighed_done.sem, weighed_done.at(b - 3, ACT_E + 2))
                else:
                    pe.wait_ge(xT_done.sem, xT_done.at(b, 1))
                transposes(bA, x_in, q).then_inc(xT_ps.sem, 1)

            def project_in(b, q):
                pe.wait_ge(xT_done.sem, xT_done.at(b, q + 1))
                if q == 0:
                    if has_earlier(b):
                        pe.wait_ge(centred.sem, centred.before(b, 2))
                    if runs(b - 3):
                        pe.wait_ge(acc_done.sem, acc_done.at(b - 3, 2 * (NE - ACT_E)))
                else:
                    pe.wait_ge(rot_done.sem, rot_done.at(b, 1))
                t.matmul(bB[:], win[:, 0, :], xT[:, q, :], start=True, stop=True)
                t.matmul(bC[:], win[:, 1, :], xT[:, q, :], start=True, stop=True).then_inc(u_ps.sem, 1)

            def mix(b, q):
                bk = (bA, bB)[q]
                if q == 0 and runs(b - 2):
                    pe.wait_ge(lshift.sem, lshift.at(b - 2, 1))
                if q == 0:
                    pe.wait_ge(xT_done.sem, xT_done.at(b, 2))
                else:
                    pe.wait_ge(rot_done.sem, rot_done.at(b, 2))
                t.matmul(bk[:], win[:, 2, :], xT[:, q, :], start=True, stop=False)
                pe.wait_ge(hid_done.sem, hid_done.at(b, 2 * q + 2))
                for n in range(2):
                    last = t.matmul(bk[:], wmid[:, n, :], post[:, 2 * n, HALF * q:HALF * q + HALF, :].rearrange("p s t -> p (s t)"),
                                    start=False, stop=(n == 1))
                last.then_inc(out_ps.sem, 1)

            def mlp_in(b, q):
                pe.wait_ge(outT_done.sem, outT_done.at(b, 2 * q + 1))
                t.matmul((bC, bA)[q][:], w1[:], outT[:, q, :], start=True, stop=True).then_inc(z_ps.sem, 1)

            def mlp_out(b, q):
                pe.wait_ge(outT_done.sem, outT_done.at(b, 4))
                pe.wait_ge(gT_done.sem, gT_done.at(b, q + 1))
                bk = (bB, bC)[q]
                for n in tiles(q):
                    t.matmul(bk[:, cols(n)], gT[:, q, cols(n)], w2[:], start=True, stop=False)
                    last = t.matmul(bk[:, cols(n)], outT2[:, q, cols(n)], idn, start=False, stop=True)
                last.then_inc(y_ps.sem, 1)

            def transpose_xh(j, q):
                pe.wait_ge(xh_done.sem, xh_done.at(j, q + 1))
                if has_earlier(j):
                    pe.wait_ge(l2S_done.sem, l2S_done.before(j, q + 1))
                transposes((bD, bE)[q], xh, q).then_inc(xhT_ps.sem, 1)

            def project_qkv(j, n):
                if n < 2:
                    pe.wait_ge(lnT_done.sem, lnT_done.at(j, 2))
                else:
                    pe.wait_ge(qkv_done.sem, qkv_done.at(j, 2 * n - 2))
                bk = (bD, bE)[n % 2]
                for m in range(2):
                    s = 2 * n + m
                    last = t.matmul(bk[:, 256 * m:256 * m + QKV], lnT[:, s // HALF, cols(s)], qkvT[:], start=True, stop=True)
                last.then_inc(qkv_ps.sem, 1)

            def transpose_att(j, q):
                pe.wait_ge(att_done.sem, att_done.at(j, NS))
                pe.wait_ge(qkv_done.sem, qkv_done.at(j, 8))
                if q and runs(j - 1):
                    pe.wait_ge(acc_done.sem, acc_done.at(j - 1, 7 - ACT_E + 1))
                transposes((bD, bE)[q], att, q).then_inc(attT_ps.sem, 1)

            def project_att(j, q):
                pe.wait_ge(attT_done.sem, attT_done.at(j, q + 1))
                bk = (bD, bE)[q]
                for n in tiles(q):
                    last = t.matmul(bk[:, cols(n)], attT[:, q, cols(n)], projT[:], start=True, stop=True)
                last.then_inc(proj_ps.sem, 1)

            def transpose_xh2(j, q):
                pe.wait_ge(xh2_done.sem, xh2_done.at(j, q + 1))
                pe.wait_ge(h2_done.sem, h2_done.at(j, q + 1))
                transposes((bD, bE)[q], xh2, q).then_inc(l2_ps.sem, 1)

            def route(j):
                if runs(j + 2):
                    pe.wait_ge(xT_done.sem, xT_done.at(j + 2, 2))
                pe.wait_ge(l2T_done.sem, l2T_done.at(j, 2))
                for n in range(NS):
                    last = t.matmul(bA[:, NE * n:NE * n + NE], l2T[:, n // HALF, cols(n)], routerT[:], start=True, stop=True)
                last.then_inc(logit_ps.sem, 1)

            def experts_in(k, g):
                q, e = divmod(g, NE)
                if g == 0 and not has_earlier(k):
                    pe.wait_ge(late_loaded, LATE_ALL)
                    pe.wait_ge(ew1_split, 4)
                if e == 0:
                    pe.wait_ge(l2_low_done[q].sem, l2_low_done[q].at(k, 1))
                for f in range(NF):
                    if g:
                        pe.wait_ge(hT_done.sem, hT_done.at(k, NF * (g - 1) + f + 1))
                    else:
                        if has_earlier(k):
                            pe.wait_ge(hT_done.sem, hT_done.before(k, NF * (GROUPS - 1) + f + 1))
                    wh, wl = (w[:, e, 128 * f:128 * f + 128] for w in (ew1_high, ew1_low))
                    t.matmul((bF, bG)[f][:], wl, l2_high[:, q, :], start=True, stop=False)
                    t.matmul((bF, bG)[f][:], wh, l2_low[:, q, :], start=False, stop=False)
                    t.matmul((bF, bG)[f][:], wh, l2_high[:, q, :], start=False, stop=True).then_inc(h_ps.sem, 1)

            def experts_out(k, g):
                q, e = divmod(g, NE)
                pe.wait_ge(hT_done.sem, hT_done.at(k, NF * (g + 1)))
                bk, earlier = group_bank[g], earlier_in_bank(g)
                if earlier is None:
                    if bk is bH:
                        if has_earlier(k):
                            pe.wait_ge(acc_done.sem, acc_done.before(k, 2 * (NE - ACT_E) - 1))
                    elif bk is bE:
                        if runs(k + 1):
                            pe.wait_ge(qkv_done.sem, qkv_done.at(k + 1, 8))
                    elif runs(k + 2):
                        if bk is bA:
                            pe.wait_ge(gT_done.sem, gT_done.at(k + 2, 2))
                        else:
                            pe.wait_ge(centred.sem, centred.at(k + 2, 2))
                elif earlier % NE < ACT_E:
                    pe.wait_ge(weighed_done.sem, weighed_done.at(k, ACT_E * (earlier // NE) + earlier % NE + 1))
                else:
                    pe.wait_ge(acc_done.sem, acc_done.at(k, (NE - ACT_E) * (earlier // NE) + earlier % NE - ACT_E + 1))
                for n in tiles(q):
                    for f in range(NF):
                        last = t.matmul(bk[:, cols(n)], hT[:, g % 2, f, cols(n)], ew2[:, e, f, :], start=(f == 0),
                                        stop=(f == NF - 1))
                last.then_inc(moe_ps.sem, 1)

            def warm_up(i):
                if runs(i - 1):
                    transpose_xh2(i - 1, 1)
                if runs(i + 1):
                    transpose_x(i + 1, 0)
                if runs(i):
                    transpose_xh(i, 0)
                if runs(i + 1):
                    transpose_x(i + 1, 1)
                    project_in(i + 1, 0)
                if runs(i):
                    transpose_xh(i, 1)
                if runs(i - 1):
                    route(i - 1)
                if runs(i + 1):
                    project_in(i + 1, 1)
                if runs(i - 1):
                    experts_in(i - 1, 0)
                if runs(i):
                    project_qkv(i, 0)
                    project_qkv(i, 1)
                if runs(i - 1):
                    experts_in(i - 1, 1)
                    experts_out(i - 1, 0)
                if runs(i):
                    project_qkv(i, 2)
                    project_qkv(i, 3)
                if runs(i - 1):
                    experts_in(i - 1, 2)
                    experts_out(i - 1, 1)
                    experts_in(i - 1, 3)
                    experts_out(i - 1, 2)
                    experts_in(i - 1, 4)
                if runs(i + 1):
                    mix(i + 1, 0)
                    mix(i + 1, 1)
                    mlp_in(i + 1, 0)
                if runs(i - 1):
                    experts_out(i - 1, 3)
                    experts_in(i - 1, 5)
                if runs(i + 1):
                    mlp_in(i + 1, 1)
                if runs(i - 1):
                    experts_out(i - 1, 4)
                    experts_in(i - 1, 6)
                    experts_out(i - 1, 5)
                    experts_in(i - 1, 7)
                    experts_out(i - 1, 6)
                if runs(i + 1):
                    mlp_out(i + 1, 0)
                if runs(i - 1):
                    experts_out(i - 1, 7)
                if runs(i + 1):
                    mlp_out(i + 1, 1)
                if runs(i - 1):
                    experts_in(i - 1, 8)
                    experts_out(i - 1, 8)
                    experts_in(i - 1, 9)
                    experts_out(i - 1, 9)
                if runs(i):
                    transpose_att(i, 0)
                    transpose_att(i, 1)
                if runs(i - 1):
                    experts_in(i - 1, 10)
                    experts_in(i - 1, 11)
                if runs(i):
                    project_att(i, 0)
                    project_att(i, 1)
                if runs(i - 1):
                    experts_out(i - 1, 10)
                    experts_in(i - 1, 12)
                    experts_out(i - 1, 11)
                    experts_in(i - 1, 13)
                    experts_out(i - 1, 12)
                    experts_in(i - 1, 14)
                    experts_in(i - 1, 15)
                    experts_out(i - 1, 13)
                if runs(i):
                    transpose_xh2(i, 0)
                if runs(i - 1):
                    experts_out(i - 1, 14)
                    experts_out(i - 1, 15)

            def iteration(i):
                if runs(i):
                    transpose_xh(i, 0)
                if runs(i + 1):
                    transpose_x(i + 1, 0)
                if runs(i - 1):
                    transpose_xh2(i - 1, 1)
                if runs(i + 1):
                    transpose_x(i + 1, 1)
                    project_in(i + 1, 0)
                if runs(i):
                    transpose_xh(i, 1)
                if runs(i - 1):
                    route(i - 1)
                    experts_in(i - 1, 0)
                if runs(i):
                    project_qkv(i, 0)
                if runs(i + 1):
                    project_in(i + 1, 1)
                if runs(i):
                    project_qkv(i, 1)
                if runs(i - 1):
                    experts_in(i - 1, 1)
                    experts_out(i - 1, 0)
                if runs(i):
                    project_qkv(i, 2)
                    project_qkv(i, 3)
                if runs(i - 1):
                    experts_out(i - 1, 1)
                    experts_in(i - 1, 2)
                    experts_in(i - 1, 3)
                    experts_out(i - 1, 2)
                    experts_in(i - 1, 4)
                if runs(i + 1):
                    mix(i + 1, 0)
                    mix(i + 1, 1)
                    mlp_in(i + 1, 0)
                if runs(i - 1):
                    experts_out(i - 1, 3)
                    experts_in(i - 1, 5)
                    experts_out(i - 1, 4)
                    experts_in(i - 1, 6)
                    experts_out(i - 1, 5)
                if runs(i + 1):
                    mlp_in(i + 1, 1)
                if runs(i - 1):
                    experts_in(i - 1, 7)
                    experts_out(i - 1, 6)
                if runs(i + 1):
                    mlp_out(i + 1, 0)
                if runs(i - 1):
                    experts_out(i - 1, 7)
                if runs(i + 1):
                    mlp_out(i + 1, 1)
                if runs(i - 1):
                    experts_in(i - 1, 8)
                    experts_in(i - 1, 9)
                    experts_out(i - 1, 8)
                    experts_out(i - 1, 9)
                if runs(i):
                    transpose_att(i, 0)
                    transpose_att(i, 1)
                if runs(i - 1):
                    experts_in(i - 1, 10)
                    experts_in(i - 1, 11)
                if runs(i):
                    project_att(i, 0)
                    project_att(i, 1)
                if runs(i - 1):
                    experts_out(i - 1, 10)
                    experts_out(i - 1, 11)
                    experts_in(i - 1, 12)
                    experts_in(i - 1, 13)
                    experts_out(i - 1, 12)
                    experts_in(i - 1, 14)
                    experts_out(i - 1, 13)
                    experts_in(i - 1, 15)
                    experts_out(i - 1, 14)
                    experts_out(i - 1, 15)
                if runs(i):
                    transpose_xh2(i, 0)

            def wind_down(i):
                if runs(i - 1):
                    transpose_xh2(i - 1, 1)
                if runs(i):
                    transpose_xh(i, 0)
                    transpose_xh(i, 1)
                if runs(i - 1):
                    route(i - 1)
                if runs(i):
                    project_qkv(i, 0)
                if runs(i - 1):
                    experts_in(i - 1, 0)
                if runs(i):
                    project_qkv(i, 1)
                if runs(i - 1):
                    experts_in(i - 1, 1)
                    experts_out(i - 1, 0)
                if runs(i):
                    project_qkv(i, 2)
                    project_qkv(i, 3)
                if runs(i - 1):
                    experts_in(i - 1, 2)
                    experts_out(i - 1, 1)
                    experts_in(i - 1, 3)
                    experts_out(i - 1, 2)
                    experts_in(i - 1, 4)
                    experts_out(i - 1, 3)
                    experts_in(i - 1, 5)
                    experts_out(i - 1, 4)
                    experts_in(i - 1, 6)
                    experts_out(i - 1, 5)
                    experts_out(i - 1, 6)
                    experts_in(i - 1, 7)
                    experts_in(i - 1, 8)
                    experts_out(i - 1, 7)
                    experts_in(i - 1, 9)
                    experts_out(i - 1, 8)
                    experts_in(i - 1, 10)
                    experts_out(i - 1, 9)
                if runs(i):
                    transpose_att(i, 0)
                    transpose_att(i, 1)
                    project_att(i, 0)
                if runs(i - 1):
                    experts_in(i - 1, 11)
                if runs(i):
                    project_att(i, 1)
                if runs(i - 1):
                    experts_out(i - 1, 10)
                    experts_in(i - 1, 12)
                    experts_out(i - 1, 11)
                    experts_in(i - 1, 13)
                    experts_out(i - 1, 12)
                    experts_in(i - 1, 14)
                    experts_out(i - 1, 13)
                    experts_in(i - 1, 15)
                    experts_out(i - 1, 14)
                    experts_out(i - 1, 15)
                if runs(i):
                    transpose_xh2(i, 0)

            pipeline(pe, warm_up, iteration, wind_down)


_INS = ["L0_attn_x", "L0_attn_W_in", "L0_attn_b_in", "L0_attn_params_log", "L0_attn_W_mid", "L0_attn_b_mid",
        "L0_attn_w1_w", "L0_attn_w1_b", "L0_attn_w2_w", "L0_attn_w2_b", "L0_attn_ln_g", "L0_attn_ln_b",
        "L0_ffn_ln1_weight", "L0_ffn_ln1_bias", "L0_ffn_ln2_weight", "L0_ffn_ln2_bias", "L0_ffn_qkv_weight",
        "L0_ffn_proj_weight", "L0_ffn_router_weight", "L0_ffn_moe_w1", "L0_ffn_moe_w2"]


def kernel(**inputs):
    import numpy as _np
    import concourse.bacc as _bacc
    from concourse.bass_utils import run_bass_kernel_spmd as _run

    nc = _bacc.Bacc("TRN2", target_bir_lowering=False, num_devices=1)
    arrays, args = {}, []
    for name in _INS:
        a = _np.ascontiguousarray(inputs[name])
        arrays[name] = a
        args.append(nc.dram_tensor(name, a.shape, F32, kind="ExternalInput").ap())
    args.append(nc.dram_tensor("out", arrays["L0_attn_x"].shape, F32, kind="ExternalOutput").ap())
    build(nc, *args)
    return _run(nc, [arrays], core_ids=[0]).results[0]["out"]
```
